# Optimizing a Trainium2 kernel written in Bass

```python
import numpy as np
import jax
import jax.numpy as jnp

def _softmax(x, axis=-1):
    return jax.nn.softmax(x, axis=axis)

def _gelu(x):
    return jax.nn.gelu(x, approximate=True)

def _silu(x):
    return jax.nn.silu(x)

def _sigmoid(x):
    return jax.nn.sigmoid(x)

def _layernorm(x, axis=-1, eps=1e-05):
    m = jnp.mean(x, axis=axis, keepdims=True)
    v = jnp.var(x, axis=axis, keepdims=True)
    return (x - m) / jnp.sqrt(v + eps)

def _scatter_add(tgt, idx, src, axis=0):
    return tgt.at[idx].add(src)

def _segment_sum(src, seg, n):
    return jax.ops.segment_sum(src, seg, n)
kernel_name = 'mk_flamingo_gated_d2_seqx_r4_3fc0b2'

def setup_inputs(seed: int=0):
    np.random.seed(seed)
    _w = jnp.asarray

    def _rec_inputs():
        import jax
        import jax.numpy as jnp
        _rk = jax.random.key(seed)
        x = 7.22e-05 + 1 * jax.random.normal(jax.random.fold_in(_rk, 1), (8, 112, 256), jnp.float32)
        _lenS = 112 - jax.random.randint(jax.random.fold_in(_rk, 7), (8,), 0, max(1, 112 // 4) + 1, jnp.int32)
        _lenS2 = 375 - jax.random.randint(jax.random.fold_in(_rk, 8), (8,), 0, max(1, 375 // 4) + 1, jnp.int32)
        _ctx_1024P = jax.random.normal(jax.random.fold_in(_rk, 11), (8, 16, 256), jnp.float32)
        _ctx_1024c = jax.random.dirichlet(jax.random.fold_in(_rk, 511), 0.3 * jnp.ones((16,), jnp.float32), (8, 375))
        _ctx_1024t = jnp.einsum('bsk,bkd->bsd', _ctx_1024c, _ctx_1024P)
        _ctx_1024t = _ctx_1024t * jax.lax.rsqrt(jnp.mean(jnp.square(_ctx_1024t)) + 1e-12) * 0.953939
        ctx_1024 = -0.000514642 + 1.00011 * (_ctx_1024t + 0.3 * jax.random.normal(jax.random.fold_in(_rk, 611), (8, 375, 256), jnp.float32))
        _validS = jnp.arange(112)[None, :] < _lenS[:, None]
        _validS2 = jnp.arange(375)[None, :] < _lenS2[:, None]
        _causal = jnp.tril(jnp.ones((112, 112), dtype=bool))
        mask_BxS_ik0 = jnp.where(jnp.broadcast_to(_validS[:, :], (8, 112)), 0, 1).astype(jnp.int32)
        mask_BxS_ff1 = jnp.where(jnp.ones((8, 112), dtype=bool), 1.0, 0.0).astype(jnp.float32)
        mask_BxS2_ik0 = jnp.where(jnp.broadcast_to(_validS2[:, :], (8, 375)), 0, 1).astype(jnp.int32)
        _g = jax.random.normal(jax.random.fold_in(_rk, 9001), (2, 2), jnp.float32)
        _g = jnp.sign(_g) * jnp.maximum(jnp.abs(_g), 1.0) + (_g == 0) * 1.0
        g_xattn = _g[0]
        g_ffn = _g[1]
        return (x, ctx_1024, mask_BxS_ik0, mask_BxS_ff1, mask_BxS2_ik0, g_xattn, g_ffn)
    x, ctx_1024, mask_BxS_ik0, mask_BxS_ff1, mask_BxS2_ik0, g_xattn, g_ffn = _rec_inputs()

    def _L0_xattn_setup():
        import jax, jax.numpy as jnp
        import numpy as np
        B, S, P, D, H = (2, 1024, 256, 256, 16)
        key = jax.random.key(seed)
        ks = jax.random.split(key, 8)
        init = 0.02
        queries = jax.random.normal(ks[0], (B, S, D), dtype=jnp.float32)
        patch_representations = jax.random.normal(ks[1], (B, P, D), dtype=jnp.float32)
        patch_boundaries = jax.random.randint(ks[2], (B, S), 0, 2, dtype=jnp.int32)
        wq = jax.random.normal(ks[3], (D, D), dtype=jnp.float32) * init
        wk = jax.random.normal(ks[4], (D, D), dtype=jnp.float32) * init
        wv = jax.random.normal(ks[5], (D, D), dtype=jnp.float32) * init
        wo = jax.random.normal(ks[6], (D, D), dtype=jnp.float32) * init
        bq = jnp.zeros((D,), jnp.float32)
        bk = jnp.zeros((D,), jnp.float32)
        bv = jnp.zeros((D,), jnp.float32)
        bo = jnp.zeros((D,), jnp.float32)
        return {'queries': queries, 'patch_representations': patch_representations, 'patch_boundaries': patch_boundaries, 'wq': wq, 'wk': wk, 'wv': wv, 'wo': wo, 'bq': bq, 'bk': bk, 'bv': bv, 'bo': bo}
    _L0_xattn_all = _L0_xattn_setup()
    _L0_xattn_in = {k: v for k, v in _L0_xattn_all.items() if k in ('wq', 'wk', 'wv', 'wo', 'bq', 'bk', 'bv', 'bo')}
    del _L0_xattn_all

    def _L0_ffn_setup():
        import jax, jax.numpy as jnp
        import numpy as np
        K = 2
        TEMP = 1.0
        key = jax.random.key(seed)
        ks = jax.random.split(key, 5)
        B, S, D, O, E = (4, 512, 256, 256, 8)
        scale = 1.0 / np.sqrt(D)
        x = jax.random.normal(ks[0], (B, S, D), dtype=jnp.float32)
        W = jax.random.normal(ks[1], (E, O, D), dtype=jnp.float32) * scale
        b = jax.random.normal(ks[2], (E, O), dtype=jnp.float32) * 0.01
        Wg = jax.random.normal(ks[3], (E, D), dtype=jnp.float32) * scale
        bg = jnp.zeros((E,), dtype=jnp.float32)
        return {'x': x, 'W': W, 'b': b, 'Wg': Wg, 'bg': bg}
    _L0_ffn_all = _L0_ffn_setup()
    _L0_ffn_in = {k: v for k, v in _L0_ffn_all.items() if k in ('W', 'b', 'Wg', 'bg')}
    del _L0_ffn_all

    def _L1_xattn_setup():
        import jax, jax.numpy as jnp
        import numpy as np
        B, F, T, D = (8, 64, 32, 256)
        NEG = -1e+30
        key = jax.random.key(seed)
        ks = jax.random.split(key, 10)
        s = 1.0 / np.sqrt(D)
        return {'features': jax.random.normal(ks[0], (B, F, D), jnp.float32), 'masks': jnp.ones((B, F), jnp.float32), 'textual_features': jax.random.normal(ks[1], (B, T, D), jnp.float32), 'q_masks': jax.random.randint(ks[2], (B, T), 0, 2, jnp.int32), 'Ws': jax.random.normal(ks[3], (D, D), jnp.float32) * s, 'W': jax.random.normal(ks[4], (D, D), jnp.float32) * s, 'w': jax.random.normal(ks[5], (D, 1), jnp.float32) * s, 'b': jax.random.normal(ks[6], (1, D), jnp.float32) * s, 'Wcw': jax.random.normal(ks[7], (1, D), jnp.float32) * s, 'bcw': jnp.zeros((1,), jnp.float32), 'Wcb': jax.random.normal(ks[8], (1, D), jnp.float32) * s, 'bcb': jnp.zeros((1,), jnp.float32)}
    _L1_xattn_all = _L1_xattn_setup()
    _L1_xattn_in = {k: v for k, v in _L1_xattn_all.items() if k in ('Ws', 'W', 'w', 'b', 'Wcw', 'bcw', 'Wcb', 'bcb')}
    del _L1_xattn_all

    def _L1_ffn_setup():
        import jax, jax.numpy as jnp
        import numpy as np
        H, HP, NH_M, NH_D = (256, 64, 8, 8)
        B, T = (2, 512)
        SPARSITY = 8
        N_ROT = 32
        BASE = 10000.0

        def _rope(x, pos, n_rot, base):
            half = n_rot // 2
            inv = base ** (-jnp.arange(half, dtype=x.dtype) / half)
            ang = pos[..., None] * inv
            cos, sin = (jnp.cos(ang), jnp.sin(ang))
            x1, x2 = (x[..., :half], x[..., half:n_rot])
            rot = jnp.concatenate([x1 * cos - x2 * sin, x1 * sin + x2 * cos], axis=-1)
            return jnp.concatenate([rot, x[..., n_rot:]], axis=-1)

        def _mosa_branch(X, router_w, wqkv, wo):
            b, t, _ = X.shape
            k = t // SPARSITY
            scores = jnp.einsum('bth,hn->bnt', X, router_w)
            _, idx = jax.lax.top_k(scores, k)
            idx = jnp.sort(idx, axis=-1)
            gates = jax.nn.sigmoid(jnp.take_along_axis(scores, idx, axis=-1))
            Xg = jnp.take_along_axis(X[:, None], idx[..., None], axis=2)
            qkv = jnp.einsum('bnkh,hnd->bnkd', Xg, wqkv)
            Q, K, V = jnp.split(qkv, 3, axis=-1)
            pos = idx.astype(X.dtype)
            Q = _rope(Q, pos, N_ROT, BASE)
            K = _rope(K, pos, N_ROT, BASE)
            att = jnp.einsum('bnqd,bnkd->bnqk', Q, K) / jnp.sqrt(jnp.asarray(HP, X.dtype))
            causal = idx[..., :, None] >= idx[..., None, :]
            att = jnp.where(causal, att, -jnp.inf)
            AV = jnp.einsum('bnqk,bnkd->bnqd', jax.nn.softmax(att, axis=-1), V)
            AV = AV * gates[..., None]
            out = jnp.zeros((b, NH_M, t, HP), X.dtype)
            bi = jnp.arange(b)[:, None, None]
            hi = jnp.arange(NH_M)[None, :, None]
            out = out.at[bi, hi, idx].set(AV)
            out = out.transpose(0, 2, 1, 3).reshape(b, t, NH_M * HP)
            return out @ wo

        def _dense_branch(X, wqkv, wo):
            b, t, _ = X.shape
            qkv = jnp.einsum('bth,hnd->bntd', X, wqkv)
            Q, K, V = jnp.split(qkv, 3, axis=-1)
            pos = jnp.arange(t, dtype=X.dtype)
            Q = _rope(Q, pos, N_ROT, BASE)
            K = _rope(K, pos, N_ROT, BASE)
            att = jnp.einsum('bnqd,bnkd->bnqk', Q, K) / jnp.sqrt(jnp.asarray(HP, X.dtype))
            causal = jnp.tril(jnp.ones((t, t), bool))
            att = jnp.where(causal, att, -jnp.inf)
            AV = jnp.einsum('bnqk,bnkd->bnqd', jax.nn.softmax(att, axis=-1), V)
            return AV.transpose(0, 2, 1, 3).reshape(b, t, NH_D * HP) @ wo
        key = jax.random.key(seed)
        ks = jax.random.split(key, 6)
        s = 0.02
        return {'X': jax.random.normal(ks[0], (B, T, H), jnp.float32), 'mosa_router_w': jax.random.normal(ks[1], (H, NH_M), jnp.float32) * s, 'mosa_wqkv': jax.random.normal(ks[2], (H, NH_M, 3 * HP), jnp.float32) * s, 'mosa_wo': jax.random.normal(ks[3], (NH_M * HP, H), jnp.float32) * s, 'dense_wqkv': jax.random.normal(ks[4], (H, NH_D, 3 * HP), jnp.float32) * s, 'dense_wo': jax.random.normal(ks[5], (NH_D * HP, H), jnp.float32) * s}
    _L1_ffn_all = _L1_ffn_setup()
    _L1_ffn_in = {k: v for k, v in _L1_ffn_all.items() if k in ('mosa_router_w', 'mosa_wqkv', 'mosa_wo', 'dense_wqkv', 'dense_wo')}
    del _L1_ffn_all
    return {'x': x, 'ctx_1024': ctx_1024, 'mask_BxS_ik0': mask_BxS_ik0, 'mask_BxS_ff1': mask_BxS_ff1, 'mask_BxS2_ik0': mask_BxS2_ik0, 'g_xattn': g_xattn, 'g_ffn': g_ffn, 'L0_xattn_wq': _L0_xattn_in['wq'], 'L0_xattn_wk': _L0_xattn_in['wk'], 'L0_xattn_wv': _L0_xattn_in['wv'], 'L0_xattn_wo': _L0_xattn_in['wo'], 'L0_xattn_bq': _L0_xattn_in['bq'], 'L0_xattn_bk': _L0_xattn_in['bk'], 'L0_xattn_bv': _L0_xattn_in['bv'], 'L0_xattn_bo': _L0_xattn_in['bo'], 'L0_ffn_W': _L0_ffn_in['W'], 'L0_ffn_b': _L0_ffn_in['b'], 'L0_ffn_Wg': _L0_ffn_in['Wg'], 'L0_ffn_bg': _L0_ffn_in['bg'], 'L1_xattn_Ws': _L1_xattn_in['Ws'], 'L1_xattn_W': _L1_xattn_in['W'], 'L1_xattn_w': _L1_xattn_in['w'], 'L1_xattn_b': _L1_xattn_in['b'], 'L1_xattn_Wcw': _L1_xattn_in['Wcw'], 'L1_xattn_bcw': _L1_xattn_in['bcw'], 'L1_xattn_Wcb': _L1_xattn_in['Wcb'], 'L1_xattn_bcb': _L1_xattn_in['bcb'], 'L1_ffn_mosa_router_w': _L1_ffn_in['mosa_router_w'], 'L1_ffn_mosa_wqkv': _L1_ffn_in['mosa_wqkv'], 'L1_ffn_mosa_wo': _L1_ffn_in['mosa_wo'], 'L1_ffn_dense_wqkv': _L1_ffn_in['dense_wqkv'], 'L1_ffn_dense_wo': _L1_ffn_in['dense_wo']}

def reference(x, ctx_1024, mask_BxS_ik0, mask_BxS_ff1, mask_BxS2_ik0, g_xattn, g_ffn, L0_xattn_wq, L0_xattn_wk, L0_xattn_wv, L0_xattn_wo, L0_xattn_bq, L0_xattn_bk, L0_xattn_bv, L0_xattn_bo, L0_ffn_W, L0_ffn_b, L0_ffn_Wg, L0_ffn_bg, L1_xattn_Ws, L1_xattn_W, L1_xattn_w, L1_xattn_b, L1_xattn_Wcw, L1_xattn_bcw, L1_xattn_Wcb, L1_xattn_bcb, L1_ffn_mosa_router_w, L1_ffn_mosa_wqkv, L1_ffn_mosa_wo, L1_ffn_dense_wqkv, L1_ffn_dense_wo):
    import jax
    import jax.numpy as jnp

    def _L0_xattn_ref(queries, patch_representations, patch_boundaries, wq, wk, wv, wo, bq, bk, bv, bo):
        import jax, jax.numpy as jnp
        import numpy as np
        B, S, P, D, H = (2, 1024, 256, 256, 16)
        b, s, d = queries.shape
        p = patch_representations.shape[1]
        h = H
        dh = d // h
        scale = 1.0 / jnp.sqrt(jnp.asarray(dh, queries.dtype))
        q = (queries @ wq.T + bq).reshape(b, s, h, dh)
        k = (patch_representations @ wk.T + bk).reshape(b, p, h, dh)
        v = (patch_representations @ wv.T + bv).reshape(b, p, h, dh)
        scores = jnp.einsum('bqhd,bkhd->bhqk', q, k) * scale
        patch_idx = jnp.cumsum(patch_boundaries, axis=1)
        mask = jnp.arange(p)[None, None, :] > patch_idx[:, :, None]
        scores = jnp.where(mask[:, None, :, :], jnp.finfo(scores.dtype).min, scores)
        attn = jax.nn.softmax(scores, axis=-1)
        out = jnp.einsum('bhqk,bkhd->bqhd', attn, v).reshape(b, s, d)
        return out @ wo.T + bo

    def _L0_ffn_ref(x, W, b, Wg, bg):
        import jax, jax.numpy as jnp
        import numpy as np
        K = 2
        TEMP = 1.0
        gate_logits = (jnp.einsum('bsd,ed->bse', x, Wg) + bg) / TEMP
        gate_scores = jax.nn.softmax(gate_logits, axis=-1)
        topk_scores, topk_idx = jax.lax.top_k(gate_scores, K)
        expert_outputs = jnp.einsum('bsd,eod->bseo', x, W) + b
        selected = jnp.take_along_axis(expert_outputs, topk_idx[..., None], axis=2)
        output = jnp.sum(selected * topk_scores[..., None], axis=2)
        return output

    def _L1_xattn_ref(features, masks, textual_features, q_masks, Ws, W, w, b, Wcw, bcw, Wcb, bcb):
        import jax, jax.numpy as jnp
        import numpy as np
        B, F, T, D = (8, 64, 32, 256)
        NEG = -1e+30
        txt_proj = jnp.einsum('btd,de->bte', textual_features, Ws)
        feat_proj = jnp.einsum('bfd,de->bfe', features, W)
        h = jnp.tanh(txt_proj[:, None, :, :] + feat_proj[:, :, None, :] + b[None, None, :, :][..., 0, :])
        rho = jnp.einsum('bftd,d->bft', h, w[:, 0])
        qm = q_masks.astype(jnp.float32)
        rho = rho + (1.0 - qm)[:, None, :] * NEG
        att = jax.nn.softmax(rho, axis=-1)
        txt_h = jnp.einsum('bft,btd->bfd', att, textual_features)
        w_s = jnp.tanh(jnp.einsum('bfd,od->bfo', txt_h, Wcw) + bcw)
        b_s = jnp.tanh(jnp.einsum('bfd,od->bfo', txt_h, Wcb) + bcb)
        return w_s * features + b_s

    def _L1_ffn_ref(X, mosa_router_w, mosa_wqkv, mosa_wo, dense_wqkv, dense_wo):
        import jax, jax.numpy as jnp
        import numpy as np
        H, HP, NH_M, NH_D = (256, 64, 8, 8)
        B, T = (2, 512)
        SPARSITY = 8
        N_ROT = 32
        BASE = 10000.0

        def _rope(x, pos, n_rot, base):
            half = n_rot // 2
            inv = base ** (-jnp.arange(half, dtype=x.dtype) / half)
            ang = pos[..., None] * inv
            cos, sin = (jnp.cos(ang), jnp.sin(ang))
            x1, x2 = (x[..., :half], x[..., half:n_rot])
            rot = jnp.concatenate([x1 * cos - x2 * sin, x1 * sin + x2 * cos], axis=-1)
            return jnp.concatenate([rot, x[..., n_rot:]], axis=-1)

        def _mosa_branch(X, router_w, wqkv, wo):
            b, t, _ = X.shape
            k = t // SPARSITY
            scores = jnp.einsum('bth,hn->bnt', X, router_w)
            _, idx = jax.lax.top_k(scores, k)
            idx = jnp.sort(idx, axis=-1)
            gates = jax.nn.sigmoid(jnp.take_along_axis(scores, idx, axis=-1))
            Xg = jnp.take_along_axis(X[:, None], idx[..., None], axis=2)
            qkv = jnp.einsum('bnkh,hnd->bnkd', Xg, wqkv)
            Q, K, V = jnp.split(qkv, 3, axis=-1)
            pos = idx.astype(X.dtype)
            Q = _rope(Q, pos, N_ROT, BASE)
            K = _rope(K, pos, N_ROT, BASE)
            att = jnp.einsum('bnqd,bnkd->bnqk', Q, K) / jnp.sqrt(jnp.asarray(HP, X.dtype))
            causal = idx[..., :, None] >= idx[..., None, :]
            att = jnp.where(causal, att, -jnp.inf)
            AV = jnp.einsum('bnqk,bnkd->bnqd', jax.nn.softmax(att, axis=-1), V)
            AV = AV * gates[..., None]
            out = jnp.zeros((b, NH_M, t, HP), X.dtype)
            bi = jnp.arange(b)[:, None, None]
            hi = jnp.arange(NH_M)[None, :, None]
            out = out.at[bi, hi, idx].set(AV)
            out = out.transpose(0, 2, 1, 3).reshape(b, t, NH_M * HP)
            return out @ wo

        def _dense_branch(X, wqkv, wo):
            b, t, _ = X.shape
            qkv = jnp.einsum('bth,hnd->bntd', X, wqkv)
            Q, K, V = jnp.split(qkv, 3, axis=-1)
            pos = jnp.arange(t, dtype=X.dtype)
            Q = _rope(Q, pos, N_ROT, BASE)
            K = _rope(K, pos, N_ROT, BASE)
            att = jnp.einsum('bnqd,bnkd->bnqk', Q, K) / jnp.sqrt(jnp.asarray(HP, X.dtype))
            causal = jnp.tril(jnp.ones((t, t), bool))
            att = jnp.where(causal, att, -jnp.inf)
            AV = jnp.einsum('bnqk,bnkd->bnqd', jax.nn.softmax(att, axis=-1), V)
            return AV.transpose(0, 2, 1, 3).reshape(b, t, NH_D * HP) @ wo
        return _mosa_branch(X, mosa_router_w, mosa_wqkv, mosa_wo) + _dense_branch(X, dense_wqkv, dense_wo)
    x = x + jnp.tanh(g_xattn[0]) * _L0_xattn_ref(_layernorm(x, axis=-1), ctx_1024, mask_BxS_ik0, L0_xattn_wq, L0_xattn_wk, L0_xattn_wv, L0_xattn_wo, L0_xattn_bq, L0_xattn_bk, L0_xattn_bv, L0_xattn_bo)
    x = x + jnp.tanh(g_ffn[0]) * _L0_ffn_ref(_layernorm(x, axis=-1), L0_ffn_W, L0_ffn_b, L0_ffn_Wg, L0_ffn_bg)
    x = x + jnp.tanh(g_xattn[1]) * _L1_xattn_ref(_layernorm(x, axis=-1), mask_BxS_ff1, ctx_1024, mask_BxS2_ik0, L1_xattn_Ws, L1_xattn_W, L1_xattn_w, L1_xattn_b, L1_xattn_Wcw, L1_xattn_bcw, L1_xattn_Wcb, L1_xattn_bcb)
    x = x + jnp.tanh(g_ffn[1]) * _L1_ffn_ref(_layernorm(x, axis=-1), L1_ffn_mosa_router_w, L1_ffn_mosa_wqkv, L1_ffn_mosa_wo, L1_ffn_dense_wqkv, L1_ffn_dense_wo)
    return x

_drawn_inputs = setup_inputs


def setup_inputs(seed=0):
    import zlib

    import numpy as np

    out = dict(_drawn_inputs(seed))
    spreads = {'g_ffn': (-1.0, 0.6),
     'L0_xattn_bq': (0.0, 0.8),
     'L0_xattn_bk': (0.0, 2.0),
     'L0_xattn_bv': (0.0, 0.1),
     'L0_xattn_bo': (0.0, 0.1),
     'L0_ffn_bg': (0.0, 0.1)}
    factors = {'L0_xattn_wq': 8.0,
     'L0_xattn_wk': 8.0,
     'L0_ffn_b': 8.0,
     'L1_xattn_b': 30.121,
     'L1_ffn_mosa_router_w': 5.968,
     'L1_ffn_mosa_wqkv': 5.872,
     'L1_ffn_mosa_wo': 5.816,
     'L1_ffn_dense_wqkv': 2.667,
     'L1_ffn_dense_wo': 2.72}
    for name, (base, spread) in spreads.items():
        noise = np.random.default_rng([zlib.crc32(name.encode()), seed]).standard_normal(out[name].shape)
        drawn = base * np.exp(spread * noise) if base else spread * noise
        out[name] = jnp.asarray(drawn.astype(out[name].dtype))
    for name, factor in factors.items():
        out[name] = (out[name] * factor).astype(out[name].dtype)
    return out
```

```python
import concourse.bass as bass
from concourse import mybir
from contextlib import ExitStack

F32 = mybir.dt.float32
I32 = mybir.dt.int32
U32 = mybir.dt.uint32
ALU = mybir.AluOpType
ACT = mybir.ActivationFunctionType
AX_X = mybir.AxisListType.X

B, T, D = 8, 112, 256
TC = 375
DC = D // 128
PAIRS = B // 2
KT = 125
NKT = TC // KT
H0, DH0, PAD0 = 16, 16, 32
NE = 8
NH, HP = 8, 64
ROT = 32
KSEL = T // 8
CH = 16
NCH = -(-TC // CH)
TCP = NCH * CH
RING = 4
LOWEST = -3.4028234663852886e38
MASKED = -1e30

CONST = {}
_at = 0
for _name, _n in (("ident", 128), ("tri", T), ("headmask", 8), ("keyidx", TC), ("causal", T), ("batchmask", T),
                  ("tokcol", 1), ("tokrow", T), ("cos", ROT), ("sin", ROT), ("iota8", NE), ("ones", 128)):
    CONST[_name] = (_at, _at + _n)
    _at += _n
NCONST = _at


class Attention:

    def __init__(self, sem, name, bufs, tiles, nh, keys, kt, scale):
        self.tiles, self.nh, self.keys, self.kt, self.scale = tiles, nh, keys, kt, scale
        self.nkt = keys // kt
        self.ident, self.score_ps, self.probsT_ps = bufs["ident"], bufs["score_ps"], bufs["probsT_ps"]
        self.score_sb, self.probsT_sb = bufs["score_sb"], bufs["probsT_sb"]
        self.max_sb, self.sum_sb, self.recip_sb = bufs["max_sb"], bufs["sum_sb"], bufs["recip_sb"]
        self.scores_full = sem(name + "_scores_full")
        self.scores_taken = [sem(f"{name}_scores_taken{s}") for s in range(2)]
        self.max_ready = sem(name + "_max_ready")
        self.shifted = sem(name + "_shifted")
        self.exp_ready = sem(name + "_exp_ready")
        self.sum_ready = sem(name + "_sum_ready")
        self.recip_ready = sem(name + "_recip_ready")
        self.probs_ready = sem(name + "_probs_ready")
        self.probsT_full = [sem(f"{name}_probsT_full{s}") for s in range(RING)]
        self.probsT_taken = [sem(f"{name}_probsT_taken{s}") for s in range(2)]
        self.values_done = [sem(f"{name}_values_done{s}") for s in range(2)]

    def tile(self, g):
        return self.score_sb[0:T, g % RING, 0:self.nh * self.keys]

    def heads(self, g):
        return self.tile(g).rearrange("p (h k) -> p h k", h=self.nh)

    def tensor(self, pe, i, scores, values, after):
        n = self.nh * self.nkt

        def do_scores(g):
            pe.wait_ge(self.scores_taken[g % 2], i * (self.tiles // 2) + g // 2)
            scores(g, self.score_ps[g % 2]).then_inc(self.scores_full, 1)

        def do_transposes(g):
            pe.wait_ge(self.probs_ready, i * self.tiles + g + 1)
            pe.wait_ge(self.probsT_taken[g % 2], i * (self.tiles // 2) + g // 2)
            for j in range(n):
                last = pe.transpose(self.probsT_ps[g % 2][0:self.kt, j * T:(j + 1) * T],
                                    self.tile(g)[:, j * self.kt:(j + 1) * self.kt], self.ident[0:T, 0:T])
            last.then_inc(self.probsT_full[g % RING], 1)

        for g in range(RING):
            do_scores(g)
        for g in range(self.tiles):
            do_transposes(g)
            if g + RING < self.tiles:
                do_scores(g + RING)
            pe.wait_ge(self.probsT_taken[g % 2], i * (self.tiles // 2) + g // 2 + 1)
            values(g, self.probsT_sb[g % 2]).then_inc(self.values_done[g % 2], 1)
            after(g)

    def vector(self, dve, i, mask, after):
        def first(g):
            dve.wait_ge(self.scores_full, i * self.tiles + g + 1)
            dve.wait_ge(self.probsT_full[g % RING], i * (self.tiles // RING) + g // RING)
            ps = self.score_ps[g % 2][0:T, 0:self.nh * self.keys].rearrange("p (h k) -> p h k", h=self.nh)
            dve.tensor_tensor(self.heads(g), ps, mask(g), ALU.add).then_inc(self.scores_taken[g % 2], 1)
            dve.wait_ge(self.scores_taken[g % 2], i * (self.tiles // 2) + g // 2 + 1)
            dve.tensor_reduce(self.max_sb[0:T, g % RING, 0:self.nh], self.heads(g), AX_X, ALU.max)\
               .then_inc(self.max_ready, 1)

        def second(g):
            dve.wait_ge(self.exp_ready, i * self.tiles + g + 1)
            dve.tensor_reduce(self.sum_sb[0:T, g % RING, 0:self.nh], self.heads(g), AX_X, ALU.add)\
               .then_inc(self.sum_ready, 1)
            dve.wait_ge(self.sum_ready, i * self.tiles + g + 1)
            dve.reciprocal(self.recip_sb[0:T, g % RING, 0:self.nh], self.sum_sb[0:T, g % RING, 0:self.nh])\
               .then_inc(self.recip_ready, 1)

        for g in range(RING):
            first(g)
        for g in range(self.tiles):
            second(g)
            if g + RING < self.tiles:
                first(g + RING)
            after(g)

    def gpsimd(self, pool, i, before, after):
        def shift(g):
            before(g)
            pool.wait_ge(self.max_ready, i * self.tiles + g + 1)
            m = self.max_sb[0:T, g % RING, 0:self.nh].unsqueeze(2).to_broadcast([T, self.nh, self.keys])
            pool.tensor_tensor(self.heads(g), self.heads(g), m, ALU.subtract).then_inc(self.shifted, 1)

        def divide(g):
            pool.wait_ge(self.recip_ready, i * self.tiles + g + 1)
            r = self.recip_sb[0:T, g % RING, 0:self.nh].unsqueeze(2).to_broadcast([T, self.nh, self.keys])
            pool.tensor_tensor(self.heads(g), self.heads(g), r, ALU.mult).then_inc(self.probs_ready, 1)

        for g in range(RING):
            shift(g)
        for g in range(self.tiles):
            divide(g)
            if g + RING < self.tiles:
                shift(g + RING)
            after(g)

    def scalar(self, act, i, after):
        def exp(g):
            act.wait_ge(self.shifted, i * self.tiles + g + 1)
            act.activation(self.tile(g), self.tile(g), ACT.Exp, scale=self.scale).then_inc(self.exp_ready, 1)

        def take(g):
            act.wait_ge(self.probsT_full[g % RING], i * (self.tiles // RING) + g // RING + 1)
            act.wait_ge(self.values_done[g % 2], i * (self.tiles // 2) + g // 2)
            cols = self.nh * self.nkt * T
            act.activation(self.probsT_sb[g % 2][0:self.kt, 0:cols], self.probsT_ps[g % 2][0:self.kt, 0:cols],
                           ACT.Copy).then_inc(self.probsT_taken[g % 2], 1)

        for g in range(RING):
            exp(g)
        for g in range(self.tiles):
            take(g)
            if g + RING < self.tiles:
                exp(g + RING)
            after(g)


class Chain:

    def __init__(self, eng, sem, i, per, scratch=None):
        self.eng, self.sem, self.base, self.per, self.n, self.scratch = eng, sem, i * per, per, 0, scratch

    def __call__(self, ins, carry=False):
        self.n += 1
        ins.then_inc(self.sem, 1)
        self.eng.wait_ge(self.sem, self.base + self.n)
        if carry:
            self.eng.memset(self.scratch, 0.0)

    def end(self):
        assert self.n == self.per, (self.n, self.per)


def flamingo_kernel(nc, a, out):
    ctx = ExitStack()
    with ctx:
        scope = [ctx]

        def sb(name, shape, dt=F32):
            return scope[-1].enter_context(nc.sbuf_tensor(name, shape, dt))

        def stage_buffers():
            scope.append(ExitStack())

        def end_stage_buffers():
            scope.pop().close()

        sems = {}

        def sem(name):
            if name not in sems:
                sems[name] = ctx.enter_context(nc.semaphore(name))
            return sems[name]

        X = sb("X", [T, B, D])
        XN = [sb(f"XN{u}", [T, D]) for u in range(2)]
        consts = sb("consts", [128, NCONST])
        gates = sb("gates", [T, 4])
        tanh_gates = sb("tanh_gates", [T, 4])
        XT = [sb(f"XT{u}", [128, DC, T]) for u in range(2)]
        CT = [sb(f"CT{u}", [128, DC, TC]) for u in range(2)]
        bn = sb("bn", [T, 2, 6])
        mv = sb("mv", [T, 2, 2])
        rstd = sb("rstd", [T, 2])
        scratch = sb("scratch", [T, 1])
        var_eps = sb("var_eps", [T, 2, 2])
        ps = [ctx.enter_context(nc.psum_tensor(f"bank{n}", [128, 512], F32)) for n in range(8)]

        def const(name, rows=128):
            lo, hi = CONST[name]
            return consts[0:rows, lo:hi]

        ident = const("ident")
        att_bufs = dict(
            ident=ident, score_ps=[ps[4], ps[5]], probsT_ps=[ps[6], ps[7]],
            score_sb=sb("score_sb", [T, RING, 4 * KT]), max_sb=sb("max_sb", [T, RING, 4]),
            sum_sb=sb("sum_sb", [T, RING, 4]), recip_sb=sb("recip_sb", [T, RING, 4]),
            probsT_sb=[sb(f"probsT_sb{s}", [128, 4 * T]) for s in range(2)])

        bqk0 = sb("bqk0", [128, 2, DC])
        bv0 = sb("bv0", [128, D])
        bo0 = sb("bo0", [1, D])
        bnd_i = sb("bnd_i", [T, B], I32)
        bnd_f = sb("bnd_f", [T, B])
        last_key = sb("last_key", [T, B])
        wide_col = sb("wide_col", [T, 1])
        wide_i = sb("wide_i", [1, 1], I32)

        wg0 = sb("wg0", [128, DC, NE])
        bg0 = sb("bg0", [1, NE])
        we0 = sb("we0", [128, DC, NE * D])
        be0 = sb("be0", [NE, D])
        logit = sb("logit", [T, NE])
        router = sb("router", [T, 8, NE])
        router_i = sb("router_i", [T, NE], U32)
        G = [sb(f"G{u}", [T, NE]) for u in range(2)]
        GT = [sb(f"GT{u}", [NE, T]) for u in range(2)]
        Y = sb("Y", [T, D])

        ws1 = sb("ws1", [128, DC, D])
        wf1 = sb("wf1", [128, DC, D])
        w1_col = sb("w1_col", [128, DC])
        w1_rep = sb("w1_rep", [128, DC, 32])
        wcwb_col = sb("wcwb_col", [128, 2, DC])
        wcwb_rep = sb("wcwb_rep", [128, 2, DC, T])
        bf1 = sb("bf1", [128, DC])
        bcwb = sb("bcwb", [T, 2])
        qmask_i = sb("qmask_i", [T, B, TC], I32)
        TT = [sb(f"TT{u}", [128, DC, TCP]) for u in range(2)]
        live = sb("live", [1, 4, B, NCH])
        span = sb("span", [1, 8, B])
        steps_of = sb("steps_of", [1, B, 6], I32)

        wqkv1 = sb("wqkv1", [128, DC, 3 * NH * HP])
        wo1 = sb("wo1", [128, 4, D])
        wr1 = sb("wr1", [128, DC, NH])
        wqkvm = sb("wqkvm", [128, DC, NH, 3 * HP])
        wom = sb("wom", [128, 4, D])
        zeros = sb("zeros", [T, 1])

        stage_buffers()
        wq0 = sb("wq0", [128, DC, D])
        wk0 = sb("wk0", [128, DC, D])
        wv0 = sb("wv0", [128, DC, D])
        wo0 = sb("wo0", [128, 4, D])
        beyond = sb("beyond", [T, 3, B])
        QT0 = [sb(f"QT0{u}", [128, DC, T]) for u in range(2)]
        KT0 = [sb(f"KT0{u}", [128, DC, TC]) for u in range(2)]
        KBD = [sb(f"KBD{u}", [128, H0 * KT]) for u in range(2)]
        V0 = [sb(f"V0{u}", [128, NKT, H0, PAD0]) for u in range(2)]
        MB = [sb(f"MB{u}", [T, TC]) for u in range(2)]
        O0 = sb("O0", [128, 4 * T])
        QBD = [sb(f"QBD{s}", [128, T]) for s in range(2)]
        end_stage_buffers()

        stage_buffers()
        FT = [sb(f"FT{u}", [128, DC, T]) for u in range(2)]
        H = [sb(f"H{v}", [128, DC, CH, T]) for v in range(2)]
        R = [sb(f"R{v}", [128, 4 * T]) for v in range(2)]
        RHO = [sb(f"RHO{u}", [T, TCP]) for u in range(2)]
        PEN = sb("PEN", [T, TC])
        soft = [sb(f"soft{u}", [T, 8]) for u in range(2)]
        end_stage_buffers()

        stage_buffers()
        XNA = sb("XNA", [T, B, D])
        QK1 = [sb(f"QK1{u}", [T, 2, NH, HP]) for u in range(2)]
        RA = sb("RA", [T, 2, NH, ROT])
        RB = sb("RB", [T, 2, NH, ROT])
        V1 = [sb(f"V1{u}", [T, NH * HP]) for u in range(2)]
        QT1 = [sb(f"QT1{u}", [128, 4, T]) for u in range(2)]
        KBD1 = [sb(f"KBD1{u}", [128, 4, 2 * T]) for u in range(2)]
        O1 = sb("O1", [128, 4 * T])
        SC = sb("SC", [NH, B, T])
        top = sb("top", [NH, B, 16])
        top_i = sb("top_i", [NH, B, 16], U32)
        rest = sb("rest", [NH, B, T])
        IDX = sb("IDX", [NH, B, KSEL])
        VAL = sb("VAL", [NH, B, KSEL])
        BD = sb("BD", [NH, NH, T])
        POSC = sb("POSC", [T, NH])
        GATE = sb("GATE", [T, NH])
        POSB = sb("POSB", [T, NH, T])
        OH = sb("OH", [T, NH, B, KSEL])
        OHB = sb("OHB", [T, B, NH, KSEL])
        MM = sb("MM", [T, NH, T])
        XG = sb("XG", [128, DC, NH, B, KSEL])
        CS = sb("CS", [T, NH, 2 * ROT])
        POSN = sb("POSN", [T, B])
        Z = sb("Z", [T, NH, D])
        Z2 = sb("Z2", [T, B, D])
        OHR = [sb(f"OHR{u}", [T, T]) for u in range(2)]
        end_stage_buffers()

        consts_in = sem("consts_in")
        weights0_in = sem("weights0_in")
        weights_moe_in = sem("weights_moe_in")
        x_in = sem("x_in")
        small_in = sem("small_in")
        weights_c_in = sem("weights_c_in")
        weights_d_in = sem("weights_d_in")
        qmask_in = sem("qmask_in")
        ctx1_in = [sem(f"ctx1_in{u}") for u in range(2)]
        ctx0_in = [sem(f"ctx0_in{u}") for u in range(2)]
        stored = sem("stored")
        x_updated = sem("x_updated")
        bnd_ready = sem("bnd_ready")
        last_key_full = sem("last_key_full")
        wide_ready = sem("wide_ready")
        wide_full = sem("wide_full")
        wide_set = sem("wide_set")
        tanh_ready = sem("tanh_ready")
        zeroed = sem("zeroed")
        dve_step = sem("dve_step")
        stats_ready = sem("stats_ready")
        rstd_ready = sem("rstd_ready")
        xn_ready = sem("xn_ready")
        ln_step = sem("ln_step")

        steps = {"n": 0}

        def link(dve, ins):
            steps["n"] += 1
            ins.then_inc(dve_step, 1)
            dve.wait_ge(dve_step, steps["n"])

        def layer_norm(dve, pair, n, taken):
            for u in range(2):
                dve.bn_stats(bn[:, u, :], X[:, bass.ds(2 * pair + u, 1), :]).then_inc(ln_step, 1)
            dve.wait_ge(ln_step, n * 4 + 2)
            dve.memset(scratch[:, :], 0.0)
            for u in range(2):
                dve.bn_aggr(mv[:, u, :], bn[:, u, :]).then_inc(ln_step, 1)
            dve.wait_ge(ln_step, n * 4 + 4)
            dve.tensor_scalar(var_eps[:, 0, :], mv[:, :, 1], 1e-5, None, ALU.add).then_inc(stats_ready, 1)
            dve.wait_ge(rstd_ready, n + 1)
            taken()
            for u in range(2):
                dve.tensor_scalar(XN[u][:, :], X[:, bass.ds(2 * pair + u, 1), :].rearrange("p o d -> p (o d)"),
                                  mv[:, u, 0:1], rstd[:, u:u + 1], ALU.subtract, ALU.mult).then_inc(xn_ready, 1)

        def layer_norm_root(pool, n):
            pool.wait_ge(stats_ready, n + 1)
            pool.tensor_tensor(rstd[:, :], var_eps[:, 0, :], var_eps[:, 1, :], ALU.pow).then_inc(rstd_ready, 1)

        def transpose_xn(pe, b, n, u, bank, full):
            pe.wait_ge(xn_ready, n + 1)
            for c in range(DC):
                last = pe.transpose(bank[:, c * T:(c + 1) * T], XN[u][:, c * 128:(c + 1) * 128], ident[0:T, 0:T])
            last.then_inc(full, 1)

        def cross0(nkt):
            nm = "x"
            keys = nkt * KT
            nh = 4 if nkt == 1 else 1
            tiles = 2 * H0 // nh
            per = tiles // 2
            att = Attention(sem, nm, att_bufs, tiles, nh, keys, KT, DH0 ** -0.5)
            kturns = 1 if nkt == 1 else DC
            AT, BT = 1 + kturns, 1 + nkt
            a_full, a_taken = sem(nm + "_a_full"), sem(nm + "_a_taken")
            b_full, b_taken = sem(nm + "_b_full"), sem(nm + "_b_taken")
            o_full, o_taken = sem(nm + "_o_full"), sem(nm + "_o_taken")
            y_full, y_taken = sem(nm + "_y_full"), x_updated
            kbd_ready = sem(nm + "_kbd_ready")
            qbd_ready = sem(nm + "_qbd_ready")
            mask_ready = sem(nm + "_mask_ready")

            def sync(sp):
                for u in range(2):
                    sp.dma_start(CT[u][:, :, :], a["ctxT"][:, :, u * TC:(u + 1) * TC]).then_inc(ctx0_in[u], 16)
                with sp.Fori(1, PAIRS) as i:
                    for u in range(2):
                        sp.wait_ge(b_full, (i - 1) * (2 * BT) + (u + 1) * BT)
                        sp.dma_start(CT[u][:, :, :], a["ctxT"][:, :, bass.ds((2 * i + u) * TC, TC)])\
                          .then_inc(ctx0_in[u], 16)

            def tensor(pe):
                with pe.Fori(0, PAIRS) as i:
                    for u in range(2):
                        b = 2 * i + u
                        at, bt = i * (2 * AT) + u * AT, i * (2 * BT) + u * BT
                        pe.wait_ge(a_taken, at)
                        transpose_xn(pe, b, b, u, ps[0], a_full)
                        pe.wait_ge(a_taken, at + 1)
                        pe.wait_ge(b_taken, bt)
                        for e in range(DC):
                            for c in range(DC):
                                last = pe.matmul(ps[1][:, e * T:(e + 1) * T], wq0[:, c, e * 128:(e + 1) * 128],
                                                 XT[u][:, c, :], start=(c == 0), stop=(c == DC - 1))
                        last.then_inc(b_full, 1)
                        pe.wait_ge(ctx0_in[u], 16 * (i + 1))
                        for k in range(kturns):
                            pe.wait_ge(a_taken, at + 1 + k)
                            es = range(DC) if nkt == 1 else [k]
                            for j, e in enumerate(es):
                                for c in range(DC):
                                    last = pe.matmul(ps[0][:, j * keys:(j + 1) * keys],
                                                     wk0[:, c, e * 128:(e + 1) * 128], CT[u][:, c, 0:keys],
                                                     start=(c == 0), stop=(c == DC - 1))
                            last.then_inc(a_full, 1)
                        for k in range(nkt):
                            pe.wait_ge(b_taken, bt + 1 + k)
                            for c in range(DC):
                                last = pe.matmul(ps[1][0:KT, 0:D], CT[u][:, c, k * KT:(k + 1) * KT], wv0[:, c, :],
                                                 start=(c == 0), stop=(c == DC - 1))
                            last.then_inc(b_full, 1)

                    def scores(g, bank):
                        u, j = g // per, g % per
                        head = j * nh
                        e, k = head // 8, head % 8
                        if j == 0:
                            pe.wait_ge(b_taken, i * (2 * BT) + u * BT + 1)
                            if nkt == 1:
                                pe.wait_ge(kbd_ready, 2 * i + u + 1)
                            else:
                                pe.wait_ge(a_taken, i * (2 * AT) + (u + 1) * AT)
                        if nkt == 1:
                            return pe.matmul(bank[0:T, 0:nh * keys], QT0[u][:, e, :],
                                             KBD[u][:, head * KT:(head + nh) * KT], start=True, stop=True)
                        pe.wait_ge(qbd_ready, i * tiles + g + 1)
                        return pe.matmul(bank[0:T, 0:keys], QBD[g % 2][:, :], KT0[u][:, e, :],
                                         start=True, stop=True)

                    def values(g, probsT):
                        u, j = g // per, g % per
                        if j == 0:
                            pe.wait_ge(b_taken, i * (2 * BT) + (u + 1) * BT)
                            pe.wait_ge(o_taken, 2 * i + u)
                        for h in range(nh):
                            head = j * nh + h
                            r, q = PAD0 * (head % 4), head // 4
                            for k in range(nkt):
                                last = pe.matmul(ps[2][r:r + PAD0, q * T:(q + 1) * T], V0[u][0:KT, k, head, :],
                                                 probsT[0:KT, (h * nkt + k) * T:(h * nkt + k + 1) * T],
                                                 start=(k == 0), stop=(k == nkt - 1))
                        return last

                    def after(g):
                        u, j = g // per, g % per
                        if j == per - 1:
                            b = 2 * i + u
                            pe.wait_ge(o_taken, b + 1)
                            pe.wait_ge(y_taken, b)
                            for q in range(4):
                                pe.matmul(ps[3][0:T, 0:D], O0[:, q * T:(q + 1) * T], wo0[:, q, :],
                                          start=(q == 0), stop=False)
                            pe.matmul(ps[3][0:T, 0:D], const("ones")[0:1, 0:T], bo0[:, :], start=False, stop=True)\
                              .then_inc(y_full, 1)

                    att.tensor(pe, i, scores, values, after)

            def scalar(act):
                with act.Fori(0, PAIRS) as i:
                    for u in range(2):
                        at = i * (2 * AT) + u * AT
                        act.wait_ge(a_full, at + 1)
                        act.activation(XT[u][:, :, :].rearrange("p c t -> p (c t)"), ps[0][:, 0:DC * T], ACT.Copy)\
                           .then_inc(a_taken, 1)
                        for k in range(kturns):
                            act.wait_ge(a_full, at + 2 + k)
                            es = range(DC) if nkt == 1 else [k]
                            for j, e in enumerate(es):
                                last = act.activation(KT0[u][:, e, 0:keys], ps[0][:, j * keys:(j + 1) * keys],
                                                      ACT.Identity, bias=bqk0[:, 1, e:e + 1])
                            last.then_inc(a_taken, 1)

                    def after(g):
                        if g % per == per - 1:
                            b = 2 * i + g // per
                            act.wait_ge(att.values_done[g % 2], i * (tiles // 2) + g // 2 + 1)
                            act.wait_ge(y_full, b)
                            act.activation(O0[:, :], ps[2][:, 0:4 * T], ACT.Copy).then_inc(o_taken, 1)

                    att.scalar(act, i, after)

            def vector(dve):
                with dve.Fori(0, PAIRS) as i:
                    for u in range(2):
                        b = 2 * i + u
                        bt = i * (2 * BT) + u * BT
                        dve.tensor_scalar(MB[u][:, 0:keys], const("keyidx", T)[:, 0:keys],
                                          last_key[:, bass.ds(b, 1)], LOWEST, ALU.is_gt, ALU.mult)\
                           .then_inc(mask_ready, 1)
                        dve.wait_ge(b_full, bt + 1)
                        for e in range(DC):
                            last = dve.tensor_scalar(QT0[u][:, e, :], ps[1][:, e * T:(e + 1) * T],
                                                     bqk0[:, 0, e:e + 1], None, ALU.add)
                        last.then_inc(b_taken, 1)
                        for k in range(nkt):
                            dve.wait_ge(b_full, bt + 2 + k)
                            dve.tensor_tensor(V0[u][0:KT, k, :, 0:DH0],
                                              ps[1][0:KT, 0:D].rearrange("p (h d) -> p h d", h=H0),
                                              bv0[0:KT, :].rearrange("p (h d) -> p h d", h=H0), ALU.add)\
                               .then_inc(b_taken, 1)

                    def mask(g):
                        if g % per == 0:
                            dve.wait_ge(mask_ready, 2 * i + g // per + 1)
                        return MB[g // per][:, 0:keys].unsqueeze(1).to_broadcast([T, nh, keys])

                    def after(g):
                        if g % per == per - 1:
                            b = 2 * i + g // per
                            dve.wait_ge(y_full, b + 1)
                            xb = X[:, bass.ds(b, 1), :].rearrange("p o d -> p (o d)")
                            dve.scalar_tensor_tensor(xb, ps[3][0:T, 0:D], tanh_gates[:, 0:1], xb,
                                                     ALU.mult, ALU.add).then_inc(y_taken, 1)
                        if g == per - 1:
                            layer_norm(dve, (i + 1) & (PAIRS - 1), i + 1,
                                       lambda: dve.wait_ge(a_full, i * (2 * AT) + AT + 1))

                    att.vector(dve, i, mask, after)

            def gpsimd(pool):
                with pool.Fori(0, PAIRS) as i:
                    for u in range(2):
                        pool.wait_ge(a_taken, i * (2 * AT) + (u + 1) * AT)
                        if nkt > 1:
                            continue
                        for e in range(DC):
                            k = KT0[u][:, e, 0:KT].unsqueeze(1).to_broadcast([128, 8, KT])
                            m = const("headmask").unsqueeze(2).to_broadcast([128, 8, KT])
                            last = pool.tensor_tensor(
                                KBD[u][:, e * 8 * KT:(e + 1) * 8 * KT].rearrange("p (h k) -> p h k", h=8), k, m, ALU.mult)
                        last.then_inc(kbd_ready, 1)

                    def before(g):
                        if nkt == 1:
                            return
                        u, head = g // per, g % per
                        if head == 0:
                            pool.wait_ge(b_taken, i * (2 * BT) + u * BT + 1)
                        pool.wait_ge(att.scores_taken[g % 2], i * (tiles // 2) + g // 2)
                        pool.tensor_tensor(QBD[g % 2][:, :], QT0[u][:, head // 8, :],
                                           const("headmask")[:, head % 8:head % 8 + 1].to_broadcast([128, T]), ALU.mult)\
                            .then_inc(qbd_ready, 1)

                    def after(g):
                        if g == per - 1:
                            layer_norm_root(pool, i + 1)

                    att.gpsimd(pool, i, before, after)

            return sync, tensor, scalar, vector, gpsimd

        m_a_full, m_a_taken = sem("m_a_full"), sem("m_a_taken")
        m_logit_full, m_logit_taken = sem("m_logit_full"), sem("m_logit_taken")
        m_neg_max, m_exp = sem("m_neg_max"), sem("m_exp")
        m_gates = sem("m_gates")
        m_gt_full, m_gt_taken = sem("m_gt_full"), sem("m_gt_taken")
        m_bias_full = sem("m_bias_full")
        m_expert_full = sem("m_expert_full")
        m_expert_taken = [sem(f"m_expert_taken{q}") for q in range(4)]
        m_step = sem("m_step")

        def experts_tensor(pe):
            pe.wait_ge(weights_moe_in, 16 * 4)
            with pe.Fori(0, PAIRS) as i:
                for u in range(2):
                    b = 2 * i + u
                    pe.wait_ge(m_a_taken, b)
                    transpose_xn(pe, b, 2 * PAIRS + b, u, ps[0], m_a_full)
                    pe.wait_ge(m_a_taken, b + 1)
                    pe.wait_ge(m_logit_taken, b)
                    for c in range(DC):
                        pe.matmul(ps[1][0:T, 0:NE], XT[u][:, c, :], wg0[:, c, :], start=(c == 0), stop=False)
                    pe.matmul(ps[1][0:T, 0:NE], const("ones")[0:1, 0:T], bg0[:, :], start=False, stop=True)\
                      .then_inc(m_logit_full, 1)
                for u in range(2):
                    b = 2 * i + u
                    for q in range(4):
                        pe.wait_ge(m_expert_taken[q], b)
                        for c in range(DC):
                            last = pe.matmul(ps[2 + q][0:T, :], XT[u][:, c, :], we0[:, c, q * 512:(q + 1) * 512],
                                             start=(c == 0), stop=(c == DC - 1))
                        last.then_inc(m_expert_full, 1)
                        if q == 0:
                            pe.wait_ge(m_gates, b + 1)
                            pe.wait_ge(m_gt_taken, b)
                            pe.transpose(ps[6][0:NE, 0:T], G[u][:, :], ident[0:T, 0:T]).then_inc(m_gt_full, 1)
                    pe.wait_ge(m_gt_taken, b + 1)
                    pe.wait_ge(x_updated, B + b)
                    pe.matmul(ps[7][0:T, 0:D], GT[u][:, :], be0[:, :], start=True, stop=True).then_inc(m_bias_full, 1)

        def experts_scalar(act):
            with act.Fori(0, PAIRS) as i:
                for u in range(2):
                    b = 2 * i + u
                    act.wait_ge(m_a_full, b + 1)
                    act.activation(XT[u][:, :, :].rearrange("p c t -> p (c t)"), ps[0][:, 0:DC * T], ACT.Copy)\
                       .then_inc(m_a_taken, 1)
                    act.wait_ge(m_neg_max, b + 1)
                    act.activation(router[:, 1, :], logit[:, :], ACT.Exp, bias=router[:, 0, 0:1],
                                   accum_out=router[:, 0, 1:2]).then_inc(m_exp, 1)
                for u in range(2):
                    b = 2 * i + u
                    act.wait_ge(m_gt_full, b + 1)
                    act.activation(GT[u][:, :], ps[6][0:NE, 0:T], ACT.Copy).then_inc(m_gt_taken, 1)

        def experts_vector(dve):
            dve.wait_ge(consts_in, 16)
            with dve.Fori(0, PAIRS) as i:
                chain = Chain(dve, m_step, i, 2 * 7 + 2 * 5, scratch[:, :])
                for u in range(2):
                    b = 2 * i + u
                    dve.wait_ge(m_logit_full, b + 1)
                    dve.tensor_copy(logit[:, :], ps[1][0:T, 0:NE]).then_inc(m_logit_taken, 1)
                    dve.wait_ge(m_logit_taken, b + 1)
                    dve.tensor_reduce(router[:, 0, 0:1], logit[:, :], AX_X, ALU.max, negate=True).then_inc(m_neg_max, 1)
                    dve.wait_ge(m_exp, b + 1)
                    chain(dve.reciprocal(router[:, 0, 2:3], router[:, 0, 1:2]))
                    chain(dve.tensor_scalar(router[:, 2, :], router[:, 1, :], router[:, 0, 2:3], None, ALU.mult), carry=True)
                    chain(dve.max(router[:, 3, :], router[:, 2, :]), carry=True)
                    chain(dve.max_index(router_i[:, :], router[:, 3, :], router[:, 2, :]))
                    chain(dve.tensor_copy(router[:, 4, :], router_i[:, :]))
                    for j in range(2):
                        chain(dve.tensor_scalar(router[:, 5 + j, :], const("iota8", T), router[:, 4, j:j + 1],
                                                router[:, 3, j:j + 1], ALU.is_equal, ALU.mult))
                    dve.tensor_tensor(G[u][:, :], router[:, 5, :], router[:, 6, :], ALU.add).then_inc(m_gates, 1)
                    dve.wait_ge(m_gates, b + 1)
                layer_norm(dve, (i + 1) & (PAIRS - 1), PAIRS + i + 1, lambda: dve.wait_ge(m_a_full, 2 * i + 2))
                for u in range(2):
                    b = 2 * i + u
                    for e in range(NE):
                        p = ps[2 + e // 2][0:T, (e % 2) * D:(e % 2 + 1) * D]
                        if e % 2 == 0:
                            dve.wait_ge(m_expert_full, 4 * b + e // 2 + 1)
                        if e == 0:
                            ins = dve.tensor_scalar(Y[:, :], p, G[u][:, e:e + 1], None, ALU.mult)
                        else:
                            ins = dve.scalar_tensor_tensor(Y[:, :], p, G[u][:, e:e + 1], Y[:, :], ALU.mult, ALU.add)
                        if e % 2 == 1:
                            ins.then_inc(m_expert_taken[e // 2], 1)
                            dve.wait_ge(m_expert_taken[e // 2], b + 1)
                        else:
                            chain(ins)
                    dve.wait_ge(m_bias_full, b + 1)
                    chain(dve.tensor_tensor(Y[:, :], Y[:, :], ps[7][0:T, 0:D], ALU.add))
                    xb = X[:, bass.ds(b, 1), :].rearrange("p o d -> p (o d)")
                    dve.scalar_tensor_tensor(xb, Y[:, :], tanh_gates[:, 2:3], xb, ALU.mult, ALU.add)\
                       .then_inc(x_updated, 1)
                    dve.wait_ge(x_updated, B + b + 1)
                chain.end()

        def experts_gpsimd(pool):
            with pool.Fori(0, PAIRS) as i:
                layer_norm_root(pool, PAIRS + i + 1)

        c_ctx_used = sem("c_ctx_used")
        c_a_full, c_a_taken = sem("c_a_full"), sem("c_a_taken")
        c_f_full, c_f_taken = sem("c_f_full"), sem("c_f_taken")
        c_wb_taken = sem("c_wb_taken")
        c_zeroed = sem("c_zeroed")
        c_added = [sem(f"c_added{v}") for v in range(2)]
        c_tanh = [sem(f"c_tanh{v}") for v in range(2)]
        c_rho_full = [sem(f"c_rho_full{v}") for v in range(2)]
        c_rho_taken = [sem(f"c_rho_taken{v}") for v in range(2)]
        c_rhoT_full = [sem(f"c_rhoT_full{v}") for v in range(2)]
        c_rhoT_taken = [sem(f"c_rhoT_taken{v}") for v in range(2)]
        c_neg_max, c_exp, c_recip, c_ws = sem("c_neg_max"), sem("c_exp"), sem("c_recip"), sem("c_ws")
        c_step = sem("c_step")
        reps_ready = sem("reps_ready")
        steps_set = sem("steps_set")

        def prepare_steps(dve):
            dve.wait_ge(qmask_in, 16)
            key = const("keyidx", 1)[:, 0:NCH]
            row = lambda ap: ap.unsqueeze(1).to_broadcast([1, B, NCH])
            link(dve, dve.memset(TT[0][0:1, :, :], 0.0))
            for part in range(B // DC):
                link(dve, dve.tensor_copy(TT[0][0:1, :, 0:TC], qmask_i[0:1, DC * part:DC * (part + 1), :]))
                link(dve, dve.tensor_reduce(live[:, 0, DC * part:DC * (part + 1), :],
                                            TT[0][0:1, :, :].rearrange("p b (c k) -> p b c k", k=CH), AX_X, ALU.max,
                                            apply_absolute_value=True))
            link(dve, dve.tensor_scalar(live[:, 1, :, :], live[:, 0, :, :], 0.0, None, ALU.is_gt))
            link(dve, dve.tensor_scalar(live[:, 2, 0, :], key, -1.0, float(NCH), ALU.mult, ALU.add))
            link(dve, dve.tensor_scalar(live[:, 2, 1, :], key, 1.0, None, ALU.add))
            link(dve, dve.tensor_scalar(live[:, 2, 2, :], key, 2.0, None, ALU.mult))
            link(dve, dve.tensor_tensor(live[:, 3, :, :], live[:, 1, :, :], row(live[:, 2, 0, :]), ALU.mult))
            link(dve, dve.tensor_reduce(span[:, 0, :], live[:, 3, :, :], AX_X, ALU.max))
            link(dve, dve.tensor_tensor(live[:, 3, :, :], live[:, 1, :, :], row(live[:, 2, 1, :]), ALU.mult))
            link(dve, dve.tensor_reduce(span[:, 1, :], live[:, 3, :, :], AX_X, ALU.max))
            link(dve, dve.tensor_scalar(span[:, 2, :], span[:, 0, :], -1.0, float(NCH), ALU.mult, ALU.add))
            link(dve, dve.tensor_tensor(span[:, 3, :], span[:, 1, :], span[:, 2, :], ALU.subtract))
            link(dve, dve.tensor_scalar(span[:, 3, :], span[:, 3, :], 0.0, None, ALU.max))
            link(dve, dve.tensor_tensor(live[:, 3, :, :], span[:, 3, :].unsqueeze(2).to_broadcast([1, B, NCH]),
                                        row(live[:, 2, 2, :]), ALU.is_gt))
            link(dve, dve.tensor_reduce(span[:, 4, :], live[:, 3, :, :], AX_X, ALU.add))
            link(dve, dve.tensor_tensor(span[:, 5, :], span[:, 3, :], span[:, 4, :], ALU.subtract))
            ones = const("ones", 1)[:, 0:B]
            for v in range(2):
                link(dve, dve.tensor_tensor_scan(span[:, 6 + v, :], ones, span[:, 4 + v, :], 0.0, ALU.mult, ALU.add))
            link(dve, dve.tensor_scalar(steps_of[:, :, 0], span[:, 2, :], float(CH), None, ALU.mult))
            link(dve, dve.tensor_copy(steps_of[:, :, 1], span[:, 3, :]))
            for v in range(2):
                link(dve, dve.tensor_tensor(steps_of[:, :, 2 + v], span[:, 6 + v, :], span[:, 4 + v, :], ALU.subtract))
                ins = dve.tensor_copy(steps_of[:, :, 4 + v], span[:, 6 + v, :])
                if v == 0:
                    link(dve, ins)
            ins.then_inc(steps_set, 1)
            dve.wait_ge(steps_set, 1)
            link(dve, dve.memset(TT[0][:, :, TC:TCP], 0.0))
            link(dve, dve.memset(TT[1][:, :, TC:TCP], 0.0))
            dve.wait_ge(weights_c_in, 16 * 6)
            for e in range(DC):
                link(dve, dve.tensor_copy(w1_rep[:, e, :], w1_col[:, e:e + 1].to_broadcast([128, 32])))
                for k in range(2):
                    ins = dve.tensor_copy(wcwb_rep[:, k, e, :], wcwb_col[:, k, e:e + 1].to_broadcast([128, T]))
                    if (e, k) != (1, 1):
                        link(dve, ins)
            ins.then_inc(reps_ready, 1)

        def steps_loop(eng, b, front, back=None, back2=None):
            row0 = eng.value_load(steps_of[0:1, bass.ds(b, 1), 0:1], min_val=0, max_val=TCP)
            count = eng.value_load(steps_of[0:1, bass.ds(b, 1), 1:2], min_val=0, max_val=NCH)
            before = [eng.value_load(steps_of[0:1, bass.ds(b, 1), 2 + v:3 + v], min_val=0, max_val=B * NCH)
                      for v in range(2)]
            skip = lambda *x: None
            row = lambda j: (row0 + j * CH).with_bounds(min_val=0, max_val=TCP - CH)
            back, back2 = back or skip, back2 or skip
            with eng.If(count > 0):
                front(0, before[0], row(0))
            with eng.Fori(0, NCH // 2) as j:
                with eng.If(count > 2 * j):
                    with eng.If(count > 2 * j + 1):
                        front(1, before[1] + j, row(2 * j + 1))
                    back(0, before[0] + j, row(2 * j))
                    with eng.If(count > 2 * j + 2):
                        front(0, before[0] + j + 1, row(2 * j + 2))
                    back2(0, before[0] + j, row(2 * j))
                    with eng.If(count > 2 * j + 1):
                        back(1, before[1] + j, row(2 * j + 1))
                        back2(1, before[1] + j, row(2 * j + 1))

        def additive_sync(sp):
            sp.wait_ge(x_updated, B)
            for u in range(2):
                sp.dma_start(CT[u][:, :, :], a["ctxT"][:, :, u * TC:(u + 1) * TC]).then_inc(ctx1_in[u], 16)
            with sp.Fori(1, PAIRS) as i:
                for u in range(2):
                    sp.wait_ge(c_ctx_used, 2 * (i - 1) + u + 1)
                    sp.dma_start(CT[u][:, :, :], a["ctxT"][:, :, bass.ds((2 * i + u) * TC, TC)]).then_inc(ctx1_in[u], 16)

        def additive_tensor(pe):
            pe.wait_ge(weights_c_in, 16 * 6)
            pe.wait_ge(reps_ready, 1)
            pe.wait_ge(steps_set, 1)
            with pe.Fori(0, PAIRS) as i:
                for u in range(2):
                    b = 2 * i + u
                    pe.wait_ge(c_a_taken, 3 * b)
                    transpose_xn(pe, b, 4 * PAIRS + b, u, ps[0], c_a_full)
                    pe.wait_ge(c_a_taken, 3 * b + 1)
                    pe.wait_ge(c_f_taken, b)
                    for e in range(DC):
                        for c in range(DC):
                            last = pe.matmul(ps[1][:, e * T:(e + 1) * T], wf1[:, c, e * 128:(e + 1) * 128],
                                             XT[u][:, c, :], start=(c == 0), stop=(c == DC - 1))
                    last.then_inc(c_f_full, 1)
                    pe.wait_ge(ctx1_in[u], 16 * (i + 1))
                    for e in range(DC):
                        pe.wait_ge(c_a_taken, 3 * b + 1 + e)
                        for c in range(DC):
                            last = pe.matmul(ps[0][:, 0:TC], ws1[:, c, e * 128:(e + 1) * 128], CT[u][:, c, :],
                                             start=(c == 0), stop=(c == DC - 1))
                        last.then_inc(c_a_full, 1)
                for u in range(2):
                    b = 2 * i + u

                    def front(v, n, row):
                        pe.wait_ge(c_tanh[v], n + 1)
                        pe.wait_ge(c_rho_taken[v], n)
                        for e in range(DC):
                            for q in range(4):
                                last = pe.matmul(ps[4 + v][32 * q:32 * q + 32, 0:4 * T], w1_rep[:, e, :],
                                                 H[v][:, e, 4 * q:4 * q + 4, :].rearrange("p k t -> p (k t)"),
                                                 start=(e == 0), stop=(e == DC - 1))
                        last.then_inc(c_rho_full[v], 1)

                    def back(v, n, row):
                        pe.wait_ge(c_rho_taken[v], n + 1)
                        pe.wait_ge(c_rhoT_taken[v], n)
                        for k in range(4):
                            last = pe.transpose(ps[6 + v][0:T, k * 128:(k + 1) * 128], R[v][:, k * T:(k + 1) * T], ident)
                        last.then_inc(c_rhoT_full[v], 1)

                    steps_loop(pe, b, front, back)
                    pe.wait_ge(c_wb_taken, b)
                    for k in range(2):
                        for c in range(DC):
                            last = pe.matmul(ps[2 + k][0:T, 0:TC], wcwb_rep[:, k, c, :], CT[u][:, c, :],
                                             start=(c == 0), stop=(c == DC - 1))
                    last.then_inc(c_ctx_used, 1)

        def additive_scalar(act):
            act.wait_ge(steps_set, 1)
            with act.Fori(0, PAIRS) as i:
                for u in range(2):
                    b = 2 * i + u
                    act.wait_ge(c_a_full, 3 * b + 1)
                    act.activation(XT[u][:, :, :].rearrange("p c t -> p (c t)"), ps[0][:, 0:DC * T], ACT.Copy)\
                       .then_inc(c_a_taken, 1)
                    for e in range(DC):
                        act.wait_ge(c_a_full, 3 * b + 2 + e)
                        act.activation(TT[u][:, e, 0:TC], ps[0][:, 0:TC], ACT.Copy).then_inc(c_a_taken, 1)
                for u in range(2):
                    b = 2 * i + u

                    def front(v, n, row):
                        act.wait_ge(c_added[v], n + 1)
                        h = H[v][:, :, :, :].rearrange("p e k t -> p (e k t)")
                        act.activation(h, h, ACT.Tanh).then_inc(c_tanh[v], 1)

                    def back(v, n, row):
                        act.wait_ge(c_rho_full[v], n + 1)
                        act.wait_ge(c_rhoT_full[v], n)
                        act.activation(R[v][:, :], ps[4 + v][:, 0:4 * T], ACT.Copy).then_inc(c_rho_taken[v], 1)

                    def back2(v, n, row):
                        act.wait_ge(c_rhoT_full[v], n + 1)
                        act.activation(RHO[u][:, bass.ds(row, CH)].rearrange("p (q k) -> p k q", q=4),
                                       ps[6 + v][0:T, :].rearrange("p (k q r) -> p k q r", k=4, q=4)[:, :, :, 0],
                                       ACT.Copy).then_inc(c_rhoT_taken[v], 1)

                    act.wait_ge(c_zeroed, b + 1)
                    steps_loop(act, b, front, back, back2)
                for u in range(2):
                    b = 2 * i + u
                    act.wait_ge(c_neg_max, b + 1)
                    act.activation(RHO[u][:, 0:TC], RHO[u][:, 0:TC], ACT.Exp, bias=soft[u][:, 0:1],
                                   accum_out=soft[u][:, 1:2]).then_inc(c_exp, 1)
                    act.wait_ge(c_recip, b + 1)
                    for k in range(2):
                        act.activation(soft[u][:, 5 + k:6 + k], soft[u][:, 3 + k:4 + k], ACT.Tanh,
                                       bias=bcwb[:, k:k + 1], scale=soft[u][:, 2:3]).then_inc(c_ws, 1)

        def additive_vector(dve):
            with dve.Fori(0, PAIRS) as i:
                chain = Chain(dve, c_step, i, 2 * 5, scratch[:, :])
                for u in range(2):
                    b = 2 * i + u
                    dve.wait_ge(c_f_full, b + 1)
                    for e in range(DC):
                        last = dve.tensor_scalar(FT[u][:, e, :], ps[1][:, e * T:(e + 1) * T], bf1[:, e:e + 1], None, ALU.add)
                    last.then_inc(c_f_taken, 1)
                for u in range(2):
                    b = 2 * i + u
                    dve.wait_ge(c_f_taken, b + 1)
                    dve.wait_ge(c_a_taken, 3 * b + 3)

                    def front(v, n, row):
                        dve.wait_ge(c_rho_full[v], n)
                        for e in range(DC):
                            t = TT[u][:, e, bass.ds(row, CH)].unsqueeze(2).to_broadcast([128, CH, T])
                            f = FT[u][:, e, :].unsqueeze(1).to_broadcast([128, CH, T])
                            last = dve.tensor_tensor(H[v][:, e, :, :], t, f, ALU.add)
                        last.then_inc(c_added[v], 1)

                    steps_loop(dve, b, front)
                for u in range(2):
                    b = 2 * i + u
                    for v in range(2):
                        end = dve.value_load(steps_of[0:1, bass.ds(b, 1), 4 + v:5 + v], min_val=0, max_val=B * NCH)
                        dve.wait_ge(c_rhoT_taken[v], end)
                    dve.wait_ge(c_zeroed, b + 1)
                    chain(dve.tensor_scalar(PEN[:, :], qmask_i[:, bass.ds(b, 1), :].rearrange("p o k -> p (o k)"),
                                            -MASKED, MASKED, ALU.mult, ALU.add))
                    chain(dve.tensor_tensor(RHO[u][:, 0:TC], RHO[u][:, 0:TC], PEN[:, :], ALU.add))
                    dve.tensor_reduce(soft[u][:, 0:1], RHO[u][:, 0:TC], AX_X, ALU.max, negate=True).then_inc(c_neg_max, 1)
                    dve.wait_ge(c_exp, b + 1)
                    dve.wait_ge(c_ctx_used, b + 1)
                    chain(dve.reciprocal(soft[u][:, 2:3], soft[u][:, 1:2]))
                    for k in range(2):
                        last = dve.tensor_tensor_reduce(PEN[:, :], RHO[u][:, 0:TC], ps[2 + k][0:T, 0:TC], 1.0, 0.0,
                                                        ALU.mult, ALU.add, soft[u][:, 3 + k:4 + k])
                        if k == 0:
                            chain(last)
                    last.then_inc(c_recip, 1)
                    dve.wait_ge(c_recip, b + 1)
                    dve.memset(scratch[:, :], 0.0).then_inc(c_wb_taken, 1)
                    dve.wait_ge(c_ws, 2 * b + 2)
                    chain(dve.tensor_scalar(Y[:, :], XN[u][:, :], soft[u][:, 5:6], soft[u][:, 6:7], ALU.mult, ALU.add))
                    xb = X[:, bass.ds(b, 1), :].rearrange("p o d -> p (o d)")
                    dve.scalar_tensor_tensor(xb, Y[:, :], tanh_gates[:, 1:2], xb, ALU.mult, ALU.add)\
                       .then_inc(x_updated, 1)
                    dve.wait_ge(x_updated, 2 * B + b + 1)
                layer_norm(dve, (i + 1) & (PAIRS - 1), 2 * PAIRS + i + 1, lambda: dve.wait_ge(c_a_full, 6 * i + 6))
                chain.end()

        def additive_gpsimd(pool):
            for u in range(2):
                pool.memset(RHO[u][:, :], 0.0).then_inc(c_zeroed, 1)
            zero = zeros[:, :].to_broadcast([T, TCP])
            with pool.Fori(0, PAIRS) as i:
                for u in range(2):
                    pool.wait_ge(x_updated, 2 * B + 2 * i + u + 1)
                    pool.tensor_tensor(RHO[u][:, :], zero, zero, ALU.mult).then_inc(c_zeroed, 1)
                layer_norm_root(pool, 2 * PAIRS + i + 1)
            pool.wait_ge(c_zeroed, 2 + B)

        PER1 = 2
        dense = Attention(sem, "d", att_bufs, 2 * PER1, 4, T, T, HP ** -0.5)
        d_a_full, d_a_taken = sem("d_a_full"), sem("d_a_taken")
        d_q_full, d_q_taken = sem("d_q_full"), sem("d_q_taken")
        d_v_full, d_v_taken = sem("d_v_full"), sem("d_v_taken")
        d_o_taken = sem("d_o_taken")
        d_rope_step, d_roped = sem("d_rope_step"), sem("d_roped")
        d_kept = sem("d_kept")
        d_zeroed = sem("d_zeroed")
        d_y_full = sem("d_y_full")

        def rotate(eng, qk, cos, sin, step, base, done):
            h = ROT // 2
            ins = eng.tensor_tensor(RA[:, :, :, :], qk[:, :, :, 0:ROT], cos, ALU.mult)
            ins.then_inc(step, 1)
            for r in range(2):
                eng.tensor_tensor(RB[:, :, :, r * h:(r + 1) * h], qk[:, :, :, (1 - r) * h:(2 - r) * h],
                                  sin[:, :, :, r * h:(r + 1) * h], ALU.mult).then_inc(step, 1)
            eng.wait_ge(step, base + 3)
            eng.tensor_tensor(qk[:, :, :, 0:ROT], RA[:, :, :, :], RB[:, :, :, :], ALU.add).then_inc(done, 1)

        def transpose_qk(pe, qk, full, taken, at):
            for k in range(2):
                pe.wait_ge(taken, at + k)
                for q in range(4):
                    last = pe.transpose(ps[0][:, q * T:(q + 1) * T],
                                        qk[:, k, 2 * q:2 * q + 2, :].rearrange("p h d -> p (h d)"), ident[0:T, 0:T])
                last.then_inc(full, 1)

        def take_qk(act, qt, kbd, full, taken, at):
            act.wait_ge(full, at + 1)
            act.activation(qt[:, :, :].rearrange("p q t -> p (q t)"), ps[0][:, 0:4 * T], ACT.Copy).then_inc(taken, 1)
            act.wait_ge(full, at + 2)
            for k in range(2):
                last = act.activation(kbd[64 * k:64 * k + 64, :, k * T:(k + 1) * T],
                                      ps[0][64 * k:64 * k + 64, 0:4 * T].rearrange("p (q t) -> p q t", q=4), ACT.Copy)
            last.then_inc(taken, 1)

        def pair_scores(pe, bank, qt, kbd, first, n):
            for k in range(n):
                last = pe.matmul(bank[0:T, k * 2 * T:(k + 1) * 2 * T], qt[:, first + k, :], kbd[:, first + k, :],
                                 start=True, stop=True)
            return last

        def pair_values(pe, v, probsT, first, n):
            for k in range(n):
                head = first + k
                r = 64 * (head % 2)
                last = pe.matmul(ps[3][r:r + 64, (head // 2) * T:(head // 2 + 1) * T], v[:, head * HP:(head + 1) * HP],
                                 probsT[0:T, k * T:(k + 1) * T], start=True, stop=True)
            return last

        def dense_tensor(pe):
            pe.wait_ge(weights_d_in, 16 * 5)
            with pe.Fori(0, PAIRS) as i:
                for u in range(2):
                    b = 2 * i + u
                    pe.wait_ge(d_a_taken, 3 * b)
                    transpose_xn(pe, b, 6 * PAIRS + b, u, ps[0], d_a_full)
                    pe.wait_ge(d_a_taken, 3 * b + 1)
                    for k in range(2):
                        pe.wait_ge(d_q_taken, 2 * b + k)
                        for c in range(DC):
                            last = pe.matmul(ps[1][0:T, :], XT[u][:, c, :], wqkv1[:, c, k * 512:(k + 1) * 512],
                                             start=(c == 0), stop=(c == DC - 1))
                        last.then_inc(d_q_full, 1)
                    pe.wait_ge(d_v_taken, 2 * b)
                    pe.wait_ge(x_updated, 3 * B + 2 * i)
                    for c in range(DC):
                        last = pe.matmul(ps[2][0:T, :], XT[u][:, c, :], wqkv1[:, c, 1024:1536],
                                         start=(c == 0), stop=(c == DC - 1))
                    last.then_inc(d_v_full, 1)
                    pe.wait_ge(d_v_taken, 2 * b + 1)
                    for c in range(DC):
                        last = pe.matmul(ps[2][0:NH, 0:T], wr1[:, c, :], XT[u][:, c, :], start=(c == 0), stop=(c == DC - 1))
                    last.then_inc(d_v_full, 1)
                    pe.wait_ge(d_roped, b + 1)
                    transpose_qk(pe, QK1[u], d_a_full, d_a_taken, 3 * b + 1)

                def scores(g, bank):
                    u, j = g // PER1, g % PER1
                    if j == 0:
                        pe.wait_ge(d_a_taken, 3 * (2 * i + u) + 3)
                    return pair_scores(pe, bank, QT1[u], KBD1[u], 2 * j, 2)

                def values(g, probsT):
                    u, j = g // PER1, g % PER1
                    if j == 0:
                        pe.wait_ge(d_o_taken, 2 * i + u)
                    return pair_values(pe, V1[u], probsT, 4 * j, 4)

                def after(g):
                    u, j = g // PER1, g % PER1
                    if j == PER1 - 1:
                        b = 2 * i + u
                        pe.wait_ge(d_o_taken, b + 1)
                        pe.wait_ge(x_updated, 3 * B + b)
                        pe.wait_ge(d_v_taken, 4 * i + 4)
                        for q in range(4):
                            last = pe.matmul(ps[2][0:T, 0:D], O1[:, q * T:(q + 1) * T], wo1[:, q, :],
                                             start=(q == 0), stop=(q == 3))
                        last.then_inc(d_y_full, 1)

                dense.tensor(pe, i, scores, values, after)

        def dense_scalar(act):
            act.wait_ge(d_zeroed, 2)
            with act.Fori(0, PAIRS) as i:
                for u in range(2):
                    b = 2 * i + u
                    act.wait_ge(d_a_full, 3 * b + 1)
                    act.activation(XT[u][:, :, :].rearrange("p c t -> p (c t)"), ps[0][:, 0:DC * T], ACT.Copy)\
                       .then_inc(d_a_taken, 1)
                    for k in range(2):
                        act.wait_ge(d_q_full, 2 * b + k + 1)
                        act.activation(QK1[u][:, k, :, :].rearrange("p h d -> p (h d)"), ps[1][0:T, :], ACT.Copy)\
                           .then_inc(d_q_taken, 1)
                    take_qk(act, QT1[u], KBD1[u], d_a_full, d_a_taken, 3 * b + 1)

                def after(g):
                    if g % PER1 == PER1 - 1:
                        b = 2 * i + g // PER1
                        act.wait_ge(dense.values_done[g % 2], i * PER1 + g // 2 + 1)
                        act.wait_ge(d_y_full, b)
                        act.activation(O1[:, :], ps[3][:, 0:4 * T], ACT.Copy).then_inc(d_o_taken, 1)

                dense.scalar(act, i, after)

        def dense_vector(dve):
            with dve.Fori(0, PAIRS) as i:
                for u in range(2):
                    b = 2 * i + u
                    dve.wait_ge(d_v_full, 2 * b + 1)
                    dve.tensor_copy(V1[u][:, :], ps[2][0:T, :]).then_inc(d_v_taken, 1)
                    dve.wait_ge(d_v_full, 2 * b + 2)
                    dve.tensor_copy(SC[:, bass.ds(b, 1), :].rearrange("p o t -> p (o t)"), ps[2][0:NH, 0:T])\
                       .then_inc(d_v_taken, 1)

                def mask(g):
                    return const("causal", T).unsqueeze(1).to_broadcast([T, 4, T])

                def after(g):
                    if g % PER1 == PER1 - 1:
                        b = 2 * i + g // PER1
                        dve.wait_ge(d_y_full, b + 1)
                        xb = X[:, bass.ds(b, 1), :].rearrange("p o d -> p (o d)")
                        dve.scalar_tensor_tensor(xb, ps[2][0:T, 0:D], tanh_gates[:, 3:4], xb, ALU.mult, ALU.add)\
                           .then_inc(x_updated, 1)
                    if g == 0:
                        layer_norm(dve, (i + 1) & (PAIRS - 1), 3 * PAIRS + i + 1,
                                   lambda: (dve.wait_ge(d_a_full, 6 * i + 6), dve.wait_ge(d_kept, 2 * i + 2)))

                dense.vector(dve, i, mask, after)

        def dense_gpsimd(pool):
            cos = const("cos", T).unsqueeze(1).unsqueeze(1).to_broadcast([T, 2, NH, ROT])
            sin = const("sin", T).unsqueeze(1).unsqueeze(1).to_broadcast([T, 2, NH, ROT])
            pool.wait_ge(x_updated, 3 * B)
            for u in range(2):
                pool.memset(KBD1[u][:, :, :], 0.0).then_inc(d_zeroed, 1)
            with pool.Fori(0, PAIRS) as i:
                for u in range(2):
                    b = 2 * i + u
                    pool.wait_ge(xn_ready, 6 * PAIRS + b + 1)
                    pool.tensor_copy(XNA[:, bass.ds(b, 1), :].rearrange("p o d -> p (o d)"), XN[u][:, :]).then_inc(d_kept, 1)
                    pool.wait_ge(d_q_taken, 2 * b + 2)
                    rotate(pool, QK1[u][:, :, :, :], cos, sin, d_rope_step, 3 * b, d_roped)

                def after(g):
                    if g == 0:
                        layer_norm_root(pool, 3 * PAIRS + i + 1)

                dense.gpsimd(pool, i, lambda g: None, after)

        mosa = Attention(sem, "d", att_bufs, dense.tiles, NH // RING, T, T, HP ** -0.5)
        assert mosa.tiles == RING
        o_step = sem("o_step")
        o_picked, o_cols_full = sem("o_picked"), sem("o_cols_full")
        o_bd, o_pos_full, o_pos_taken = sem("o_bd"), sem("o_pos_full"), sem("o_pos_taken")
        o_onehot = sem("o_onehot")
        o_g_full, o_g_taken = sem("o_g_full"), sem("o_g_taken")
        o_cs_full, o_cs_taken = sem("o_cs_full"), sem("o_cs_taken")
        o_pn_full, o_pn_taken = sem("o_pn_full"), sem("o_pn_taken")
        o_qkv_full, o_qkv_taken = sem("o_qkv_full"), sem("o_qkv_taken")
        o_rope_step, o_roped = sem("o_rope_step"), sem("o_roped")
        o_a_full, o_a_taken = sem("o_a_full"), sem("o_a_taken")
        o_mask, o_halved, o_gate = sem("o_mask"), sem("o_halved"), sem("o_gate")
        o_o_taken = sem("o_o_taken")
        o_z_full, o_z_taken = sem("o_z_full"), sem("o_z_taken")
        o_z_out, o_z_in = sem("o_z_out"), sem("o_z_in")
        o_row = sem("o_row")
        o_y_full = sem("o_y_full")
        z_rows = nc.dram_tensor("z_rows", (T, NH, D), F32, kind="Internal").ap()

        def mosa_sync(sp):
            sp.wait_ge(o_z_taken, NH)
            sp.dma_start(z_rows, Z[:, :, :]).then_inc(o_z_out, 16)
            sp.wait_ge(o_z_out, 16)
            by_head = z_rows.rearrange("(b j) n d -> n j b d", b=B)
            for n in range(NH):
                sp.dma_start(Z2[n * KSEL:(n + 1) * KSEL, :, :], by_head[n]).then_inc(o_z_in, 16)
            with sp.Fori(0, B) as b:
                sp.wait_ge(x_updated, 4 * B + b + 1)
                sp.dma_start(out[bass.ds(b, 1), :, :].rearrange("o t d -> t (o d)"),
                             X[:, bass.ds(b, 1), :].rearrange("p o d -> p (o d)")).then_inc(stored, 16)
            sp.wait_ge(stored, 16 * B)

        def mosa_tensor(pe):
            pe.wait_ge(o_picked, 2)
            pe.transpose(ps[1][0:T, 0:NH], IDX[:, :, :].rearrange("n b j -> n (b j)"), ident[0:NH, 0:NH])
            pe.transpose(ps[1][0:T, NH:2 * NH], VAL[:, :, :].rearrange("n b j -> n (b j)"), ident[0:NH, 0:NH])\
              .then_inc(o_cols_full, 1)
            pe.wait_ge(o_bd, 1)
            for k in range(2):
                pe.matmul(ps[4 + k][0:T, 0:4 * T], const("ones", NH)[:, 0:T],
                          BD[:, 4 * k:4 * k + 4, :].rearrange("p n r -> p (n r)"), start=True, stop=True)\
                  .then_inc(o_pos_full, 1)
            pe.wait_ge(o_onehot, 1)
            for n in range(NH):
                last = pe.matmul(ps[6][0:T, n * 2 * ROT:(n + 1) * 2 * ROT], OH[:, n, :, :].rearrange("p b j -> p (b j)"),
                                 consts[0:T, CONST["cos"][0]:CONST["sin"][1]], start=True, stop=True)
            last.then_inc(o_cs_full, 1)
            for turn in range(4):
                c, half = turn // 2, turn % 2
                if turn >= 2:
                    pe.wait_ge(o_g_taken, turn - 1)
                for b in range(4):
                    last = pe.matmul(ps[2 * (turn % 2)][:, b * T:(b + 1) * T], XNA[:, 4 * half + b, c * 128:(c + 1) * 128],
                                     OH[:, :, 4 * half + b, :], start=True, stop=True)
                last.then_inc(o_g_full, 1)
            pe.wait_ge(o_onehot, 2)
            for b in range(B):
                last = pe.matmul(ps[7][0:T, b:b + 1], OHB[:, b, :, :].rearrange("p n j -> p (n j)"), const("tokcol", T),
                                 start=True, stop=True)
            last.then_inc(o_pn_full, 1)
            pe.wait_ge(o_g_taken, 4)
            pe.wait_ge(o_pos_taken, 2)
            for turn in range(4):
                if turn >= 2:
                    pe.wait_ge(o_qkv_taken, turn - 1)
                for k in range(2):
                    n = 2 * turn + k
                    for c in range(DC):
                        last = pe.matmul(ps[4 + turn % 2][0:T, k * 3 * HP:(k + 1) * 3 * HP],
                                         XG[:, c, n, :, :].rearrange("p b j -> p (b j)"), wqkvm[:, c, n, :],
                                         start=(c == 0), stop=(c == DC - 1))
                last.then_inc(o_qkv_full, 1)
            pe.wait_ge(o_roped, 1)
            transpose_qk(pe, QK1[0], o_a_full, o_a_taken, 0)
            pe.wait_ge(o_a_taken, 2)
            pe.wait_ge(o_qkv_taken, 4)
            pe.wait_ge(o_cs_taken, 1)
            pe.wait_ge(o_pn_taken, 1)

            mosa.tensor(pe, PAIRS, lambda g, bank: pair_scores(pe, bank, QT1[0], KBD1[0], g, 1),
                        lambda g, probsT: pair_values(pe, V1[0], probsT, 2 * g, 2), lambda g: None)
            pe.wait_ge(o_o_taken, 1)
            for turn in range(4):
                if turn >= 2:
                    pe.wait_ge(o_z_taken, 2 * (turn - 1))
                for k in range(2):
                    n = 4 * (turn // 2) + 2 * k + turn % 2
                    r = 64 * (n % 2)
                    last = pe.matmul(ps[1 + turn % 2][0:T, k * D:(k + 1) * D],
                                     O1[r:r + 64, (n // 2) * T:(n // 2 + 1) * T], wom[r:r + 64, n // 2, :],
                                     start=True, stop=True)
                last.then_inc(o_z_full, 1)
            pe.wait_ge(o_z_in, 16 * NH)
            with pe.Fori(0, PAIRS) as i:
                for u in range(2):
                    b = 2 * i + u
                    pe.wait_ge(o_row, b + 1)
                    pe.wait_ge(x_updated, 4 * B + 2 * i)
                    pe.matmul(ps[6 + u][0:T, 0:D], OHR[u][:, :], Z2[:, bass.ds(b, 1), :].rearrange("p o d -> p (o d)"),
                              start=True, stop=True).then_inc(o_y_full, 1)

        def mosa_scalar(act):
            act.wait_ge(o_halved, 1)
            act.activation(GATE[:, :], GATE[:, :], ACT.Tanh).then_inc(o_gate, 1)
            for k in range(2):
                act.wait_ge(o_pos_full, k + 1)
                act.activation(POSB[:, 4 * k:4 * k + 4, :].rearrange("p n r -> p (n r)"), ps[4 + k][0:T, 0:4 * T],
                               ACT.Copy).then_inc(o_pos_taken, 1)
            act.wait_ge(o_cs_full, 1)
            act.activation(CS[:, :, :].rearrange("p n r -> p (n r)"), ps[6][0:T, :], ACT.Copy).then_inc(o_cs_taken, 1)
            for turn in range(4):
                c, half = turn // 2, turn % 2
                act.wait_ge(o_g_full, turn + 1)
                act.activation(XG[:, c, :, 4 * half:4 * half + 4, :].rearrange("p n b j -> p b n j"),
                               ps[2 * (turn % 2)][:, 0:4 * T].rearrange("p (b n j) -> p b n j", b=4, n=NH), ACT.Copy)\
                   .then_inc(o_g_taken, 1)
            for turn in range(4):
                act.wait_ge(o_qkv_full, turn + 1)
                src = ps[4 + turn % 2][0:T, 0:6 * HP].rearrange("p (n k d) -> p n k d", n=2, k=3)
                for k in range(2):
                    act.activation(QK1[0][:, k, 2 * turn:2 * turn + 2, :], src[:, :, k, :], ACT.Copy)
                act.activation(V1[0][:, 2 * turn * HP:(2 * turn + 2) * HP].rearrange("p (n d) -> p n d", n=2),
                               src[:, :, 2, :], ACT.Copy).then_inc(o_qkv_taken, 1)
            take_qk(act, QT1[0], KBD1[0], o_a_full, o_a_taken, 0)
            mosa.scalar(act, PAIRS, lambda g: None)
            for s in range(2):
                act.wait_ge(mosa.values_done[s], (PAIRS + 1) * RING // 2)
            act.activation(O1[:, :], ps[3][:, 0:4 * T], ACT.Copy).then_inc(o_o_taken, 1)

        def mosa_vector(dve):
            chain = Chain(dve, o_step, 0, 0, scratch[:, :])
            dve.wait_ge(d_v_taken, 2 * B)
            dve.memset(scratch[:, :], 0.0)
            def each(step):
                for b in range(B):
                    last = step(b)
                chain(last)
            each(lambda b: dve.max(top[:, b, 0:8], SC[:, b, :]))
            each(lambda b: dve.match_replace(rest[:, b, :], top[:, b, 0:8], SC[:, b, :], LOWEST))
            each(lambda b: dve.max(top[:, b, 8:16], rest[:, b, :]))
            each(lambda b: dve.max_index(top_i[:, b, 0:8], top[:, b, 0:8], SC[:, b, :]))
            each(lambda b: dve.max_index(top_i[:, b, 8:16], top[:, b, 8:16], rest[:, b, :]))
            dve.tensor_copy(IDX[:, :, :], top_i[:, :, 0:KSEL]).then_inc(o_picked, 1)
            dve.tensor_copy(VAL[:, :, :], top[:, :, 0:KSEL]).then_inc(o_picked, 1)
            dve.wait_ge(o_picked, 2)
            idx = IDX[:, :, :].rearrange("n b j -> n (b j)").unsqueeze(1).to_broadcast([NH, NH, T])
            diag = ident[0:NH, 0:NH].unsqueeze(2).to_broadcast([NH, NH, T])
            dve.tensor_tensor(BD[:, :, :], idx, diag, ALU.mult).then_inc(o_bd, 1)
            dve.wait_ge(o_cols_full, 1)
            dve.tensor_copy(POSC[:, :], ps[1][0:T, 0:NH])
            dve.tensor_scalar(GATE[:, :], ps[1][0:T, NH:2 * NH], 0.5, None, ALU.mult).then_inc(o_halved, 1)
            dve.wait_ge(o_halved, 1)
            dve.wait_ge(o_pos_taken, 2)
            tok = const("tokcol", T)
            dve.tensor_scalar(OH[:, :, :, :].rearrange("p n b j -> p (n b j)"), POSB[:, :, :].rearrange("p n r -> p (n r)"),
                              tok, None, ALU.is_equal).then_inc(o_onehot, 1)
            dve.tensor_scalar(OHB[:, :, :, :].rearrange("p b n j -> p n b j"),
                              POSB[:, :, :].rearrange("p n (b j) -> p n b j", b=B),
                              tok, None, ALU.is_equal).then_inc(o_onehot, 1)
            for n in range(NH):
                last = dve.tensor_scalar(MM[:, n, :], POSB[:, n, :], POSC[:, n:n + 1], MASKED, ALU.is_gt, ALU.mult)
            chain(last)
            dve.tensor_tensor(MM[:, :, :], MM[:, :, :], const("batchmask", T).unsqueeze(1).to_broadcast([T, NH, T]), ALU.min)\
               .then_inc(o_mask, 1)
            dve.wait_ge(o_pn_full, 1)
            dve.tensor_copy(POSN[:, :], ps[7][0:T, 0:B]).then_inc(o_pn_taken, 1)
            dve.wait_ge(o_mask, 1)
            mosa.vector(dve, PAIRS, lambda g: MM[:, 2 * g:2 * g + 2, :], lambda g: None)
            dve.wait_ge(o_gate, 1)
            chain(dve.tensor_scalar(GATE[:, :], GATE[:, :], 0.5, 0.5, ALU.mult, ALU.add))
            for turn in range(4):
                dve.wait_ge(o_z_full, turn + 1)
                for k in range(2):
                    n = 4 * (turn // 2) + 2 * k + turn % 2
                    dve.tensor_scalar(Z[:, n, :], ps[1 + turn % 2][0:T, k * D:(k + 1) * D], GATE[:, n:n + 1], None, ALU.mult)\
                       .then_inc(o_z_taken, 1)
            dve.wait_ge(o_pn_taken, 1)
            with dve.Fori(0, PAIRS) as i:
                for u in range(2):
                    b = 2 * i + u
                    dve.wait_ge(o_y_full, 2 * i)
                    dve.tensor_scalar(OHR[u][:, :], const("tokrow", T), POSN[:, bass.ds(b, 1)], None, ALU.is_equal)\
                       .then_inc(o_row, 1)
                for u in range(2):
                    b = 2 * i + u
                    dve.wait_ge(o_y_full, b + 1)
                    xb = X[:, bass.ds(b, 1), :].rearrange("p o d -> p (o d)")
                    dve.scalar_tensor_tensor(xb, ps[6 + u][0:T, 0:D], tanh_gates[:, 3:4], xb, ALU.mult, ALU.add)\
                       .then_inc(x_updated, 1)

        def mosa_gpsimd(pool):
            pool.wait_ge(o_cs_taken, 1)
            pool.wait_ge(o_qkv_taken, 4)
            cos = CS[:, :, 0:ROT].unsqueeze(1).to_broadcast([T, 2, NH, ROT])
            sin = CS[:, :, ROT:2 * ROT].unsqueeze(1).to_broadcast([T, 2, NH, ROT])
            rotate(pool, QK1[0][:, :, :, :], cos, sin, o_rope_step, 0, o_roped)
            mosa.gpsimd(pool, PAIRS, lambda g: None, lambda g: None)

        narrow, wide = cross0(1), cross0(NKT)
        SYNC, PE_, ACT_, DVE_, POOL_ = range(5)

        def cross0_on(eng, which):
            eng.wait_ge(wide_set, 1)
            flag = eng.value_load(wide_i[0:1, 0:1], min_val=0, max_val=2)
            with eng.If(flag == 0):
                narrow[which](eng)
            with eng.Else():
                wide[which](eng)

        block = ctx.enter_context(nc.Block())

        @block.sync
        def _(sp):
            sp.dma_start(consts[:, :], a["consts"]).then_inc(consts_in, 16)
            sp.dma_start(bnd_i[:, :], a["boundsT"]).then_inc(small_in, 16)
            sp.dma_start(X[:, :, :], a["x"].rearrange("b t d -> t b d")).then_inc(x_in, 16)
            for w, name in ((wq0, "wqT0"), (wk0, "wkT0"), (wv0, "wvT0"), (wo0, "woT0")):
                sp.dma_start(w[:, :, :], a[name]).then_inc(weights0_in, 16)
            sp.dma_start(bqk0[:, :, :], a["bqk0"]).then_inc(weights0_in, 16)
            sp.dma_start(bv0[:, :], a["bv0"].partition_broadcast(128)).then_inc(weights0_in, 16)
            sp.dma_start(bo0[:, :], a["bo0"].partition_broadcast(1)).then_inc(weights0_in, 16)
            sp.dma_start(gates[:, :], a["gates"].partition_broadcast(T)).then_inc(small_in, 16)
            for w, name in ((wg0, "wgT0"), (we0, "weT0")):
                sp.dma_start(w[:, :, :], a[name]).then_inc(weights_moe_in, 16)
            sp.dma_start(bg0[:, :], a["bg0"].partition_broadcast(1)).then_inc(weights_moe_in, 16)
            sp.dma_start(be0[:, :], a["be0"]).then_inc(weights_moe_in, 16)
            sp.dma_start(qmask_i[:, :, :], a["qmask"].rearrange("b t -> (b t)").partition_broadcast(T)).then_inc(qmask_in, 16)
            for w, name in ((ws1, "ws1"), (wf1, "wf1")):
                sp.dma_start(w[:, :, :], a[name]).then_inc(weights_c_in, 16)
            sp.dma_start(w1_col[:, :], a["w1_col"]).then_inc(weights_c_in, 16)
            sp.dma_start(wcwb_col[:, :, :], a["wcwb_col"]).then_inc(weights_c_in, 16)
            sp.dma_start(bf1[:, :], a["bf1"]).then_inc(weights_c_in, 16)
            sp.dma_start(bcwb[:, :], a["bcwb"].partition_broadcast(T)).then_inc(weights_c_in, 16)
            for w, name in ((wqkv1, "wqkv1"), (wo1, "wo1"), (wr1, "wr1"), (wom, "wom")):
                sp.dma_start(w[:, :, :], a[name]).then_inc(weights_d_in, 16)
            sp.dma_start(wqkvm[:, :, :, :].rearrange("p c h d -> p c (h d)"), a["wqkvm"]).then_inc(weights_d_in, 16)
            cross0_on(sp, SYNC)
            additive_sync(sp)
            mosa_sync(sp)

        @block.tensor
        def _(pe):
            pe.wait_ge(consts_in, 16)
            pe.wait_ge(bnd_ready, 1)
            pe.matmul(ps[3][0:T, 0:B], const("tri", T), bnd_f[:, :], start=True, stop=True).then_inc(last_key_full, 1)
            pe.wait_ge(wide_ready, 1)
            pe.transpose(ps[3][0:1, 0:T], wide_col[:, :], ident[0:T, 0:T]).then_inc(wide_full, 1)
            pe.wait_ge(weights0_in, 16 * 7)
            pe.wait_ge(zeroed, 1)
            cross0_on(pe, PE_)
            experts_tensor(pe)
            additive_tensor(pe)
            dense_tensor(pe)
            mosa_tensor(pe)

        @block.scalar
        def _(act):
            act.wait_ge(small_in, 32)
            act.activation(tanh_gates[:, :], gates[:, :], ACT.Tanh).then_inc(tanh_ready, 1)
            act.wait_ge(weights0_in, 16 * 7)
            cross0_on(act, ACT_)
            experts_scalar(act)
            additive_scalar(act)
            dense_scalar(act)
            mosa_scalar(act)

        @block.vector
        def _(dve):
            dve.wait_ge(small_in, 32)
            dve.tensor_copy(bnd_f[:, :], bnd_i[:, :]).then_inc(bnd_ready, 1)
            link(dve, dve.memset(var_eps[:, 1, :], -0.5))
            dve.wait_ge(last_key_full, 1)
            link(dve, dve.tensor_copy(last_key[:, :], ps[3][0:T, 0:B]))
            link(dve, dve.tensor_scalar(beyond[:, 0, :], last_key[:, :], KT - 1.0, None, ALU.is_gt))
            link(dve, dve.tensor_scalar(beyond[:, 1, :], last_key[:, :], 0.0, None, ALU.is_lt))
            link(dve, dve.tensor_tensor(beyond[:, 2, :], beyond[:, 0, :], beyond[:, 1, :], ALU.add))
            dve.tensor_reduce(wide_col[:, :], beyond[:, 2, :], AX_X, ALU.max).then_inc(wide_ready, 1)
            dve.wait_ge(wide_full, 1)
            dve.tensor_reduce(wide_i[:, :], ps[3][0:1, 0:T], AX_X, ALU.max).then_inc(wide_set, 1)
            dve.wait_ge(x_in, 16)
            layer_norm(dve, 0, 0, lambda: None)
            prepare_steps(dve)
            dve.wait_ge(weights0_in, 16 * 7)
            dve.wait_ge(tanh_ready, 1)
            dve.wait_ge(zeroed, 1)
            cross0_on(dve, DVE_)
            experts_vector(dve)
            additive_vector(dve)
            dense_vector(dve)
            mosa_vector(dve)

        @block.gpsimd
        def _(pool):
            pool.memset(zeros[:, :], 0.0)
            for u in range(2):
                last = pool.memset(V0[u][:, :, :, :], 0.0)
            last.then_inc(zeroed, 1)
            layer_norm_root(pool, 0)
            pool.wait_ge(consts_in, 16)
            cross0_on(pool, POOL_)
            experts_gpsimd(pool)
            additive_gpsimd(pool)
            dense_gpsimd(pool)
            mosa_gpsimd(pool)


def layout(i):
    import numpy as np
    n = {k: np.asarray(v) for k, v in i.items()}

    def rows(w):
        return np.ascontiguousarray(w.reshape(w.shape[0] // 128, 128, -1).transpose(1, 0, 2))

    a = {"x": np.ascontiguousarray(n["x"])}
    a["ctxT"] = rows(n["ctx_1024"].transpose(2, 0, 1).reshape(D, B * TC))
    a["boundsT"] = np.ascontiguousarray(n["mask_BxS_ik0"].T)
    a["wqT0"] = rows(n["L0_xattn_wq"].T)
    a["wkT0"] = rows(n["L0_xattn_wk"].T)
    a["wvT0"] = rows(n["L0_xattn_wv"].T)
    wo = np.zeros((128, 4, D), n["L0_xattn_wo"].dtype)
    for q in range(4):
        for h in range(4):
            head = 4 * q + h
            wo[PAD0 * h:PAD0 * h + DH0, q] = n["L0_xattn_wo"].T[head * DH0:(head + 1) * DH0]
    a["woT0"] = wo
    a["bqk0"] = np.ascontiguousarray(np.stack([n["L0_xattn_bq"], n["L0_xattn_bk"]]).reshape(2, DC, 128).transpose(2, 0, 1))
    a["bv0"] = n["L0_xattn_bv"]
    a["bo0"] = n["L0_xattn_bo"]
    a["wgT0"] = rows(n["L0_ffn_Wg"].T)
    a["bg0"] = n["L0_ffn_bg"]
    a["weT0"] = rows(n["L0_ffn_W"].transpose(2, 0, 1).reshape(D, NE * D))
    a["be0"] = n["L0_ffn_b"]
    a["qmask"] = np.ascontiguousarray(n["mask_BxS2_ik0"])
    a["ws1"] = rows(n["L1_xattn_Ws"])
    a["wf1"] = rows(n["L1_xattn_W"])
    a["w1_col"] = np.ascontiguousarray(n["L1_xattn_w"].reshape(DC, 128).T)
    a["wcwb_col"] = np.ascontiguousarray(
        np.concatenate([n["L1_xattn_Wcw"], n["L1_xattn_Wcb"]]).reshape(2, DC, 128).transpose(2, 0, 1))
    a["bf1"] = np.ascontiguousarray(n["L1_xattn_b"].reshape(DC, 128).T)
    a["bcwb"] = np.concatenate([n["L1_xattn_bcw"], n["L1_xattn_bcb"]])
    a["wqkv1"] = rows(n["L1_ffn_dense_wqkv"].reshape(D, NH, 3, HP).transpose(0, 2, 1, 3).reshape(D, 3 * NH * HP))
    a["wo1"] = rows(n["L1_ffn_dense_wo"])
    a["wr1"] = rows(n["L1_ffn_mosa_router_w"])
    a["wqkvm"] = rows(n["L1_ffn_mosa_wqkv"].reshape(D, NH * 3 * HP))
    a["wom"] = rows(n["L1_ffn_mosa_wo"])
    a["gates"] = np.concatenate([n["g_xattn"], n["g_ffn"]])
    a["consts"] = shape_constants(np)
    return a


def shape_constants(np):
    c = np.zeros((128, NCONST), np.float32)

    def put(name, v):
        lo, hi = CONST[name]
        c[:v.shape[0], lo:hi] = v

    put("ident", np.eye(128))
    t = np.arange(T)
    put("tri", (t[:, None] <= t[None, :]) * 1.0)
    put("headmask", (np.arange(128)[:, None] // DH0 == np.arange(8)[None, :]) * 1.0)
    put("keyidx", np.broadcast_to(np.arange(TC), (128, TC)))
    put("causal", (t[None, :] > t[:, None]) * MASKED)
    k = T // B
    put("batchmask", (t[None, :] // k != t[:, None] // k) * MASKED)
    put("tokcol", t[:, None])
    put("tokrow", np.broadcast_to(t, (128, T)))
    half = ROT // 2
    inv = np.float32(10000.0) ** (-np.arange(half, dtype=np.float32) / half)
    ang = t[:, None].astype(np.float32) * inv
    put("cos", np.concatenate([np.cos(ang), np.cos(ang)], 1))
    put("sin", np.concatenate([-np.sin(ang), np.sin(ang)], 1))
    put("iota8", np.broadcast_to(np.arange(NE), (128, NE)))
    put("ones", np.ones((128, 128)))
    return c


def kernel(**inputs):
    import numpy as np
    import concourse.bacc as bacc
    from concourse.bass_utils import run_bass_kernel_spmd

    nc = bacc.Bacc("TRN2", target_bir_lowering=False, num_devices=1)
    arrays, args = {}, {}
    for name, v in layout(inputs).items():
        v = np.ascontiguousarray(v)
        arrays["in_" + name] = v
        args[name] = nc.dram_tensor("in_" + name, v.shape, mybir.dt.from_np(v.dtype), kind="ExternalInput").ap()
    out = nc.dram_tensor("out", (B, T, D), F32, kind="ExternalOutput").ap()
    flamingo_kernel(nc, args, out)
    r = run_bass_kernel_spmd(nc, [arrays], core_ids=[0])
    return r.results[0]["out"]
```

```python
import concourse.bass as bass
from concourse import mybir
from contextlib import ExitStack

F32 = mybir.dt.float32
I32 = mybir.dt.int32
U32 = mybir.dt.uint32
ALU = mybir.AluOpType
ACT = mybir.ActivationFunctionType
AX_X = mybir.AxisListType.X

B, T, D = 8, 112, 256
TC = 375
DC = D // 128
PAIRS = B // 2
KT = 125
NKT = TC // KT
H0, DH0, PAD0 = 16, 16, 32
NE = 8
NH, HP = 8, 64
ROT = 32
KSEL = T // 8
CH = 16
NCH = -(-TC // (2 * CH))
TCP = NCH * 2 * CH
FRONT = TCP - TC
NPAIRS = B * NCH
PACK = 512
SEG = 8
POOL_ROWS = 6
RING = 4
LOWEST = -3.4028234663852886e38
MASKED = -1e30

CONST = {}
_at = 0
for _name, _n in (("ident", 128), ("tri", T), ("headmask", 8), ("keyidx", TC), ("causal", T), ("batchmask", T),
                  ("tokcol", 1), ("tokrow", T), ("cos", ROT), ("sin", ROT), ("iota8", NE), ("ones", 128)):
    CONST[_name] = (_at, _at + _n)
    _at += _n
NCONST = _at


class Attention:

    def __init__(self, sem, name, bufs, tiles, nh, keys, kt, scale):
        self.tiles, self.nh, self.keys, self.kt, self.scale = tiles, nh, keys, kt, scale
        self.nkt = keys // kt
        self.ident, self.score_ps, self.probsT_ps = bufs["ident"], bufs["score_ps"], bufs["probsT_ps"]
        self.score_sb, self.probsT_sb = bufs["score_sb"], bufs["probsT_sb"]
        self.max_sb, self.sum_sb, self.recip_sb = bufs["max_sb"], bufs["sum_sb"], bufs["recip_sb"]
        self.scores_full = sem(name + "_scores_full")
        self.scores_taken = [sem(f"{name}_scores_taken{s}") for s in range(2)]
        self.max_ready = sem(name + "_max_ready")
        self.shifted = sem(name + "_shifted")
        self.exp_ready = sem(name + "_exp_ready")
        self.sum_ready = sem(name + "_sum_ready")
        self.recip_ready = sem(name + "_recip_ready")
        self.probs_ready = sem(name + "_probs_ready")
        self.probsT_full = [sem(f"{name}_probsT_full{s}") for s in range(RING)]
        self.probsT_taken = [sem(f"{name}_probsT_taken{s}") for s in range(2)]
        self.values_done = [sem(f"{name}_values_done{s}") for s in range(2)]

    def tile(self, g):
        return self.score_sb[0:T, g % RING, 0:self.nh * self.keys]

    def heads(self, g):
        return self.tile(g).rearrange("p (h k) -> p h k", h=self.nh)

    def tensor(self, pe, i, scores, values, after):
        n = self.nh * self.nkt

        def do_scores(g):
            pe.wait_ge(self.scores_taken[g % 2], i * (self.tiles // 2) + g // 2)
            scores(g, self.score_ps[g % 2]).then_inc(self.scores_full, 1)

        def do_transposes(g):
            pe.wait_ge(self.probs_ready, i * self.tiles + g + 1)
            pe.wait_ge(self.probsT_taken[g % 2], i * (self.tiles // 2) + g // 2)
            for j in range(n):
                last = pe.transpose(self.probsT_ps[g % 2][0:self.kt, j * T:(j + 1) * T],
                                    self.tile(g)[:, j * self.kt:(j + 1) * self.kt], self.ident[0:T, 0:T])
            last.then_inc(self.probsT_full[g % RING], 1)

        for g in range(RING):
            do_scores(g)
        for g in range(self.tiles):
            do_transposes(g)
            if g + RING < self.tiles:
                do_scores(g + RING)
            pe.wait_ge(self.probsT_taken[g % 2], i * (self.tiles // 2) + g // 2 + 1)
            values(g, self.probsT_sb[g % 2]).then_inc(self.values_done[g % 2], 1)
            after(g)

    def vector(self, dve, i, mask, after):
        def first(g):
            dve.wait_ge(self.scores_full, i * self.tiles + g + 1)
            dve.wait_ge(self.probsT_full[g % RING], i * (self.tiles // RING) + g // RING)
            ps = self.score_ps[g % 2][0:T, 0:self.nh * self.keys].rearrange("p (h k) -> p h k", h=self.nh)
            dve.tensor_tensor(self.heads(g), ps, mask(g), ALU.add).then_inc(self.scores_taken[g % 2], 1)
            dve.wait_ge(self.scores_taken[g % 2], i * (self.tiles // 2) + g // 2 + 1)
            dve.tensor_reduce(self.max_sb[0:T, g % RING, 0:self.nh], self.heads(g), AX_X, ALU.max)\
               .then_inc(self.max_ready, 1)

        def second(g):
            dve.wait_ge(self.exp_ready, i * self.tiles + g + 1)
            dve.tensor_reduce(self.sum_sb[0:T, g % RING, 0:self.nh], self.heads(g), AX_X, ALU.add)\
               .then_inc(self.sum_ready, 1)
            dve.wait_ge(self.sum_ready, i * self.tiles + g + 1)
            dve.reciprocal(self.recip_sb[0:T, g % RING, 0:self.nh], self.sum_sb[0:T, g % RING, 0:self.nh])\
               .then_inc(self.recip_ready, 1)

        for g in range(RING):
            first(g)
        for g in range(self.tiles):
            second(g)
            if g + RING < self.tiles:
                first(g + RING)
            after(g)

    def gpsimd(self, pool, i, before, after):
        def shift(g):
            before(g)
            pool.wait_ge(self.max_ready, i * self.tiles + g + 1)
            m = self.max_sb[0:T, g % RING, 0:self.nh].unsqueeze(2).to_broadcast([T, self.nh, self.keys])
            pool.tensor_tensor(self.heads(g), self.heads(g), m, ALU.subtract).then_inc(self.shifted, 1)

        def divide(g):
            pool.wait_ge(self.recip_ready, i * self.tiles + g + 1)
            r = self.recip_sb[0:T, g % RING, 0:self.nh].unsqueeze(2).to_broadcast([T, self.nh, self.keys])
            pool.tensor_tensor(self.heads(g), self.heads(g), r, ALU.mult).then_inc(self.probs_ready, 1)

        for g in range(RING):
            shift(g)
        for g in range(self.tiles):
            divide(g)
            if g + RING < self.tiles:
                shift(g + RING)
            after(g)

    def scalar(self, act, i, after):
        def exp(g):
            act.wait_ge(self.shifted, i * self.tiles + g + 1)
            act.activation(self.tile(g), self.tile(g), ACT.Exp, scale=self.scale).then_inc(self.exp_ready, 1)

        def take(g):
            act.wait_ge(self.probsT_full[g % RING], i * (self.tiles // RING) + g // RING + 1)
            act.wait_ge(self.values_done[g % 2], i * (self.tiles // 2) + g // 2)
            cols = self.nh * self.nkt * T
            act.activation(self.probsT_sb[g % 2][0:self.kt, 0:cols], self.probsT_ps[g % 2][0:self.kt, 0:cols],
                           ACT.Copy).then_inc(self.probsT_taken[g % 2], 1)

        for g in range(RING):
            exp(g)
        for g in range(self.tiles):
            take(g)
            if g + RING < self.tiles:
                exp(g + RING)
            after(g)


class Chain:

    def __init__(self, eng, sem, i, per, scratch=None):
        self.eng, self.sem, self.base, self.per, self.n, self.scratch = eng, sem, i * per, per, 0, scratch

    def __call__(self, ins, carry=False):
        self.n += 1
        ins.then_inc(self.sem, 1)
        self.eng.wait_ge(self.sem, self.base + self.n)
        if carry:
            self.eng.memset(self.scratch, 0.0)

    def end(self):
        assert self.n == self.per, (self.n, self.per)


def flamingo_kernel(nc, a, out):
    ctx = ExitStack()
    with ctx:
        scope = [ctx]

        def sb(name, shape, dt=F32):
            return scope[-1].enter_context(nc.sbuf_tensor(name, shape, dt))

        def stage_buffers():
            scope.append(ExitStack())

        def end_stage_buffers():
            scope.pop().close()

        sems = {}

        def sem(name):
            if name not in sems:
                sems[name] = ctx.enter_context(nc.semaphore(name))
            return sems[name]

        X = sb("X", [T, B, D])
        XN = [sb(f"XN{u}", [T, D]) for u in range(2)]
        consts = sb("consts", [128, NCONST])
        gates = sb("gates", [T, 4])
        tanh_gates = sb("tanh_gates", [T, 4])
        XT = [sb(f"XT{u}", [128, DC, T]) for u in range(2)]
        CT = [sb(f"CT{u}", [128, DC, TC]) for u in range(2)]
        bn = sb("bn", [T, 2, 6])
        mv = sb("mv", [T, 2, 2])
        rstd = sb("rstd", [T, 2])
        scratch = sb("scratch", [T, 1])
        var_eps = sb("var_eps", [T, 2, 2])
        ps = [ctx.enter_context(nc.psum_tensor(f"bank{n}", [128, 512], F32)) for n in range(8)]

        def const(name, rows=128):
            lo, hi = CONST[name]
            return consts[0:rows, lo:hi]

        ident = const("ident")
        att_bufs = bufs = dict(
            ident=ident, score_ps=[ps[4], ps[5]], probsT_ps=[ps[6], ps[7]],
            score_sb=sb("score_sb", [T, RING, 4 * KT]), max_sb=sb("max_sb", [T, RING, 4]),
            sum_sb=sb("sum_sb", [T, RING, 4]), recip_sb=sb("recip_sb", [T, RING, 4]),
            probsT_sb=[sb(f"probsT_sb{s}", [128, 4 * T]) for s in range(2)])

        bqk0 = sb("bqk0", [128, 2, DC])
        bv0 = sb("bv0", [128, D])
        bo0 = sb("bo0", [1, D])
        bnd_i = sb("bnd_i", [T, B], I32)
        bnd_f = sb("bnd_f", [T, B])
        last_key = sb("last_key", [T, B])
        wide_col = sb("wide_col", [T, 1])
        wide_i = sb("wide_i", [1, 1], I32)

        wg0 = sb("wg0", [128, DC, NE])
        bg0 = sb("bg0", [1, NE])
        we0 = sb("we0", [128, DC, NE * D])
        be0 = sb("be0", [NE, D])
        logit = sb("logit", [T, NE])
        router = sb("router", [T, 8, NE])
        router_i = sb("router_i", [T, NE], U32)
        G = [sb(f"G{u}", [T, NE]) for u in range(2)]
        GT = [sb(f"GT{u}", [NE, T]) for u in range(2)]
        Y = sb("Y", [T, D])

        ws1 = sb("ws1", [128, DC, D])
        wf1 = sb("wf1", [128, DC, D])
        w1_col = sb("w1_col", [128, DC])
        w1_rep = sb("w1_rep", [128, DC, 32])
        wcwb_col = sb("wcwb_col", [128, 2, DC])
        wcwb_rep = sb("wcwb_rep", [128, 2, DC, T])
        bf1 = sb("bf1", [128, DC])
        bcwb = sb("bcwb", [T, 2])
        qmask_i = sb("qmask_i", [T, B, TC], I32)
        XNA = sb("XNA", [T, B, D])
        live = sb("live", [1, 4, B, NCH])
        span = sb("span", [1, 8, B])
        steps_of = sb("steps_of", [1, NPAIRS], I32)
        pairs_of = sb("pairs_of", [1, 2], I32)

        wqkv1 = sb("wqkv1", [128, DC, 3 * NH * HP])
        wo1 = sb("wo1", [128, 4, D])
        wr1 = sb("wr1", [128, DC, NH])
        wqkvm = sb("wqkvm", [128, DC, NH, 3 * HP])
        wom = sb("wom", [128, 4, D])
        zeros = sb("zeros", [T, 1])

        stage_buffers()
        wq0 = sb("wq0", [128, DC, D])
        wk0 = sb("wk0", [128, DC, D])
        wv0 = sb("wv0", [128, DC, D])
        wo0 = sb("wo0", [128, 4, D])
        beyond = sb("beyond", [T, 3, B])
        QT0 = [sb(f"QT0{u}", [128, DC, T]) for u in range(2)]
        KT0 = [sb(f"KT0{u}", [128, DC, TC]) for u in range(2)]
        KBD = [sb(f"KBD{u}", [128, H0 * KT]) for u in range(2)]
        V0 = [sb(f"V0{u}", [128, NKT, H0, PAD0]) for u in range(2)]
        MB = [sb(f"MB{u}", [T, TC]) for u in range(2)]
        O0 = sb("O0", [128, 4 * T])
        QBD = [sb(f"QBD{s}", [128, T]) for s in range(2)]
        end_stage_buffers()

        stage_buffers()
        FT = sb("FT", [128, DC, B * T])
        TT = sb("TT", [128, DC, B * TCP])
        H = [sb(f"H{v}", [128, DC, CH, T]) for v in range(2)]
        R = [sb(f"R{v}", [128, 4 * T]) for v in range(2)]
        RHO = sb("RHO", [T, B * TCP])
        weighed = [sb(f"weighed{u}", [T, 2, TC]) for u in range(2)]
        W = [sb(f"W{u}", [T, D]) for u in range(2)]
        soft = sb("soft", [T, 7, B])
        E = [sb(f"E{u}", [T, TC]) for u in range(2)]
        share = sb("share", [T, 2, 2])
        end_stage_buffers()

        stage_buffers()
        QK1 = [sb(f"QK1{u}", [T, 2, NH, HP]) for u in range(2)]
        RA = sb("RA", [T, 2, NH, ROT])
        RB = sb("RB", [T, 2, NH, ROT])
        V1 = [sb(f"V1{u}", [T, NH * HP]) for u in range(2)]
        QT1 = [sb(f"QT1{u}", [128, 4, T]) for u in range(2)]
        KBD1 = [sb(f"KBD1{u}", [128, 4, 2 * T]) for u in range(2)]
        O1 = sb("O1", [128, 4 * T])
        SC = sb("SC", [NH, B, T])
        top = sb("top", [NH, B, 16])
        top_i = sb("top_i", [NH, B, 16], U32)
        rest = sb("rest", [NH, B, T])
        IDX = sb("IDX", [NH, B, KSEL])
        VAL = sb("VAL", [NH, B, KSEL])
        BD = sb("BD", [NH, NH, T])
        POSC = sb("POSC", [T, NH])
        GATE = sb("GATE", [T, NH])
        POSB = sb("POSB", [T, NH, T])
        OH = sb("OH", [T, NH, B, KSEL])
        OHB = sb("OHB", [T, B, NH, KSEL])
        MM = sb("MM", [T, NH, T])
        XG = sb("XG", [128, DC, NH, B, KSEL])
        CS = sb("CS", [T, NH, 2 * ROT])
        POSN = sb("POSN", [T, B])
        Z = sb("Z", [T, NH, D])
        Z2 = sb("Z2", [T, B, D])
        OHR = [sb(f"OHR{u}", [T, T]) for u in range(2)]
        end_stage_buffers()

        consts_in = sem("consts_in")
        weights0_in = sem("weights0_in")
        weights_moe_in = sem("weights_moe_in")
        x_in = sem("x_in")
        small_in = sem("small_in")
        weights_c_in = sem("weights_c_in")
        weights_d_in = sem("weights_d_in")
        qmask_in = sem("qmask_in")
        ctx1_in = [sem(f"ctx1_in{u}") for u in range(2)]
        ctx0_in = [sem(f"ctx0_in{u}") for u in range(2)]
        stored = sem("stored")
        x_updated = sem("x_updated")
        bnd_ready = sem("bnd_ready")
        last_key_full = sem("last_key_full")
        wide_ready = sem("wide_ready")
        wide_full = sem("wide_full")
        wide_set = sem("wide_set")
        tanh_ready = sem("tanh_ready")
        zeroed = sem("zeroed")
        dve_step = sem("dve_step")
        stats_ready = sem("stats_ready")
        rstd_ready = sem("rstd_ready")
        xn_ready = sem("xn_ready")
        ln_step = sem("ln_step")

        steps = {"n": 0}

        def link(dve, ins):
            steps["n"] += 1
            ins.then_inc(dve_step, 1)
            dve.wait_ge(dve_step, steps["n"])

        def layer_norm(dve, pair, n, taken):
            for u in range(2):
                dve.bn_stats(bn[:, u, :], X[:, bass.ds(2 * pair + u, 1), :]).then_inc(ln_step, 1)
            dve.wait_ge(ln_step, n * 4 + 2)
            dve.memset(scratch[:, :], 0.0)
            for u in range(2):
                dve.bn_aggr(mv[:, u, :], bn[:, u, :]).then_inc(ln_step, 1)
            dve.wait_ge(ln_step, n * 4 + 4)
            dve.tensor_scalar(var_eps[:, 0, :], mv[:, :, 1], 1e-5, None, ALU.add).then_inc(stats_ready, 1)
            dve.wait_ge(rstd_ready, n + 1)
            taken()
            for u in range(2):
                dve.tensor_scalar(XN[u][:, :], X[:, bass.ds(2 * pair + u, 1), :].rearrange("p o d -> p (o d)"),
                                  mv[:, u, 0:1], rstd[:, u:u + 1], ALU.subtract, ALU.mult).then_inc(xn_ready, 1)

        def layer_norm_root(pool, n):
            pool.wait_ge(stats_ready, n + 1)
            pool.tensor_tensor(rstd[:, :], var_eps[:, 0, :], var_eps[:, 1, :], ALU.pow).then_inc(rstd_ready, 1)

        def transpose_xn(pe, b, n, u, bank, full):
            pe.wait_ge(xn_ready, n + 1)
            for c in range(DC):
                last = pe.transpose(bank[:, c * T:(c + 1) * T], XN[u][:, c * 128:(c + 1) * 128], ident[0:T, 0:T])
            last.then_inc(full, 1)

        def cross0(nkt):
            nm = "x"
            keys = nkt * KT
            nh = 4 if nkt == 1 else 1
            tiles = 2 * H0 // nh
            per = tiles // 2
            att = Attention(sem, nm, att_bufs, tiles, nh, keys, KT, DH0 ** -0.5)
            kturns = 1 if nkt == 1 else DC
            AT, BT = 1 + kturns, 1 + nkt
            a_full, a_taken = sem(nm + "_a_full"), sem(nm + "_a_taken")
            b_full, b_taken = sem(nm + "_b_full"), sem(nm + "_b_taken")
            o_full, o_taken = sem(nm + "_o_full"), sem(nm + "_o_taken")
            y_full, y_taken = sem(nm + "_y_full"), x_updated
            kbd_ready = sem(nm + "_kbd_ready")
            qbd_ready = sem(nm + "_qbd_ready")
            mask_ready = sem(nm + "_mask_ready")

            def sync(sp):
                for u in range(2):
                    sp.dma_start(CT[u][:, :, :], a["ctxT"][:, :, u * TC:(u + 1) * TC]).then_inc(ctx0_in[u], 16)
                with sp.Fori(1, PAIRS) as i:
                    for u in range(2):
                        sp.wait_ge(b_full, (i - 1) * (2 * BT) + (u + 1) * BT)
                        sp.dma_start(CT[u][:, :, :], a["ctxT"][:, :, bass.ds((2 * i + u) * TC, TC)])\
                          .then_inc(ctx0_in[u], 16)

            def tensor(pe):
                with pe.Fori(0, PAIRS) as i:
                    for u in range(2):
                        b = 2 * i + u
                        at, bt = i * (2 * AT) + u * AT, i * (2 * BT) + u * BT
                        pe.wait_ge(a_taken, at)
                        transpose_xn(pe, b, b, u, ps[0], a_full)
                        pe.wait_ge(a_taken, at + 1)
                        pe.wait_ge(b_taken, bt)
                        for e in range(DC):
                            for c in range(DC):
                                last = pe.matmul(ps[1][:, e * T:(e + 1) * T], wq0[:, c, e * 128:(e + 1) * 128],
                                                 XT[u][:, c, :], start=(c == 0), stop=(c == DC - 1))
                        last.then_inc(b_full, 1)
                        pe.wait_ge(ctx0_in[u], 16 * (i + 1))
                        for k in range(kturns):
                            pe.wait_ge(a_taken, at + 1 + k)
                            es = range(DC) if nkt == 1 else [k]
                            for j, e in enumerate(es):
                                for c in range(DC):
                                    last = pe.matmul(ps[0][:, j * keys:(j + 1) * keys],
                                                     wk0[:, c, e * 128:(e + 1) * 128], CT[u][:, c, 0:keys],
                                                     start=(c == 0), stop=(c == DC - 1))
                            last.then_inc(a_full, 1)
                        for k in range(nkt):
                            pe.wait_ge(b_taken, bt + 1 + k)
                            for c in range(DC):
                                last = pe.matmul(ps[1][0:KT, 0:D], CT[u][:, c, k * KT:(k + 1) * KT], wv0[:, c, :],
                                                 start=(c == 0), stop=(c == DC - 1))
                            last.then_inc(b_full, 1)

                    def scores(g, bank):
                        u, j = g // per, g % per
                        head = j * nh
                        e, k = head // 8, head % 8
                        if j == 0:
                            pe.wait_ge(b_taken, i * (2 * BT) + u * BT + 1)
                            if nkt == 1:
                                pe.wait_ge(kbd_ready, 2 * i + u + 1)
                            else:
                                pe.wait_ge(a_taken, i * (2 * AT) + (u + 1) * AT)
                        if nkt == 1:
                            return pe.matmul(bank[0:T, 0:nh * keys], QT0[u][:, e, :],
                                             KBD[u][:, head * KT:(head + nh) * KT], start=True, stop=True)
                        pe.wait_ge(qbd_ready, i * tiles + g + 1)
                        return pe.matmul(bank[0:T, 0:keys], QBD[g % 2][:, :], KT0[u][:, e, :],
                                         start=True, stop=True)

                    def values(g, probsT):
                        u, j = g // per, g % per
                        if j == 0:
                            pe.wait_ge(b_taken, i * (2 * BT) + (u + 1) * BT)
                            pe.wait_ge(o_taken, 2 * i + u)
                        for h in range(nh):
                            head = j * nh + h
                            r, q = PAD0 * (head % 4), head // 4
                            for k in range(nkt):
                                last = pe.matmul(ps[2][r:r + PAD0, q * T:(q + 1) * T], V0[u][0:KT, k, head, :],
                                                 probsT[0:KT, (h * nkt + k) * T:(h * nkt + k + 1) * T],
                                                 start=(k == 0), stop=(k == nkt - 1))
                        return last

                    def after(g):
                        u, j = g // per, g % per
                        if j == per - 1:
                            b = 2 * i + u
                            pe.wait_ge(o_taken, b + 1)
                            pe.wait_ge(y_taken, b)
                            for q in range(4):
                                pe.matmul(ps[3][0:T, 0:D], O0[:, q * T:(q + 1) * T], wo0[:, q, :],
                                          start=(q == 0), stop=False)
                            pe.matmul(ps[3][0:T, 0:D], const("ones")[0:1, 0:T], bo0[:, :], start=False, stop=True)\
                              .then_inc(y_full, 1)

                    att.tensor(pe, i, scores, values, after)

            def scalar(act):
                with act.Fori(0, PAIRS) as i:
                    for u in range(2):
                        at = i * (2 * AT) + u * AT
                        act.wait_ge(a_full, at + 1)
                        act.activation(XT[u][:, :, :].rearrange("p c t -> p (c t)"), ps[0][:, 0:DC * T], ACT.Copy)\
                           .then_inc(a_taken, 1)
                        for k in range(kturns):
                            act.wait_ge(a_full, at + 2 + k)
                            es = range(DC) if nkt == 1 else [k]
                            for j, e in enumerate(es):
                                last = act.activation(KT0[u][:, e, 0:keys], ps[0][:, j * keys:(j + 1) * keys],
                                                      ACT.Identity, bias=bqk0[:, 1, e:e + 1])
                            last.then_inc(a_taken, 1)

                    def after(g):
                        if g % per == per - 1:
                            b = 2 * i + g // per
                            act.wait_ge(att.values_done[g % 2], i * (tiles // 2) + g // 2 + 1)
                            act.wait_ge(y_full, b)
                            act.activation(O0[:, :], ps[2][:, 0:4 * T], ACT.Copy).then_inc(o_taken, 1)

                    att.scalar(act, i, after)

            def vector(dve):
                with dve.Fori(0, PAIRS) as i:
                    for u in range(2):
                        b = 2 * i + u
                        bt = i * (2 * BT) + u * BT
                        dve.tensor_scalar(MB[u][:, 0:keys], const("keyidx", T)[:, 0:keys],
                                          last_key[:, bass.ds(b, 1)], LOWEST, ALU.is_gt, ALU.mult)\
                           .then_inc(mask_ready, 1)
                        dve.wait_ge(b_full, bt + 1)
                        for e in range(DC):
                            last = dve.tensor_scalar(QT0[u][:, e, :], ps[1][:, e * T:(e + 1) * T],
                                                     bqk0[:, 0, e:e + 1], None, ALU.add)
                        last.then_inc(b_taken, 1)
                        for k in range(nkt):
                            dve.wait_ge(b_full, bt + 2 + k)
                            dve.tensor_tensor(V0[u][0:KT, k, :, 0:DH0],
                                              ps[1][0:KT, 0:D].rearrange("p (h d) -> p h d", h=H0),
                                              bv0[0:KT, :].rearrange("p (h d) -> p h d", h=H0), ALU.add)\
                               .then_inc(b_taken, 1)

                    def mask(g):
                        if g % per == 0:
                            dve.wait_ge(mask_ready, 2 * i + g // per + 1)
                        return MB[g // per][:, 0:keys].unsqueeze(1).to_broadcast([T, nh, keys])

                    def after(g):
                        if g % per == per - 1:
                            b = 2 * i + g // per
                            dve.wait_ge(y_full, b + 1)
                            xb = X[:, bass.ds(b, 1), :].rearrange("p o d -> p (o d)")
                            dve.scalar_tensor_tensor(xb, ps[3][0:T, 0:D], tanh_gates[:, 0:1], xb,
                                                     ALU.mult, ALU.add).then_inc(y_taken, 1)
                        if g == per - 1:
                            layer_norm(dve, (i + 1) & (PAIRS - 1), i + 1,
                                       lambda: dve.wait_ge(a_full, i * (2 * AT) + AT + 1))

                    att.vector(dve, i, mask, after)

            def gpsimd(pool):
                with pool.Fori(0, PAIRS) as i:
                    for u in range(2):
                        pool.wait_ge(a_taken, i * (2 * AT) + (u + 1) * AT)
                        if nkt > 1:
                            continue
                        for e in range(DC):
                            k = KT0[u][:, e, 0:KT].unsqueeze(1).to_broadcast([128, 8, KT])
                            m = const("headmask").unsqueeze(2).to_broadcast([128, 8, KT])
                            last = pool.tensor_tensor(
                                KBD[u][:, e * 8 * KT:(e + 1) * 8 * KT].rearrange("p (h k) -> p h k", h=8), k, m, ALU.mult)
                        last.then_inc(kbd_ready, 1)

                    def before(g):
                        if nkt == 1:
                            return
                        u, head = g // per, g % per
                        if head == 0:
                            pool.wait_ge(b_taken, i * (2 * BT) + u * BT + 1)
                        pool.wait_ge(att.scores_taken[g % 2], i * (tiles // 2) + g // 2)
                        pool.tensor_tensor(QBD[g % 2][:, :], QT0[u][:, head // 8, :],
                                           const("headmask")[:, head % 8:head % 8 + 1].to_broadcast([128, T]), ALU.mult)\
                            .then_inc(qbd_ready, 1)

                    def after(g):
                        if g == per - 1:
                            layer_norm_root(pool, i + 1)

                    att.gpsimd(pool, i, before, after)

            return sync, tensor, scalar, vector, gpsimd

        m_a_full, m_a_taken = sem("m_a_full"), sem("m_a_taken")
        m_logit_full, m_logit_taken = sem("m_logit_full"), sem("m_logit_taken")
        m_neg_max, m_exp = sem("m_neg_max"), sem("m_exp")
        m_gates = sem("m_gates")
        m_gt_full, m_gt_taken = sem("m_gt_full"), sem("m_gt_taken")
        m_bias_full = sem("m_bias_full")
        m_expert_full = sem("m_expert_full")
        m_expert_taken = [sem(f"m_expert_taken{q}") for q in range(4)]
        m_step = sem("m_step")

        def experts_tensor(pe):
            pe.wait_ge(weights_moe_in, 16 * 4)
            with pe.Fori(0, PAIRS) as i:
                for u in range(2):
                    b = 2 * i + u
                    pe.wait_ge(m_a_taken, b)
                    transpose_xn(pe, b, 2 * PAIRS + b, u, ps[0], m_a_full)
                    pe.wait_ge(m_a_taken, b + 1)
                    pe.wait_ge(m_logit_taken, b)
                    for c in range(DC):
                        pe.matmul(ps[1][0:T, 0:NE], XT[u][:, c, :], wg0[:, c, :], start=(c == 0), stop=False)
                    pe.matmul(ps[1][0:T, 0:NE], const("ones")[0:1, 0:T], bg0[:, :], start=False, stop=True)\
                      .then_inc(m_logit_full, 1)
                for u in range(2):
                    b = 2 * i + u
                    for q in range(4):
                        pe.wait_ge(m_expert_taken[q], b)
                        for c in range(DC):
                            last = pe.matmul(ps[2 + q][0:T, :], XT[u][:, c, :], we0[:, c, q * 512:(q + 1) * 512],
                                             start=(c == 0), stop=(c == DC - 1))
                        last.then_inc(m_expert_full, 1)
                        if q == 0:
                            pe.wait_ge(m_gates, b + 1)
                            pe.wait_ge(m_gt_taken, b)
                            pe.transpose(ps[6][0:NE, 0:T], G[u][:, :], ident[0:T, 0:T]).then_inc(m_gt_full, 1)
                    pe.wait_ge(m_gt_taken, b + 1)
                    pe.wait_ge(x_updated, B + b)
                    pe.matmul(ps[7][0:T, 0:D], GT[u][:, :], be0[:, :], start=True, stop=True).then_inc(m_bias_full, 1)

        def experts_scalar(act):
            with act.Fori(0, PAIRS) as i:
                for u in range(2):
                    b = 2 * i + u
                    act.wait_ge(m_a_full, b + 1)
                    act.activation(XT[u][:, :, :].rearrange("p c t -> p (c t)"), ps[0][:, 0:DC * T], ACT.Copy)\
                       .then_inc(m_a_taken, 1)
                    act.wait_ge(m_neg_max, b + 1)
                    act.activation(router[:, 1, :], logit[:, :], ACT.Exp, bias=router[:, 0, 0:1],
                                   accum_out=router[:, 0, 1:2]).then_inc(m_exp, 1)
                for u in range(2):
                    b = 2 * i + u
                    act.wait_ge(m_gt_full, b + 1)
                    act.activation(GT[u][:, :], ps[6][0:NE, 0:T], ACT.Copy).then_inc(m_gt_taken, 1)

        def experts_vector(dve):
            dve.wait_ge(consts_in, 16)
            with dve.Fori(0, PAIRS) as i:
                chain = Chain(dve, m_step, i, 2 * 7 + 2 * 5, scratch[:, :])
                for u in range(2):
                    b = 2 * i + u
                    dve.wait_ge(m_logit_full, b + 1)
                    dve.tensor_copy(logit[:, :], ps[1][0:T, 0:NE]).then_inc(m_logit_taken, 1)
                    dve.wait_ge(m_logit_taken, b + 1)
                    dve.tensor_reduce(router[:, 0, 0:1], logit[:, :], AX_X, ALU.max, negate=True).then_inc(m_neg_max, 1)
                    dve.wait_ge(m_exp, b + 1)
                    chain(dve.reciprocal(router[:, 0, 2:3], router[:, 0, 1:2]))
                    chain(dve.tensor_scalar(router[:, 2, :], router[:, 1, :], router[:, 0, 2:3], None, ALU.mult), carry=True)
                    chain(dve.max(router[:, 3, :], router[:, 2, :]), carry=True)
                    chain(dve.max_index(router_i[:, :], router[:, 3, :], router[:, 2, :]))
                    chain(dve.tensor_copy(router[:, 4, :], router_i[:, :]))
                    for j in range(2):
                        chain(dve.tensor_scalar(router[:, 5 + j, :], const("iota8", T), router[:, 4, j:j + 1],
                                                router[:, 3, j:j + 1], ALU.is_equal, ALU.mult))
                    dve.tensor_tensor(G[u][:, :], router[:, 5, :], router[:, 6, :], ALU.add).then_inc(m_gates, 1)
                    dve.wait_ge(m_gates, b + 1)
                layer_norm(dve, (i + 1) & (PAIRS - 1), PAIRS + i + 1, lambda: dve.wait_ge(m_a_full, 2 * i + 2))
                for u in range(2):
                    b = 2 * i + u
                    for e in range(NE):
                        p = ps[2 + e // 2][0:T, (e % 2) * D:(e % 2 + 1) * D]
                        if e % 2 == 0:
                            dve.wait_ge(m_expert_full, 4 * b + e // 2 + 1)
                        if e == 0:
                            ins = dve.tensor_scalar(Y[:, :], p, G[u][:, e:e + 1], None, ALU.mult)
                        else:
                            ins = dve.scalar_tensor_tensor(Y[:, :], p, G[u][:, e:e + 1], Y[:, :], ALU.mult, ALU.add)
                        if e % 2 == 1:
                            ins.then_inc(m_expert_taken[e // 2], 1)
                            dve.wait_ge(m_expert_taken[e // 2], b + 1)
                        else:
                            chain(ins)
                    dve.wait_ge(m_bias_full, b + 1)
                    chain(dve.tensor_tensor(Y[:, :], Y[:, :], ps[7][0:T, 0:D], ALU.add))
                    xb = X[:, bass.ds(b, 1), :].rearrange("p o d -> p (o d)")
                    dve.scalar_tensor_tensor(xb, Y[:, :], tanh_gates[:, 2:3], xb, ALU.mult, ALU.add)\
                       .then_inc(x_updated, 1)
                    dve.wait_ge(x_updated, B + b + 1)
                chain.end()

        def experts_gpsimd(pool):
            with pool.Fori(0, PAIRS) as i:
                layer_norm_root(pool, PAIRS + i + 1)

        c_ctx_used = sem("c_ctx_used")
        c_a_full, c_a_taken = sem("c_a_full"), sem("c_a_taken")
        c_f_full, c_f_taken = sem("c_f_full"), sem("c_f_taken")
        c_t_full = sem("c_t_full")
        c_t_taken = [sem(f"c_t_taken{e}") for e in range(DC)]
        c_kept = sem("c_kept")
        c_padded = sem("c_padded")
        c_penalty = sem("c_penalty")
        c_added_v, c_added_p = sem("c_added_v"), sem("c_added_p")
        c_tanh = sem("c_tanh")
        c_dotted = sem("c_dotted")
        c_r_taken = sem("c_r_taken")
        c_rT_full = sem("c_rT_full")
        c_rho = sem("c_rho")
        c_neg_max, c_exp, c_shares, c_ws = sem("c_neg_max"), sem("c_exp"), sem("c_shares"), sem("c_ws")
        c_wb_taken = [sem(f"c_wb_taken{u}") for u in range(2)]
        c_step = sem("c_step")
        c_y = sem("c_y")
        c_shared = sem("c_shared")
        reps_ready = sem("reps_ready")
        steps_set = sem("steps_set")

        def prepare_steps(dve):
            dve.wait_ge(qmask_in, 16)
            free = bufs["score_sb"][0:1, :, :].rearrange("p r k -> p (r k)")
            padded = free[:, 0:DC * TCP].rearrange("p (b k) -> p b k", b=DC)
            index = const("keyidx", 1)
            key = index[:, 0:NCH]
            row = lambda ap: ap.unsqueeze(1).to_broadcast([1, B, NCH])
            link(dve, dve.memset(padded, 0.0))
            for part in range(B // DC):
                link(dve, dve.tensor_copy(padded[:, :, FRONT:TCP], qmask_i[0:1, DC * part:DC * (part + 1), :]))
                link(dve, dve.tensor_reduce(live[:, 0, DC * part:DC * (part + 1), :],
                                            padded.rearrange("p b (c k) -> p b c k", k=2 * CH), AX_X, ALU.max,
                                            apply_absolute_value=True))
            link(dve, dve.tensor_scalar(live[:, 1, :, :], live[:, 0, :, :], 0.0, None, ALU.is_gt))
            link(dve, dve.tensor_scalar(live[:, 2, 0, :], key, -1.0, float(NCH), ALU.mult, ALU.add))
            link(dve, dve.tensor_scalar(live[:, 2, 1, :], key, 1.0, None, ALU.add))
            link(dve, dve.tensor_tensor(live[:, 3, :, :], live[:, 1, :, :], row(live[:, 2, 0, :]), ALU.mult))
            link(dve, dve.tensor_reduce(span[:, 0, :], live[:, 3, :, :], AX_X, ALU.max))
            link(dve, dve.tensor_tensor(live[:, 3, :, :], live[:, 1, :, :], row(live[:, 2, 1, :]), ALU.mult))
            link(dve, dve.tensor_reduce(span[:, 1, :], live[:, 3, :, :], AX_X, ALU.max))
            link(dve, dve.tensor_scalar(span[:, 2, :], span[:, 0, :], -1.0, float(NCH), ALU.mult, ALU.add))
            link(dve, dve.tensor_tensor(span[:, 3, :], span[:, 1, :], span[:, 2, :], ALU.subtract))
            link(dve, dve.tensor_scalar(span[:, 3, :], span[:, 3, :], 0.0, None, ALU.max))
            link(dve, dve.tensor_tensor_scan(span[:, 5, :], const("ones", 1)[:, 0:B], span[:, 3, :], 0.0,
                                             ALU.mult, ALU.add))
            link(dve, dve.tensor_tensor(span[:, 4, :], span[:, 5, :], span[:, 3, :], ALU.subtract))
            link(dve, dve.tensor_tensor(span[:, 0, :], span[:, 2, :], span[:, 4, :], ALU.subtract))
            link(dve, dve.tensor_scalar(span[:, 0, :], span[:, 0, :], 2.0 * CH, None, ALU.mult))
            link(dve, dve.tensor_scalar(span[:, 1, :], index[:, 0:B], float(PACK), None, ALU.mult))
            link(dve, dve.tensor_tensor(span[:, 6, :], span[:, 0, :], span[:, 1, :], ALU.add))
            link(dve, dve.tensor_copy(span[:, 7, 0:1], span[:, 6, 0:1]))
            link(dve, dve.tensor_tensor(span[:, 7, 1:B], span[:, 6, 1:B], span[:, 6, 0:B - 1], ALU.subtract))
            started = free[:, 0:B * NPAIRS].rearrange("p (b s) -> p b s", b=B)
            link(dve, dve.tensor_tensor(started, index[:, 0:NPAIRS].unsqueeze(1).to_broadcast([1, B, NPAIRS]),
                                        span[:, 4, :].unsqueeze(2).to_broadcast([1, B, NPAIRS]), ALU.is_ge))
            total = free[:, B * NPAIRS:(B + 1) * NPAIRS]
            link(dve, dve.tensor_tensor(started, started, span[:, 7, :].unsqueeze(2).to_broadcast([1, B, NPAIRS]),
                                        ALU.mult))
            link(dve, dve.tensor_reduce(total, started.rearrange("p b s -> p s b"), AX_X, ALU.add))
            link(dve, dve.scalar_tensor_tensor(steps_of[:, :], index[:, 0:NPAIRS], 2.0 * CH, total,
                                               ALU.mult, ALU.add))
            link(dve, dve.tensor_copy(pairs_of[:, 0:1], span[:, 5, B - 1:B]))
            dve.tensor_scalar(pairs_of[:, 1:2], span[:, 5, B - 1:B], -1.0, 0.0, ALU.add, ALU.max).then_inc(steps_set, 1)
            dve.wait_ge(steps_set, 1)
            dve.wait_ge(weights_c_in, 16 * 6)
            for e in range(DC):
                link(dve, dve.tensor_copy(w1_rep[:, e, :], w1_col[:, e:e + 1].to_broadcast([128, 32])))
                for k in range(2):
                    ins = dve.tensor_copy(wcwb_rep[:, k, e, :], wcwb_col[:, k, e:e + 1].to_broadcast([128, T]))
                    if (e, k) != (1, 1):
                        link(dve, ins)
            ins.then_inc(reps_ready, 1)

        def steps_loop(eng, pair, last=None):
            pairs = eng.value_load(pairs_of[0:1, 0:1], min_val=0, max_val=NPAIRS)
            with eng.If(pairs > 0):
                pair(0, True)
            with eng.Fori(0, NPAIRS // SEG) as g:
                with eng.If(pairs > g * SEG + 1):
                    with eng.Fori(0, SEG) as k:
                        with eng.If(pairs > g * SEG + k + 1):
                            pair((g * SEG + k + 1).with_bounds(min_val=1, max_val=NPAIRS - 1), False)
            if last is not None:
                final = eng.value_load(pairs_of[0:1, 1:2], min_val=0, max_val=NPAIRS - 1)
                with eng.If(pairs > 0):
                    last(final + 1)

        def pair_at(eng, j):
            entry = eng.value_load(steps_of[0:1, bass.ds(j, 1)], min_val=0, max_val=B * PACK - 1)
            batch = entry >> PACK.bit_length() - 1
            row = entry & (PACK - 1)
            return ((row + batch * TCP).with_bounds(min_val=0, max_val=B * TCP - 2 * CH),
                    (batch * T).with_bounds(min_val=0, max_val=(B - 1) * T))

        def additive_sync(sp):
            sp.wait_ge(x_updated, B)
            for u in range(2):
                sp.dma_start(CT[u][:, :, :], a["ctxT"][:, :, u * TC:(u + 1) * TC]).then_inc(ctx1_in[u], 16)
            with sp.Fori(1, PAIRS) as i:
                for u in range(2):
                    sp.wait_ge(c_t_full, 4 * (i - 1) + 2 * u + 2)
                    sp.dma_start(CT[u][:, :, :], a["ctxT"][:, :, bass.ds((2 * i + u) * TC, TC)]).then_inc(ctx1_in[u], 16)
            for u in range(2):
                sp.wait_ge(c_t_full, 4 * (PAIRS - 1) + 2 * u + 2)
                sp.dma_start(CT[u][:, :, :], a["ctxT"][:, :, u * TC:(u + 1) * TC]).then_inc(ctx1_in[u], 16)
            with sp.Fori(1, PAIRS) as i:
                for u in range(2):
                    sp.wait_ge(c_ctx_used, 2 * (i - 1) + u + 1)
                    sp.dma_start(CT[u][:, :, :], a["ctxT"][:, :, bass.ds((2 * i + u) * TC, TC)]).then_inc(ctx1_in[u], 16)

        def additive_tensor(pe):
            pe.wait_ge(weights_c_in, 16 * 6)
            for q in range(4):
                pe.wait_ge(m_expert_taken[q], B)
            with pe.Fori(0, PAIRS) as i:
                for u in range(2):
                    b = 2 * i + u
                    pe.wait_ge(c_a_taken, b)
                    transpose_xn(pe, b, 4 * PAIRS + b, u, ps[0], c_a_full)
                    pe.wait_ge(ctx1_in[u], 16 * (i + 1))
                    for e in range(DC):
                        pe.wait_ge(c_t_taken[e], b)
                        for c in range(DC):
                            last = pe.matmul(ps[2 + e][:, 0:TC], ws1[:, c, e * 128:(e + 1) * 128], CT[u][:, c, :],
                                             start=(c == 0), stop=(c == DC - 1))
                        last.then_inc(c_t_full, 1)
                    pe.wait_ge(c_a_taken, b + 1)
                    pe.wait_ge(c_f_taken, b)
                    for e in range(DC):
                        for c in range(DC):
                            last = pe.matmul(ps[1][:, e * T:(e + 1) * T], wf1[:, c, e * 128:(e + 1) * 128],
                                             XT[u][:, c, :], start=(c == 0), stop=(c == DC - 1))
                    last.then_inc(c_f_full, 1)
            pe.wait_ge(reps_ready, 1)
            pe.wait_ge(steps_set, 1)

            def back(j, v):
                pe.wait_ge(c_r_taken, 2 * j + v - 1)
                pe.wait_ge(c_rho, 2 * j + v - 1)
                for k in range(4):
                    last = pe.transpose(ps[6 + v][0:T, k * 128:(k + 1) * 128], R[v][:, k * T:(k + 1) * T], ident)
                last.then_inc(c_rT_full, 1)

            def pair(j, first):
                for v in range(2):
                    for e in range(DC):
                        if not first and v == 0:
                            back(j, e)
                        pe.wait_ge(c_tanh, 4 * j + 2 * v + e + 1)
                        for q in range(4):
                            last = pe.matmul(ps[4 + v][32 * q:32 * q + 32, 0:4 * T], w1_rep[:, e, :],
                                             H[v][:, e, 4 * q:4 * q + 4, :].rearrange("p k t -> p (k t)"),
                                             start=(e == 0), stop=(e == DC - 1))
                        last.then_inc(c_dotted, 1)

            steps_loop(pe, pair, lambda pairs: (back(pairs, 0), back(pairs, 1)))
            pe.wait_ge(c_f_taken, B)
            for e in range(DC):
                pe.wait_ge(c_t_taken[e], B)
            with pe.Fori(0, PAIRS) as i:
                for u in range(2):
                    pe.wait_ge(ctx1_in[u], 16 * (PAIRS + 1 + i))
                    pe.wait_ge(c_wb_taken[u], i)
                    for k in range(2):
                        for c in range(DC):
                            last = pe.matmul(ps[2 * u + k][0:T, 0:TC], wcwb_rep[:, k, c, :], CT[u][:, c, :],
                                             start=(c == 0), stop=(c == DC - 1))
                    last.then_inc(c_ctx_used, 1)

        def additive_scalar(act):
            act.wait_ge(c_padded, 3)
            act.wait_ge(steps_set, 1)
            with act.Fori(0, PAIRS) as i:
                for u in range(2):
                    b = 2 * i + u
                    act.wait_ge(c_a_full, b + 1)
                    act.activation(XT[u][:, :, :].rearrange("p c t -> p (c t)"), ps[0][:, 0:DC * T], ACT.Copy)\
                       .then_inc(c_a_taken, 1)
                    for e in range(DC):
                        act.wait_ge(c_t_full, 2 * b + 1 + e)
                        act.activation(TT[:, e, bass.ds(b * TCP + FRONT, TC)], ps[2 + e][:, 0:TC], ACT.Copy)\
                           .then_inc(c_t_taken[e], 1)

            def take(j, v):
                act.wait_ge(c_dotted, 4 * j + 2 * v - 2)
                act.activation(R[v][:, :], ps[4 + v][:, 0:4 * T], ACT.Copy).then_inc(c_r_taken, 1)

            def pair(j, first):
                for v in range(2):
                    for e in range(DC):
                        if not first and v == 0:
                            take(j, e)
                        act.wait_ge(c_added_v, 4 * j + 2 * v + e + 1)
                        act.wait_ge(c_added_p, 4 * j + 2 * v + e + 1)
                        h = H[v][:, e, :, :].rearrange("p k t -> p (k t)")
                        act.activation(h, h, ACT.Tanh).then_inc(c_tanh, 1)

            steps_loop(act, pair, lambda pairs: (take(pairs, 0), take(pairs, 1)))
            act.wait_ge(c_neg_max, 1)
            with act.Fori(0, PAIRS) as i:
                for u in range(2):
                    b = 2 * i + u
                    act.wait_ge(c_wb_taken[u], i)
                    act.activation(E[u][:, :], RHO[:, bass.ds(b * TCP + FRONT, TC)], ACT.Exp, bias=soft[:, 0, bass.ds(b, 1)],
                                   accum_out=soft[:, 1, bass.ds(b, 1)]).then_inc(c_exp, 1)
            act.wait_ge(c_shares, 1)
            for k in range(2):
                act.activation(soft[:, 5 + k, :], soft[:, 3 + k, :], ACT.Tanh, bias=bcwb[:, k:k + 1]).then_inc(c_ws, 1)

        def add_halves(eng, j, first, lo, n, done):
            at, features = pair_at(eng, j)
            for v in range(2):
                for e in range(DC):
                    if not first:
                        eng.wait_ge(c_dotted, 4 * j + 2 * v + e - 3)
                    t = TT[:, e, bass.ds(at + v * CH + lo, n)].unsqueeze(2).to_broadcast([128, n, T])
                    f = FT[:, e, bass.ds(features, T)].unsqueeze(1).to_broadcast([128, n, T])
                    eng.tensor_tensor(H[v][:, e, lo:lo + n, :], t, f, ALU.add).then_inc(done, 1)

        def additive_vector(dve):
            dve.wait_ge(c_padded, 3)

            def project(i, end):
                for u in range(2):
                    b = 2 * i + u
                    dve.tensor_scalar(RHO[:, bass.ds(b * TCP + FRONT, TC)],
                                      qmask_i[:, bass.ds(b, 1), :].rearrange("p o k -> p (o k)"),
                                      -MASKED, MASKED, ALU.mult, ALU.add).then_inc(c_penalty, 1)
                    dve.wait_ge(c_f_full, b + 1)
                    for e in range(DC):
                        last = dve.tensor_scalar(FT[:, e, bass.ds(b * T, T)], ps[1][:, e * T:(e + 1) * T], bf1[:, e:e + 1],
                                                 None, ALU.add)
                    last.then_inc(c_f_taken, 1)
                if not end:
                    layer_norm(dve, i + 1, 2 * PAIRS + i + 1,
                               lambda: (dve.wait_ge(c_a_full, 2 * i + 2), dve.wait_ge(c_kept, 2 * i + 2)))

            with dve.Fori(0, PAIRS - 1) as i:
                project(i, False)
            project(PAIRS - 1, True)
            dve.wait_ge(c_f_taken, B)
            dve.wait_ge(c_penalty, B)
            for e in range(DC):
                dve.wait_ge(c_t_taken[e], B)

            dve.memset(scratch[:, :], 0.0).then_inc(c_rho, 2)

            def keep(j):
                at, _ = pair_at(dve, j - 1)
                for v in range(2):
                    r = RHO[:, bass.ds(at + v * CH, CH)].rearrange("p (q k) -> p k q", q=4)
                    dve.wait_ge(c_rT_full, 2 * j + v - 1)
                    dve.tensor_tensor(r, ps[6 + v][0:T, :].rearrange("p (k q r) -> p k q r", k=4, q=4)[:, :, :, 0],
                                      r, ALU.add).then_inc(c_rho, 1)

            def pair(j, first):
                add_halves(dve, j, first, 0, CH - POOL_ROWS, c_added_v)
                if not first:
                    keep(j)

            steps_loop(dve, pair, keep)
            pairs = dve.value_load(pairs_of[0:1, 0:1], min_val=0, max_val=NPAIRS)
            dve.wait_ge(c_rho, 2 * pairs + 2)
            rho = RHO[:, :].rearrange("p (b k) -> p b k", b=B)[:, :, FRONT:TCP]
            dve.tensor_reduce(soft[:, 0, :], rho, AX_X, ALU.max, negate=True).then_inc(c_neg_max, 1)
            with dve.Fori(0, PAIRS) as i:
                for u in range(2):
                    b = 2 * i + u
                    dve.wait_ge(c_exp, b + 1)
                    dve.wait_ge(c_ctx_used, b + 1)
                    for k in range(2):
                        last = dve.tensor_tensor_reduce(weighed[u][:, k, :], E[u][:, :], ps[2 * u + k][0:T, 0:TC],
                                                        1.0, 0.0, ALU.mult, ALU.add, share[:, u, k:k + 1])
                    last.then_inc(c_wb_taken[u], 1)
                for u in range(2):
                    dve.wait_ge(c_wb_taken[u], i + 1)
                dve.tensor_copy(soft[:, 3:5, bass.ds(2 * i, 2)].rearrange("p k u -> p u k"), share[:, :, :])                   .then_inc(c_shared, 1)
                dve.wait_ge(c_shared, i + 1)
            chain = Chain(dve, c_step, 0, 1)
            chain(dve.reciprocal(soft[:, 2, :], soft[:, 1, :]))
            dve.tensor_tensor(soft[:, 3:5, :], soft[:, 3:5, :], soft[:, 2:3, :].to_broadcast([T, 2, B]), ALU.mult)\
               .then_inc(c_shares, 1)
            dve.wait_ge(c_ws, 2)

            def update(i):
                for u in range(2):
                    b = 2 * i + u
                    dve.tensor_scalar(W[u][:, :], XNA[:, bass.ds(b, 1), :].rearrange("p o d -> p (o d)"),
                                      soft[:, 5, bass.ds(b, 1)], soft[:, 6, bass.ds(b, 1)], ALU.mult, ALU.add)\
                       .then_inc(c_y, 1)
                for u in range(2):
                    b = 2 * i + u
                    dve.wait_ge(c_y, b + 1)
                    xb = X[:, bass.ds(b, 1), :].rearrange("p o d -> p (o d)")
                    dve.scalar_tensor_tensor(xb, W[u][:, :], tanh_gates[:, 1:2], xb, ALU.mult, ALU.add)\
                       .then_inc(x_updated, 1)
                dve.wait_ge(x_updated, 2 * B + 2 * i + 2)

            dve.wait_ge(c_kept, B)
            update(0)
            layer_norm(dve, 0, 3 * PAIRS, lambda: dve.wait_ge(c_a_full, B))
            with dve.Fori(1, PAIRS) as i:
                update(i)

        def additive_gpsimd(pool):
            pool.wait_ge(x_updated, B)
            for tile, pieces in ((RHO, [RHO[:, :]]), (TT, [TT[:, e, :] for e in range(DC)])):
                for piece in pieces:
                    pool.memset(piece, 0.0).then_inc(c_padded, 1)

            def keep_xn(i):
                for u in range(2):
                    b = 2 * i + u
                    pool.wait_ge(xn_ready, 4 * PAIRS + b + 1)
                    pool.tensor_copy(XNA[:, bass.ds(b, 1), :].rearrange("p o d -> p (o d)"), XN[u][:, :]).then_inc(c_kept, 1)

            with pool.Fori(0, PAIRS - 1) as i:
                keep_xn(i)
                layer_norm_root(pool, 2 * PAIRS + i + 1)
            keep_xn(PAIRS - 1)
            pool.wait_ge(c_f_taken, B)
            for e in range(DC):
                pool.wait_ge(c_t_taken[e], B)
            steps_loop(pool, lambda j, first: add_halves(pool, j, first, CH - POOL_ROWS, POOL_ROWS, c_added_p))
            layer_norm_root(pool, 3 * PAIRS)

        PER1 = 2
        dense = Attention(sem, "d", att_bufs, 2 * PER1, 4, T, T, HP ** -0.5)
        d_a_full, d_a_taken = sem("d_a_full"), sem("d_a_taken")
        d_q_full, d_q_taken = sem("d_q_full"), sem("d_q_taken")
        d_v_full, d_v_taken = sem("d_v_full"), sem("d_v_taken")
        d_o_taken = sem("d_o_taken")
        d_rope_step, d_roped = sem("d_rope_step"), sem("d_roped")
        d_kept = sem("d_kept")
        d_zeroed = sem("d_zeroed")
        d_y_full = sem("d_y_full")

        def rotate(eng, qk, cos, sin, step, base, done):
            h = ROT // 2
            ins = eng.tensor_tensor(RA[:, :, :, :], qk[:, :, :, 0:ROT], cos, ALU.mult)
            ins.then_inc(step, 1)
            for r in range(2):
                eng.tensor_tensor(RB[:, :, :, r * h:(r + 1) * h], qk[:, :, :, (1 - r) * h:(2 - r) * h],
                                  sin[:, :, :, r * h:(r + 1) * h], ALU.mult).then_inc(step, 1)
            eng.wait_ge(step, base + 3)
            eng.tensor_tensor(qk[:, :, :, 0:ROT], RA[:, :, :, :], RB[:, :, :, :], ALU.add).then_inc(done, 1)

        def transpose_qk(pe, qk, full, taken, at):
            for k in range(2):
                pe.wait_ge(taken, at + k)
                for q in range(4):
                    last = pe.transpose(ps[0][:, q * T:(q + 1) * T],
                                        qk[:, k, 2 * q:2 * q + 2, :].rearrange("p h d -> p (h d)"), ident[0:T, 0:T])
                last.then_inc(full, 1)

        def take_qk(act, qt, kbd, full, taken, at):
            act.wait_ge(full, at + 1)
            act.activation(qt[:, :, :].rearrange("p q t -> p (q t)"), ps[0][:, 0:4 * T], ACT.Copy).then_inc(taken, 1)
            act.wait_ge(full, at + 2)
            for k in range(2):
                last = act.activation(kbd[64 * k:64 * k + 64, :, k * T:(k + 1) * T],
                                      ps[0][64 * k:64 * k + 64, 0:4 * T].rearrange("p (q t) -> p q t", q=4), ACT.Copy)
            last.then_inc(taken, 1)

        def pair_scores(pe, bank, qt, kbd, first, n):
            for k in range(n):
                last = pe.matmul(bank[0:T, k * 2 * T:(k + 1) * 2 * T], qt[:, first + k, :], kbd[:, first + k, :],
                                 start=True, stop=True)
            return last

        def pair_values(pe, v, probsT, first, n):
            for k in range(n):
                head = first + k
                r = 64 * (head % 2)
                last = pe.matmul(ps[3][r:r + 64, (head // 2) * T:(head // 2 + 1) * T], v[:, head * HP:(head + 1) * HP],
                                 probsT[0:T, k * T:(k + 1) * T], start=True, stop=True)
            return last

        def dense_tensor(pe):
            pe.wait_ge(weights_d_in, 16 * 5)
            with pe.Fori(0, PAIRS) as i:
                for u in range(2):
                    b = 2 * i + u
                    pe.wait_ge(d_a_taken, 3 * b)
                    transpose_xn(pe, b, 6 * PAIRS + b, u, ps[0], d_a_full)
                    pe.wait_ge(d_a_taken, 3 * b + 1)
                    for k in range(2):
                        pe.wait_ge(d_q_taken, 2 * b + k)
                        for c in range(DC):
                            last = pe.matmul(ps[1][0:T, :], XT[u][:, c, :], wqkv1[:, c, k * 512:(k + 1) * 512],
                                             start=(c == 0), stop=(c == DC - 1))
                        last.then_inc(d_q_full, 1)
                    pe.wait_ge(d_v_taken, 2 * b)
                    pe.wait_ge(x_updated, 3 * B + 2 * i)
                    for c in range(DC):
                        last = pe.matmul(ps[2][0:T, :], XT[u][:, c, :], wqkv1[:, c, 1024:1536],
                                         start=(c == 0), stop=(c == DC - 1))
                    last.then_inc(d_v_full, 1)
                    pe.wait_ge(d_v_taken, 2 * b + 1)
                    for c in range(DC):
                        last = pe.matmul(ps[2][0:NH, 0:T], wr1[:, c, :], XT[u][:, c, :], start=(c == 0), stop=(c == DC - 1))
                    last.then_inc(d_v_full, 1)
                    pe.wait_ge(d_roped, b + 1)
                    transpose_qk(pe, QK1[u], d_a_full, d_a_taken, 3 * b + 1)

                def scores(g, bank):
                    u, j = g // PER1, g % PER1
                    if j == 0:
                        pe.wait_ge(d_a_taken, 3 * (2 * i + u) + 3)
                    return pair_scores(pe, bank, QT1[u], KBD1[u], 2 * j, 2)

                def values(g, probsT):
                    u, j = g // PER1, g % PER1
                    if j == 0:
                        pe.wait_ge(d_o_taken, 2 * i + u)
                    return pair_values(pe, V1[u], probsT, 4 * j, 4)

                def after(g):
                    u, j = g // PER1, g % PER1
                    if j == PER1 - 1:
                        b = 2 * i + u
                        pe.wait_ge(d_o_taken, b + 1)
                        pe.wait_ge(x_updated, 3 * B + b)
                        pe.wait_ge(d_v_taken, 4 * i + 4)
                        for q in range(4):
                            last = pe.matmul(ps[2][0:T, 0:D], O1[:, q * T:(q + 1) * T], wo1[:, q, :],
                                             start=(q == 0), stop=(q == 3))
                        last.then_inc(d_y_full, 1)

                dense.tensor(pe, i, scores, values, after)

        def dense_scalar(act):
            act.wait_ge(d_zeroed, 2)
            with act.Fori(0, PAIRS) as i:
                for u in range(2):
                    b = 2 * i + u
                    act.wait_ge(d_a_full, 3 * b + 1)
                    act.activation(XT[u][:, :, :].rearrange("p c t -> p (c t)"), ps[0][:, 0:DC * T], ACT.Copy)\
                       .then_inc(d_a_taken, 1)
                    for k in range(2):
                        act.wait_ge(d_q_full, 2 * b + k + 1)
                        act.activation(QK1[u][:, k, :, :].rearrange("p h d -> p (h d)"), ps[1][0:T, :], ACT.Copy)\
                           .then_inc(d_q_taken, 1)
                    take_qk(act, QT1[u], KBD1[u], d_a_full, d_a_taken, 3 * b + 1)

                def after(g):
                    if g % PER1 == PER1 - 1:
                        b = 2 * i + g // PER1
                        act.wait_ge(dense.values_done[g % 2], i * PER1 + g // 2 + 1)
                        act.wait_ge(d_y_full, b)
                        act.activation(O1[:, :], ps[3][:, 0:4 * T], ACT.Copy).then_inc(d_o_taken, 1)

                dense.scalar(act, i, after)

        def dense_vector(dve):
            with dve.Fori(0, PAIRS) as i:
                for u in range(2):
                    b = 2 * i + u
                    dve.wait_ge(d_v_full, 2 * b + 1)
                    dve.tensor_copy(V1[u][:, :], ps[2][0:T, :]).then_inc(d_v_taken, 1)
                    dve.wait_ge(d_v_full, 2 * b + 2)
                    dve.tensor_copy(SC[:, bass.ds(b, 1), :].rearrange("p o t -> p (o t)"), ps[2][0:NH, 0:T])\
                       .then_inc(d_v_taken, 1)

                def mask(g):
                    return const("causal", T).unsqueeze(1).to_broadcast([T, 4, T])

                def after(g):
                    if g % PER1 == PER1 - 1:
                        b = 2 * i + g // PER1
                        dve.wait_ge(d_y_full, b + 1)
                        xb = X[:, bass.ds(b, 1), :].rearrange("p o d -> p (o d)")
                        dve.scalar_tensor_tensor(xb, ps[2][0:T, 0:D], tanh_gates[:, 3:4], xb, ALU.mult, ALU.add)\
                           .then_inc(x_updated, 1)
                    if g == 0:
                        layer_norm(dve, (i + 1) & (PAIRS - 1), 3 * PAIRS + i + 1,
                                   lambda: (dve.wait_ge(d_a_full, 6 * i + 6), dve.wait_ge(d_kept, 2 * i + 2)))

                dense.vector(dve, i, mask, after)

        def dense_gpsimd(pool):
            cos = const("cos", T).unsqueeze(1).unsqueeze(1).to_broadcast([T, 2, NH, ROT])
            sin = const("sin", T).unsqueeze(1).unsqueeze(1).to_broadcast([T, 2, NH, ROT])
            pool.wait_ge(x_updated, 3 * B)
            for u in range(2):
                pool.memset(KBD1[u][:, :, :], 0.0).then_inc(d_zeroed, 1)
            with pool.Fori(0, PAIRS) as i:
                for u in range(2):
                    b = 2 * i + u
                    pool.wait_ge(xn_ready, 6 * PAIRS + b + 1)
                    pool.tensor_copy(XNA[:, bass.ds(b, 1), :].rearrange("p o d -> p (o d)"), XN[u][:, :]).then_inc(d_kept, 1)
                    pool.wait_ge(d_q_taken, 2 * b + 2)
                    rotate(pool, QK1[u][:, :, :, :], cos, sin, d_rope_step, 3 * b, d_roped)

                def after(g):
                    if g == 0:
                        layer_norm_root(pool, 3 * PAIRS + i + 1)

                dense.gpsimd(pool, i, lambda g: None, after)

        mosa = Attention(sem, "d", att_bufs, dense.tiles, NH // RING, T, T, HP ** -0.5)
        assert mosa.tiles == RING
        o_step = sem("o_step")
        o_picked, o_cols_full = sem("o_picked"), sem("o_cols_full")
        o_bd, o_pos_full, o_pos_taken = sem("o_bd"), sem("o_pos_full"), sem("o_pos_taken")
        o_onehot = sem("o_onehot")
        o_g_full, o_g_taken = sem("o_g_full"), sem("o_g_taken")
        o_cs_full, o_cs_taken = sem("o_cs_full"), sem("o_cs_taken")
        o_pn_full, o_pn_taken = sem("o_pn_full"), sem("o_pn_taken")
        o_qkv_full, o_qkv_taken = sem("o_qkv_full"), sem("o_qkv_taken")
        o_rope_step, o_roped = sem("o_rope_step"), sem("o_roped")
        o_a_full, o_a_taken = sem("o_a_full"), sem("o_a_taken")
        o_mask, o_halved, o_gate = sem("o_mask"), sem("o_halved"), sem("o_gate")
        o_o_taken = sem("o_o_taken")
        o_z_full, o_z_taken = sem("o_z_full"), sem("o_z_taken")
        o_z_out, o_z_in = sem("o_z_out"), sem("o_z_in")
        o_row = sem("o_row")
        o_y_full = sem("o_y_full")
        z_rows = nc.dram_tensor("z_rows", (T, NH, D), F32, kind="Internal").ap()

        def mosa_sync(sp):
            sp.wait_ge(o_z_taken, NH)
            sp.dma_start(z_rows, Z[:, :, :]).then_inc(o_z_out, 16)
            sp.wait_ge(o_z_out, 16)
            by_head = z_rows.rearrange("(b j) n d -> n j b d", b=B)
            for n in range(NH):
                sp.dma_start(Z2[n * KSEL:(n + 1) * KSEL, :, :], by_head[n]).then_inc(o_z_in, 16)
            with sp.Fori(0, B) as b:
                sp.wait_ge(x_updated, 4 * B + b + 1)
                sp.dma_start(out[bass.ds(b, 1), :, :].rearrange("o t d -> t (o d)"),
                             X[:, bass.ds(b, 1), :].rearrange("p o d -> p (o d)")).then_inc(stored, 16)
            sp.wait_ge(stored, 16 * B)

        def mosa_tensor(pe):
            pe.wait_ge(o_picked, 2)
            pe.transpose(ps[1][0:T, 0:NH], IDX[:, :, :].rearrange("n b j -> n (b j)"), ident[0:NH, 0:NH])
            pe.transpose(ps[1][0:T, NH:2 * NH], VAL[:, :, :].rearrange("n b j -> n (b j)"), ident[0:NH, 0:NH])\
              .then_inc(o_cols_full, 1)
            pe.wait_ge(o_bd, 1)
            for k in range(2):
                pe.matmul(ps[4 + k][0:T, 0:4 * T], const("ones", NH)[:, 0:T],
                          BD[:, 4 * k:4 * k + 4, :].rearrange("p n r -> p (n r)"), start=True, stop=True)\
                  .then_inc(o_pos_full, 1)
            pe.wait_ge(o_onehot, 1)
            for n in range(NH):
                last = pe.matmul(ps[6][0:T, n * 2 * ROT:(n + 1) * 2 * ROT], OH[:, n, :, :].rearrange("p b j -> p (b j)"),
                                 consts[0:T, CONST["cos"][0]:CONST["sin"][1]], start=True, stop=True)
            last.then_inc(o_cs_full, 1)
            for turn in range(4):
                c, half = turn // 2, turn % 2
                if turn >= 2:
                    pe.wait_ge(o_g_taken, turn - 1)
                for b in range(4):
                    last = pe.matmul(ps[2 * (turn % 2)][:, b * T:(b + 1) * T], XNA[:, 4 * half + b, c * 128:(c + 1) * 128],
                                     OH[:, :, 4 * half + b, :], start=True, stop=True)
                last.then_inc(o_g_full, 1)
            pe.wait_ge(o_onehot, 2)
            for b in range(B):
                last = pe.matmul(ps[7][0:T, b:b + 1], OHB[:, b, :, :].rearrange("p n j -> p (n j)"), const("tokcol", T),
                                 start=True, stop=True)
            last.then_inc(o_pn_full, 1)
            pe.wait_ge(o_g_taken, 4)
            pe.wait_ge(o_pos_taken, 2)
            for turn in range(4):
                if turn >= 2:
                    pe.wait_ge(o_qkv_taken, turn - 1)
                for k in range(2):
                    n = 2 * turn + k
                    for c in range(DC):
                        last = pe.matmul(ps[4 + turn % 2][0:T, k * 3 * HP:(k + 1) * 3 * HP],
                                         XG[:, c, n, :, :].rearrange("p b j -> p (b j)"), wqkvm[:, c, n, :],
                                         start=(c == 0), stop=(c == DC - 1))
                last.then_inc(o_qkv_full, 1)
            pe.wait_ge(o_roped, 1)
            transpose_qk(pe, QK1[0], o_a_full, o_a_taken, 0)
            pe.wait_ge(o_a_taken, 2)
            pe.wait_ge(o_qkv_taken, 4)
            pe.wait_ge(o_cs_taken, 1)
            pe.wait_ge(o_pn_taken, 1)

            mosa.tensor(pe, PAIRS, lambda g, bank: pair_scores(pe, bank, QT1[0], KBD1[0], g, 1),
                        lambda g, probsT: pair_values(pe, V1[0], probsT, 2 * g, 2), lambda g: None)
            pe.wait_ge(o_o_taken, 1)
            for turn in range(4):
                if turn >= 2:
                    pe.wait_ge(o_z_taken, 2 * (turn - 1))
                for k in range(2):
                    n = 4 * (turn // 2) + 2 * k + turn % 2
                    r = 64 * (n % 2)
                    last = pe.matmul(ps[1 + turn % 2][0:T, k * D:(k + 1) * D],
                                     O1[r:r + 64, (n // 2) * T:(n // 2 + 1) * T], wom[r:r + 64, n // 2, :],
                                     start=True, stop=True)
                last.then_inc(o_z_full, 1)
            pe.wait_ge(o_z_in, 16 * NH)
            with pe.Fori(0, PAIRS) as i:
                for u in range(2):
                    b = 2 * i + u
                    pe.wait_ge(o_row, b + 1)
                    pe.wait_ge(x_updated, 4 * B + 2 * i)
                    pe.matmul(ps[6 + u][0:T, 0:D], OHR[u][:, :], Z2[:, bass.ds(b, 1), :].rearrange("p o d -> p (o d)"),
                              start=True, stop=True).then_inc(o_y_full, 1)

        def mosa_scalar(act):
            act.wait_ge(o_halved, 1)
            act.activation(GATE[:, :], GATE[:, :], ACT.Tanh).then_inc(o_gate, 1)
            for k in range(2):
                act.wait_ge(o_pos_full, k + 1)
                act.activation(POSB[:, 4 * k:4 * k + 4, :].rearrange("p n r -> p (n r)"), ps[4 + k][0:T, 0:4 * T],
                               ACT.Copy).then_inc(o_pos_taken, 1)
            act.wait_ge(o_cs_full, 1)
            act.activation(CS[:, :, :].rearrange("p n r -> p (n r)"), ps[6][0:T, :], ACT.Copy).then_inc(o_cs_taken, 1)
            for turn in range(4):
                c, half = turn // 2, turn % 2
                act.wait_ge(o_g_full, turn + 1)
                act.activation(XG[:, c, :, 4 * half:4 * half + 4, :].rearrange("p n b j -> p b n j"),
                               ps[2 * (turn % 2)][:, 0:4 * T].rearrange("p (b n j) -> p b n j", b=4, n=NH), ACT.Copy)\
                   .then_inc(o_g_taken, 1)
            for turn in range(4):
                act.wait_ge(o_qkv_full, turn + 1)
                src = ps[4 + turn % 2][0:T, 0:6 * HP].rearrange("p (n k d) -> p n k d", n=2, k=3)
                for k in range(2):
                    act.activation(QK1[0][:, k, 2 * turn:2 * turn + 2, :], src[:, :, k, :], ACT.Copy)
                act.activation(V1[0][:, 2 * turn * HP:(2 * turn + 2) * HP].rearrange("p (n d) -> p n d", n=2),
                               src[:, :, 2, :], ACT.Copy).then_inc(o_qkv_taken, 1)
            take_qk(act, QT1[0], KBD1[0], o_a_full, o_a_taken, 0)
            mosa.scalar(act, PAIRS, lambda g: None)
            for s in range(2):
                act.wait_ge(mosa.values_done[s], (PAIRS + 1) * RING // 2)
            act.activation(O1[:, :], ps[3][:, 0:4 * T], ACT.Copy).then_inc(o_o_taken, 1)

        def mosa_vector(dve):
            chain = Chain(dve, o_step, 0, 0, scratch[:, :])
            dve.wait_ge(d_v_taken, 2 * B)
            dve.memset(scratch[:, :], 0.0)
            def each(step):
                for b in range(B):
                    last = step(b)
                chain(last)
            each(lambda b: dve.max(top[:, b, 0:8], SC[:, b, :]))
            each(lambda b: dve.match_replace(rest[:, b, :], top[:, b, 0:8], SC[:, b, :], LOWEST))
            each(lambda b: dve.max(top[:, b, 8:16], rest[:, b, :]))
            each(lambda b: dve.max_index(top_i[:, b, 0:8], top[:, b, 0:8], SC[:, b, :]))
            each(lambda b: dve.max_index(top_i[:, b, 8:16], top[:, b, 8:16], rest[:, b, :]))
            dve.tensor_copy(IDX[:, :, :], top_i[:, :, 0:KSEL]).then_inc(o_picked, 1)
            dve.tensor_copy(VAL[:, :, :], top[:, :, 0:KSEL]).then_inc(o_picked, 1)
            dve.wait_ge(o_picked, 2)
            idx = IDX[:, :, :].rearrange("n b j -> n (b j)").unsqueeze(1).to_broadcast([NH, NH, T])
            diag = ident[0:NH, 0:NH].unsqueeze(2).to_broadcast([NH, NH, T])
            dve.tensor_tensor(BD[:, :, :], idx, diag, ALU.mult).then_inc(o_bd, 1)
            dve.wait_ge(o_cols_full, 1)
            dve.tensor_copy(POSC[:, :], ps[1][0:T, 0:NH])
            dve.tensor_scalar(GATE[:, :], ps[1][0:T, NH:2 * NH], 0.5, None, ALU.mult).then_inc(o_halved, 1)
            dve.wait_ge(o_halved, 1)
            dve.wait_ge(o_pos_taken, 2)
            tok = const("tokcol", T)
            dve.tensor_scalar(OH[:, :, :, :].rearrange("p n b j -> p (n b j)"), POSB[:, :, :].rearrange("p n r -> p (n r)"),
                              tok, None, ALU.is_equal).then_inc(o_onehot, 1)
            dve.tensor_scalar(OHB[:, :, :, :].rearrange("p b n j -> p n b j"),
                              POSB[:, :, :].rearrange("p n (b j) -> p n b j", b=B),
                              tok, None, ALU.is_equal).then_inc(o_onehot, 1)
            for n in range(NH):
                last = dve.tensor_scalar(MM[:, n, :], POSB[:, n, :], POSC[:, n:n + 1], MASKED, ALU.is_gt, ALU.mult)
            chain(last)
            dve.tensor_tensor(MM[:, :, :], MM[:, :, :], const("batchmask", T).unsqueeze(1).to_broadcast([T, NH, T]), ALU.min)\
               .then_inc(o_mask, 1)
            dve.wait_ge(o_pn_full, 1)
            dve.tensor_copy(POSN[:, :], ps[7][0:T, 0:B]).then_inc(o_pn_taken, 1)
            dve.wait_ge(o_mask, 1)
            mosa.vector(dve, PAIRS, lambda g: MM[:, 2 * g:2 * g + 2, :], lambda g: None)
            dve.wait_ge(o_gate, 1)
            chain(dve.tensor_scalar(GATE[:, :], GATE[:, :], 0.5, 0.5, ALU.mult, ALU.add))
            for turn in range(4):
                dve.wait_ge(o_z_full, turn + 1)
                for k in range(2):
                    n = 4 * (turn // 2) + 2 * k + turn % 2
                    dve.tensor_scalar(Z[:, n, :], ps[1 + turn % 2][0:T, k * D:(k + 1) * D], GATE[:, n:n + 1], None, ALU.mult)\
                       .then_inc(o_z_taken, 1)
            dve.wait_ge(o_pn_taken, 1)
            with dve.Fori(0, PAIRS) as i:
                for u in range(2):
                    b = 2 * i + u
                    dve.wait_ge(o_y_full, 2 * i)
                    dve.tensor_scalar(OHR[u][:, :], const("tokrow", T), POSN[:, bass.ds(b, 1)], None, ALU.is_equal)\
                       .then_inc(o_row, 1)
                for u in range(2):
                    b = 2 * i + u
                    dve.wait_ge(o_y_full, b + 1)
                    xb = X[:, bass.ds(b, 1), :].rearrange("p o d -> p (o d)")
                    dve.scalar_tensor_tensor(xb, ps[6 + u][0:T, 0:D], tanh_gates[:, 3:4], xb, ALU.mult, ALU.add)\
                       .then_inc(x_updated, 1)

        def mosa_gpsimd(pool):
            pool.wait_ge(o_cs_taken, 1)
            pool.wait_ge(o_qkv_taken, 4)
            cos = CS[:, :, 0:ROT].unsqueeze(1).to_broadcast([T, 2, NH, ROT])
            sin = CS[:, :, ROT:2 * ROT].unsqueeze(1).to_broadcast([T, 2, NH, ROT])
            rotate(pool, QK1[0][:, :, :, :], cos, sin, o_rope_step, 0, o_roped)
            mosa.gpsimd(pool, PAIRS, lambda g: None, lambda g: None)

        narrow, wide = cross0(1), cross0(NKT)
        SYNC, PE_, ACT_, DVE_, POOL_ = range(5)

        def cross0_on(eng, which):
            eng.wait_ge(wide_set, 1)
            flag = eng.value_load(wide_i[0:1, 0:1], min_val=0, max_val=2)
            with eng.If(flag == 0):
                narrow[which](eng)
            with eng.Else():
                wide[which](eng)

        block = ctx.enter_context(nc.Block())

        @block.sync
        def _(sp):
            sp.dma_start(consts[:, :], a["consts"]).then_inc(consts_in, 16)
            sp.dma_start(bnd_i[:, :], a["boundsT"]).then_inc(small_in, 16)
            sp.dma_start(X[:, :, :], a["x"].rearrange("b t d -> t b d")).then_inc(x_in, 16)
            for w, name in ((wq0, "wqT0"), (wk0, "wkT0"), (wv0, "wvT0"), (wo0, "woT0")):
                sp.dma_start(w[:, :, :], a[name]).then_inc(weights0_in, 16)
            sp.dma_start(bqk0[:, :, :], a["bqk0"]).then_inc(weights0_in, 16)
            sp.dma_start(bv0[:, :], a["bv0"].partition_broadcast(128)).then_inc(weights0_in, 16)
            sp.dma_start(bo0[:, :], a["bo0"].partition_broadcast(1)).then_inc(weights0_in, 16)
            sp.dma_start(gates[:, :], a["gates"].partition_broadcast(T)).then_inc(small_in, 16)
            for w, name in ((wg0, "wgT0"), (we0, "weT0")):
                sp.dma_start(w[:, :, :], a[name]).then_inc(weights_moe_in, 16)
            sp.dma_start(bg0[:, :], a["bg0"].partition_broadcast(1)).then_inc(weights_moe_in, 16)
            sp.dma_start(be0[:, :], a["be0"]).then_inc(weights_moe_in, 16)
            sp.dma_start(qmask_i[:, :, :], a["qmask"].rearrange("b t -> (b t)").partition_broadcast(T)).then_inc(qmask_in, 16)
            for w, name in ((ws1, "ws1"), (wf1, "wf1")):
                sp.dma_start(w[:, :, :], a[name]).then_inc(weights_c_in, 16)
            sp.dma_start(w1_col[:, :], a["w1_col"]).then_inc(weights_c_in, 16)
            sp.dma_start(wcwb_col[:, :, :], a["wcwb_col"]).then_inc(weights_c_in, 16)
            sp.dma_start(bf1[:, :], a["bf1"]).then_inc(weights_c_in, 16)
            sp.dma_start(bcwb[:, :], a["bcwb"].partition_broadcast(T)).then_inc(weights_c_in, 16)
            for w, name in ((wqkv1, "wqkv1"), (wo1, "wo1"), (wr1, "wr1"), (wom, "wom")):
                sp.dma_start(w[:, :, :], a[name]).then_inc(weights_d_in, 16)
            sp.dma_start(wqkvm[:, :, :, :].rearrange("p c h d -> p c (h d)"), a["wqkvm"]).then_inc(weights_d_in, 16)
            cross0_on(sp, SYNC)
            additive_sync(sp)
            mosa_sync(sp)

        @block.tensor
        def _(pe):
            pe.wait_ge(consts_in, 16)
            pe.wait_ge(bnd_ready, 1)
            pe.matmul(ps[3][0:T, 0:B], const("tri", T), bnd_f[:, :], start=True, stop=True).then_inc(last_key_full, 1)
            pe.wait_ge(wide_ready, 1)
            pe.transpose(ps[3][0:1, 0:T], wide_col[:, :], ident[0:T, 0:T]).then_inc(wide_full, 1)
            pe.wait_ge(weights0_in, 16 * 7)
            pe.wait_ge(zeroed, 1)
            cross0_on(pe, PE_)
            experts_tensor(pe)
            additive_tensor(pe)
            dense_tensor(pe)
            mosa_tensor(pe)

        @block.scalar
        def _(act):
            act.wait_ge(small_in, 32)
            act.activation(tanh_gates[:, :], gates[:, :], ACT.Tanh).then_inc(tanh_ready, 1)
            act.wait_ge(weights0_in, 16 * 7)
            cross0_on(act, ACT_)
            experts_scalar(act)
            additive_scalar(act)
            dense_scalar(act)
            mosa_scalar(act)

        @block.vector
        def _(dve):
            dve.wait_ge(small_in, 32)
            dve.tensor_copy(bnd_f[:, :], bnd_i[:, :]).then_inc(bnd_ready, 1)
            link(dve, dve.memset(var_eps[:, 1, :], -0.5))
            dve.wait_ge(last_key_full, 1)
            link(dve, dve.tensor_copy(last_key[:, :], ps[3][0:T, 0:B]))
            link(dve, dve.tensor_scalar(beyond[:, 0, :], last_key[:, :], KT - 1.0, None, ALU.is_gt))
            link(dve, dve.tensor_scalar(beyond[:, 1, :], last_key[:, :], 0.0, None, ALU.is_lt))
            link(dve, dve.tensor_tensor(beyond[:, 2, :], beyond[:, 0, :], beyond[:, 1, :], ALU.add))
            dve.tensor_reduce(wide_col[:, :], beyond[:, 2, :], AX_X, ALU.max).then_inc(wide_ready, 1)
            dve.wait_ge(wide_full, 1)
            dve.tensor_reduce(wide_i[:, :], ps[3][0:1, 0:T], AX_X, ALU.max).then_inc(wide_set, 1)
            dve.wait_ge(x_in, 16)
            layer_norm(dve, 0, 0, lambda: None)
            prepare_steps(dve)
            dve.wait_ge(weights0_in, 16 * 7)
            dve.wait_ge(tanh_ready, 1)
            dve.wait_ge(zeroed, 1)
            cross0_on(dve, DVE_)
            experts_vector(dve)
            additive_vector(dve)
            dense_vector(dve)
            mosa_vector(dve)

        @block.gpsimd
        def _(pool):
            pool.memset(zeros[:, :], 0.0)
            for u in range(2):
                last = pool.memset(V0[u][:, :, :, :], 0.0)
            last.then_inc(zeroed, 1)
            layer_norm_root(pool, 0)
            pool.wait_ge(consts_in, 16)
            cross0_on(pool, POOL_)
            experts_gpsimd(pool)
            additive_gpsimd(pool)
            dense_gpsimd(pool)
            mosa_gpsimd(pool)


def layout(i):
    import numpy as np
    n = {k: np.asarray(v) for k, v in i.items()}

    def rows(w):
        return np.ascontiguousarray(w.reshape(w.shape[0] // 128, 128, -1).transpose(1, 0, 2))

    a = {"x": np.ascontiguousarray(n["x"])}
    a["ctxT"] = rows(n["ctx_1024"].transpose(2, 0, 1).reshape(D, B * TC))
    a["boundsT"] = np.ascontiguousarray(n["mask_BxS_ik0"].T)
    a["wqT0"] = rows(n["L0_xattn_wq"].T)
    a["wkT0"] = rows(n["L0_xattn_wk"].T)
    a["wvT0"] = rows(n["L0_xattn_wv"].T)
    wo = np.zeros((128, 4, D), n["L0_xattn_wo"].dtype)
    for q in range(4):
        for h in range(4):
            head = 4 * q + h
            wo[PAD0 * h:PAD0 * h + DH0, q] = n["L0_xattn_wo"].T[head * DH0:(head + 1) * DH0]
    a["woT0"] = wo
    a["bqk0"] = np.ascontiguousarray(np.stack([n["L0_xattn_bq"], n["L0_xattn_bk"]]).reshape(2, DC, 128).transpose(2, 0, 1))
    a["bv0"] = n["L0_xattn_bv"]
    a["bo0"] = n["L0_xattn_bo"]
    a["wgT0"] = rows(n["L0_ffn_Wg"].T)
    a["bg0"] = n["L0_ffn_bg"]
    a["weT0"] = rows(n["L0_ffn_W"].transpose(2, 0, 1).reshape(D, NE * D))
    a["be0"] = n["L0_ffn_b"]
    a["qmask"] = np.ascontiguousarray(n["mask_BxS2_ik0"])
    a["ws1"] = rows(n["L1_xattn_Ws"])
    a["wf1"] = rows(n["L1_xattn_W"])
    a["w1_col"] = np.ascontiguousarray(n["L1_xattn_w"].reshape(DC, 128).T)
    a["wcwb_col"] = np.ascontiguousarray(
        np.concatenate([n["L1_xattn_Wcw"], n["L1_xattn_Wcb"]]).reshape(2, DC, 128).transpose(2, 0, 1))
    a["bf1"] = np.ascontiguousarray(n["L1_xattn_b"].reshape(DC, 128).T)
    a["bcwb"] = np.concatenate([n["L1_xattn_bcw"], n["L1_xattn_bcb"]])
    a["wqkv1"] = rows(n["L1_ffn_dense_wqkv"].reshape(D, NH, 3, HP).transpose(0, 2, 1, 3).reshape(D, 3 * NH * HP))
    a["wo1"] = rows(n["L1_ffn_dense_wo"])
    a["wr1"] = rows(n["L1_ffn_mosa_router_w"])
    a["wqkvm"] = rows(n["L1_ffn_mosa_wqkv"].reshape(D, NH * 3 * HP))
    a["wom"] = rows(n["L1_ffn_mosa_wo"])
    a["gates"] = np.concatenate([n["g_xattn"], n["g_ffn"]])
    a["consts"] = shape_constants(np)
    return a


def shape_constants(np):
    c = np.zeros((128, NCONST), np.float32)

    def put(name, v):
        lo, hi = CONST[name]
        c[:v.shape[0], lo:hi] = v

    put("ident", np.eye(128))
    t = np.arange(T)
    put("tri", (t[:, None] <= t[None, :]) * 1.0)
    put("headmask", (np.arange(128)[:, None] // DH0 == np.arange(8)[None, :]) * 1.0)
    put("keyidx", np.broadcast_to(np.arange(TC), (128, TC)))
    put("causal", (t[None, :] > t[:, None]) * MASKED)
    k = T // B
    put("batchmask", (t[None, :] // k != t[:, None] // k) * MASKED)
    put("tokcol", t[:, None])
    put("tokrow", np.broadcast_to(t, (128, T)))
    half = ROT // 2
    inv = np.float32(10000.0) ** (-np.arange(half, dtype=np.float32) / half)
    ang = t[:, None].astype(np.float32) * inv
    put("cos", np.concatenate([np.cos(ang), np.cos(ang)], 1))
    put("sin", np.concatenate([-np.sin(ang), np.sin(ang)], 1))
    put("iota8", np.broadcast_to(np.arange(NE), (128, NE)))
    put("ones", np.ones((128, 128)))
    return c


def kernel(**inputs):
    import numpy as np
    import concourse.bacc as bacc
    from concourse.bass_utils import run_bass_kernel_spmd

    nc = bacc.Bacc("TRN2", target_bir_lowering=False, num_devices=1)
    arrays, args = {}, {}
    for name, v in layout(inputs).items():
        v = np.ascontiguousarray(v)
        arrays["in_" + name] = v
        args[name] = nc.dram_tensor("in_" + name, v.shape, mybir.dt.from_np(v.dtype), kind="ExternalInput").ap()
    out = nc.dram_tensor("out", (B, T, D), F32, kind="ExternalOutput").ap()
    flamingo_kernel(nc, args, out)
    r = run_bass_kernel_spmd(nc, [arrays], core_ids=[0])
    return r.results[0]["out"]
```

```python
import concourse.bass as bass
from concourse import mybir
from contextlib import ExitStack

F32 = mybir.dt.float32
I32 = mybir.dt.int32
U32 = mybir.dt.uint32
ALU = mybir.AluOpType
ACT = mybir.ActivationFunctionType
AX_X = mybir.AxisListType.X

B, T, D = 8, 112, 256
TC = 375
DC = D // 128
PAIRS = B // 2
KT = 125
NKT = TC // KT
H0, DH0, PAD0 = 16, 16, 32
NE = 8
NH, HP = 8, 64
ROT = 32
KSEL = T // 8
CH = 16
NCH = -(-TC // (2 * CH))
TCP = NCH * 2 * CH
FRONT = TCP - TC
NPAIRS = B * NCH
PACK = 512
SEG, RUN = 6, 4
POOL_ROWS = 7
RING = 4
AHEAD = 3
LOWEST = -3.4028234663852886e38
MASKED = -1e30

CONST = {}
_at = 0
for _name, _n in (("ident", 128), ("tri", T), ("headmask", 8), ("keyidx", TC), ("causal", T), ("batchmask", T),
                  ("tokcol", 1), ("tokrow", T), ("cos", ROT), ("sin", ROT), ("iota8", NE), ("ones", 128)):
    CONST[_name] = (_at, _at + _n)
    _at += _n
NCONST = _at


def nothing(*_):
    pass


class Attention:

    def __init__(self, sem, name, bufs, tiles, nh, keys, kt):
        self.tiles, self.nh, self.keys, self.kt = tiles, nh, keys, kt
        self.nkt = keys // kt
        self.ident, self.score_ps, self.probsT_ps = bufs["ident"], bufs["score_ps"], bufs["probsT_ps"]
        self.score_sb, self.probsT_sb = bufs["score_sb"], bufs["probsT_sb"]
        self.max_sb, self.sum_sb, self.recip_sb = bufs["max_sb"], bufs["sum_sb"], bufs["recip_sb"]
        self.scratch = bufs["scratch"]
        self.scores_full = sem(name + "_scores_full")
        self.scores_taken = [sem(f"{name}_scores_taken{s}") for s in range(2)]
        self.max_ready = sem(name + "_max_ready")
        self.exp_ready = sem(name + "_exp_ready")
        self.recip_ready = sem(name + "_recip_ready")
        self.probs_ready = sem(name + "_probs_ready")
        self.probsT_full = [sem(f"{name}_probsT_full{s}") for s in range(RING)]
        self.probsT_taken = [sem(f"{name}_probsT_taken{s}") for s in range(2)]
        self.values_done = [sem(f"{name}_values_done{s}") for s in range(2)]

    def tile(self, g):
        return self.score_sb[0:T, g % RING, 0:self.nh * self.keys]

    def heads(self, g):
        return self.tile(g).rearrange("p (h k) -> p h k", h=self.nh)


    def tensor(self, pe, i, scores, values, after, beside=nothing):
        n = self.nh * self.nkt

        def do_scores(g):
            pe.wait_ge(self.scores_taken[g % 2], i * (self.tiles // 2) + g // 2)
            scores(g, self.score_ps[g % 2]).then_inc(self.scores_full, 1)

        def do_transposes(g):
            pe.wait_ge(self.probs_ready, i * self.tiles + g + 1)
            pe.wait_ge(self.probsT_taken[g % 2], i * (self.tiles // 2) + g // 2)
            for j in range(n):
                last = pe.transpose(self.probsT_ps[g % 2][0:self.kt, j * T:(j + 1) * T],
                                    self.tile(g)[:, j * self.kt:(j + 1) * self.kt], self.ident[0:T, 0:T])
            last.then_inc(self.probsT_full[g % RING], 1)

        def do_values(g):
            pe.wait_ge(self.probsT_taken[g % 2], i * (self.tiles // 2) + g // 2 + 1)
            values(g, self.probsT_sb[g % 2]).then_inc(self.values_done[g % 2], 1)

        for g in range(AHEAD):
            do_scores(g)
        for g in range(self.tiles):
            if g + AHEAD < self.tiles:
                do_scores(g + AHEAD)
            do_transposes(g)
            if g > 0:
                do_values(g - 1)
            if g > 1:
                after(g - 2)
            beside(g)
        after(self.tiles - 2)
        do_values(self.tiles - 1)
        after(self.tiles - 1)

    def vector(self, dve, i, mask, after, beside=nothing):
        def first(g):
            dve.wait_ge(self.scores_full, i * self.tiles + g + 1)
            dve.wait_ge(self.probsT_full[g % RING], i * (self.tiles // RING) + g // RING)
            mask(g, None)
            dve.memset(self.scratch, 0.0)
            for h in range(self.nh):
                last = dve.tensor_tensor_reduce(
                    self.heads(g)[:, h, :], self.score_ps[g % 2][0:T, h * self.keys:(h + 1) * self.keys], mask(g, h),
                    1.0, LOWEST, ALU.add, ALU.max, self.max_sb[0:T, g % RING, h:h + 1])
            last.then_inc(self.scores_taken[g % 2], 1)
            dve.wait_ge(self.scores_taken[g % 2], i * (self.tiles // 2) + g // 2 + 1)
            m = self.max_sb[0:T, g % RING, 0:self.nh]
            dve.tensor_scalar(m, m, -1.0, None, ALU.mult).then_inc(self.max_ready, 1)

        def second(g):
            dve.wait_ge(self.exp_ready, i * self.tiles + g + 1)
            dve.reciprocal(self.recip_sb[0:T, g % RING, 0:self.nh], self.sum_sb[0:T, g % RING, 0:self.nh])\
               .then_inc(self.recip_ready, 1)

        for g in range(AHEAD):
            first(g)
        for g in range(self.tiles):
            second(g)
            if g + AHEAD < self.tiles:
                first(g + AHEAD)
            if g >= self.tiles // 2:
                after(g - self.tiles // 2)
            beside(g)
        for g in range(self.tiles // 2, self.tiles):
            after(g)

    def gpsimd(self, pool, i, before=nothing, beside=nothing):
        for g in range(AHEAD):
            before(g)
        for g in range(self.tiles):
            pool.wait_ge(self.recip_ready, i * self.tiles + g + 1)
            r = self.recip_sb[0:T, g % RING, 0:self.nh].unsqueeze(2).to_broadcast([T, self.nh, self.keys])
            pool.tensor_tensor(self.heads(g), self.heads(g), r, ALU.mult).then_inc(self.probs_ready, 1)
            if g + AHEAD < self.tiles:
                before(g + AHEAD)
            beside(g)

    def scalar(self, act, i, after, beside=nothing):
        def exp(g):
            act.wait_ge(self.max_ready, i * self.tiles + g + 1)
            for h in range(self.nh):
                last = act.activation(self.heads(g)[:, h, :], self.heads(g)[:, h, :], ACT.Exp,
                                      bias=self.max_sb[0:T, g % RING, h:h + 1],
                                      accum_out=self.sum_sb[0:T, g % RING, h:h + 1])
            last.then_inc(self.exp_ready, 1)

        def take(g):
            act.wait_ge(self.probsT_full[g % RING], i * (self.tiles // RING) + g // RING + 1)
            act.wait_ge(self.values_done[g % 2], i * (self.tiles // 2) + g // 2)
            cols = self.nh * self.nkt * T
            act.activation(self.probsT_sb[g % 2][0:self.kt, 0:cols], self.probsT_ps[g % 2][0:self.kt, 0:cols],
                           ACT.Copy).then_inc(self.probsT_taken[g % 2], 1)

        for g in range(AHEAD):
            exp(g)
        for g in range(self.tiles):
            take(g)
            if g + AHEAD < self.tiles:
                exp(g + AHEAD)
            if g > 0:
                after(g - 1)
            beside(g)
        after(self.tiles - 1)


class Chain:

    def __init__(self, eng, sem, i, per, scratch=None, before=0):
        self.eng, self.sem, self.base, self.per, self.n, self.scratch = eng, sem, i * per + before, per, 0, scratch

    def __call__(self, ins, carry=False):
        self.n += 1
        ins.then_inc(self.sem, 1)
        self.eng.wait_ge(self.sem, self.base + self.n)
        if carry:
            self.eng.memset(self.scratch, 0.0)

    def end(self):
        assert self.n == self.per, (self.n, self.per)


def flamingo_kernel(nc, a, out):
    ctx = ExitStack()
    with ctx:
        scope = [ctx]

        def sb(name, shape, dt=F32):
            return scope[-1].enter_context(nc.sbuf_tensor(name, shape, dt))

        def stage_buffers():
            scope.append(ExitStack())

        def end_stage_buffers():
            scope.pop().close()

        sems = {}

        def sem(name):
            if name not in sems:
                sems[name] = ctx.enter_context(nc.semaphore(name))
            return sems[name]

        X = sb("X", [T, B, D])
        XN = [sb(f"XN{u}", [T, D]) for u in range(2)]
        consts = sb("consts", [128, NCONST])
        gates = sb("gates", [T, 4])
        tanh_gates = sb("tanh_gates", [T, 4])
        XT = [sb(f"XT{u}", [128, DC, T]) for u in range(2)]
        CT = [sb(f"CT{u}", [128, DC, TC]) for u in range(2)]
        bn = sb("bn", [T, 2, 6])
        mv = sb("mv", [T, 2, 2])
        rstd = sb("rstd", [T, 2])
        scratch = sb("scratch", [T, 1])
        var_eps = sb("var_eps", [T, 2, 2])
        ps = [ctx.enter_context(nc.psum_tensor(f"bank{n}", [128, 512], F32)) for n in range(8)]

        def const(name, rows=128):
            lo, hi = CONST[name]
            return consts[0:rows, lo:hi]

        ident = const("ident")
        att_bufs = bufs = dict(scratch=scratch[:, :],
            ident=ident, score_ps=[ps[4], ps[5]], probsT_ps=[ps[6], ps[7]],
            score_sb=sb("score_sb", [T, RING, 4 * KT]), max_sb=sb("max_sb", [T, RING, 4]),
            sum_sb=sb("sum_sb", [T, RING, 4]), recip_sb=sb("recip_sb", [T, RING, 4]),
            probsT_sb=[sb(f"probsT_sb{s}", [128, 4 * T]) for s in range(2)])

        bqk0 = sb("bqk0", [128, 2, DC])
        bv0 = sb("bv0", [128, D])
        bo0 = sb("bo0", [1, D])
        bnd_i = sb("bnd_i", [T, B], I32)
        bnd_f = sb("bnd_f", [T, B])
        last_key = sb("last_key", [T, B])
        wide_col = sb("wide_col", [T, 1])
        wide_i = sb("wide_i", [1, 1], I32)

        wg0 = sb("wg0", [128, DC, NE])
        bg0 = sb("bg0", [1, NE])
        we0 = sb("we0", [128, DC, NE * D])
        be0 = sb("be0", [NE, D])
        logit = sb("logit", [T, NE])
        router = sb("router", [T, 8, NE])
        router_i = sb("router_i", [T, NE], U32)
        G = [sb(f"G{u}", [T, NE]) for u in range(2)]
        GT = [sb(f"GT{u}", [NE, T]) for u in range(2)]
        Y = sb("Y", [T, D])

        ws1 = sb("ws1", [128, DC, D])
        wf1 = sb("wf1", [128, DC, D])
        w1_col = sb("w1_col", [128, DC])
        w1_rep = sb("w1_rep", [128, DC, 32])
        wcwb_col = sb("wcwb_col", [128, 2, DC])
        wcwb_rep = sb("wcwb_rep", [128, 2, DC, T])
        bf1 = sb("bf1", [128, DC])
        bcwb = sb("bcwb", [T, 2])
        qmask_i = sb("qmask_i", [T, B, TC], I32)
        XNA = sb("XNA", [T, B, D])
        qmask_row = qmask_i[0:1, :, :]
        live = sb("live", [1, 4, B, NCH])
        span = sb("span", [1, 8, B])
        steps_of = sb("steps_of", [1, NPAIRS], I32)
        pairs_of = sb("pairs_of", [1, 2], I32)

        wqkv1 = sb("wqkv1", [128, DC, 3 * NH * HP])
        wo1 = sb("wo1", [128, 4, D])
        wr1 = sb("wr1", [128, DC, NH])
        wqkvm = sb("wqkvm", [128, DC, NH, 3 * HP])
        wom = sb("wom", [128, 4, D])
        zeros = sb("zeros", [T, 1])

        stage_buffers()
        wq0 = sb("wq0", [128, DC, D])
        wk0 = sb("wk0", [128, DC, D])
        wv0 = sb("wv0", [128, DC, D])
        wo0 = sb("wo0", [128, 4, D])
        beyond = sb("beyond", [T, 3, B])
        QT0 = [sb(f"QT0{u}", [128, DC, T]) for u in range(2)]
        KT0 = [sb(f"KT0{u}", [128, DC, TC]) for u in range(2)]
        KBD = [sb(f"KBD{u}", [128, H0 * KT]) for u in range(2)]
        V0 = [sb(f"V0{u}", [128, NKT, H0, PAD0]) for u in range(2)]
        MB = [sb(f"MB{u}", [T, TC]) for u in range(2)]
        O0 = sb("O0", [128, 4 * T])
        QBD = [sb(f"QBD{s}", [128, T]) for s in range(2)]
        end_stage_buffers()

        stage_buffers()
        FT = sb("FT", [128, DC, B * T])
        TT = sb("TT", [128, DC, B * TCP])
        H = [sb(f"H{v}", [128, DC, CH, T]) for v in range(2)]
        R = [sb(f"R{v}", [128, 4 * T]) for v in range(2)]
        RHO = sb("RHO", [T, B * TCP])
        weighed = [sb(f"weighed{u}", [T, 2, TC]) for u in range(2)]
        W = [sb(f"W{u}", [T, D]) for u in range(2)]
        soft = sb("soft", [T, 7, B])
        E = [sb(f"E{u}", [T, TC]) for u in range(2)]
        share = sb("share", [T, 2, 2])
        end_stage_buffers()

        stage_buffers()
        QK1 = [sb(f"QK1{u}", [T, 2, NH, HP]) for u in range(2)]
        RA = sb("RA", [T, 2, NH, ROT])
        RB = sb("RB", [T, 2, NH, ROT])
        V1 = [sb(f"V1{u}", [T, NH * HP]) for u in range(2)]
        QT1 = [sb(f"QT1{u}", [128, 4, T]) for u in range(2)]
        KBD1 = [sb(f"KBD1{u}", [128, 4, 2 * T]) for u in range(2)]
        O1 = sb("O1", [128, 4 * T])
        SC = sb("SC", [NH, B, T])
        top = sb("top", [NH, B, 16])
        top_i = sb("top_i", [NH, B, 16], U32)
        rest = sb("rest", [NH, B, T])
        IDX = sb("IDX", [NH, B, KSEL])
        VAL = sb("VAL", [NH, B, KSEL])
        BD = sb("BD", [NH, NH, T])
        POSC = sb("POSC", [T, NH])
        GATE = sb("GATE", [T, NH])
        POSB = sb("POSB", [T, NH, T])
        OH = sb("OH", [T, NH, B, KSEL])
        OHB = sb("OHB", [T, B, NH, KSEL])
        MM = sb("MM", [T, NH, T])
        XG = sb("XG", [128, DC, NH, B, KSEL])
        CS = sb("CS", [T, NH, 2 * ROT])
        POSN = sb("POSN", [T, B])
        Z = sb("Z", [T, NH, D])
        Z2 = sb("Z2", [T, B, D])
        OHR = [sb(f"OHR{u}", [T, T]) for u in range(2)]
        end_stage_buffers()

        consts_in = sem("consts_in")
        weights0_in = sem("weights0_in")
        weights_moe_in = sem("weights_moe_in")
        x_in = sem("x_in")
        small_in = sem("small_in")
        weights_c_in = sem("weights_c_in")
        weights_d_in = sem("weights_d_in")
        qmask_in = sem("qmask_in")
        ctx_in = [sem(f"ctx_in{u}") for u in range(2)]
        qmask_row_in = sem("qmask_row_in")
        stored = sem("stored")
        x_updated = sem("x_updated")
        bnd_ready = sem("bnd_ready")
        last_key_full = sem("last_key_full")
        wide_ready = sem("wide_ready")
        wide_full = sem("wide_full")
        wide_set = sem("wide_set")
        tanh_ready = sem("tanh_ready")
        zeroed = sem("zeroed")
        dve_step = sem("dve_step")
        stats_ready = sem("stats_ready")
        rstd_ready = sem("rstd_ready")
        xn_ready = sem("xn_ready")
        ln_step = sem("ln_step")

        steps = {"n": 0}

        def link(dve, ins):
            steps["n"] += 1
            ins.then_inc(dve_step, 1)
            dve.wait_ge(dve_step, steps["n"])

        def layer_norm(dve, pair, n, taken):
            for u in range(2):
                dve.bn_stats(bn[:, u, :], X[:, bass.ds(2 * pair + u, 1), :]).then_inc(ln_step, 1)
            dve.wait_ge(ln_step, n * 4 + 2)
            dve.memset(scratch[:, :], 0.0)
            for u in range(2):
                dve.bn_aggr(mv[:, u, :], bn[:, u, :]).then_inc(ln_step, 1)
            dve.wait_ge(ln_step, n * 4 + 4)
            dve.tensor_scalar(var_eps[:, 0, :], mv[:, :, 1], 1e-5, None, ALU.add).then_inc(stats_ready, 1)
            dve.wait_ge(rstd_ready, n + 1)
            taken()
            for u in range(2):
                dve.tensor_scalar(XN[u][:, :], X[:, bass.ds(2 * pair + u, 1), :].rearrange("p o d -> p (o d)"),
                                  mv[:, u, 0:1], rstd[:, u:u + 1], ALU.subtract, ALU.mult).then_inc(xn_ready, 1)

        def layer_norm_root(pool, n):
            pool.wait_ge(stats_ready, n + 1)
            pool.tensor_tensor(rstd[:, :], var_eps[:, 0, :], var_eps[:, 1, :], ALU.pow).then_inc(rstd_ready, 1)

        def transpose_xn(pe, b, n, u, bank, full):
            pe.wait_ge(xn_ready, n + 1)
            for c in range(DC):
                last = pe.transpose(bank[:, c * T:(c + 1) * T], XN[u][:, c * 128:(c + 1) * 128], ident[0:T, 0:T])
            last.then_inc(full, 1)

        def over_pairs(eng, first, body):
            first()
            with eng.Fori(0, PAIRS - 1) as i:
                body(i, False)
            body(PAIRS - 1, True)

        def cross0(nkt):
            nm = "x"
            keys = nkt * KT
            nh = 4 if nkt == 1 else 1
            tiles = 2 * H0 // nh
            per = tiles // 2
            att = Attention(sem, nm, att_bufs, tiles, nh, keys, KT)
            kturns = 1 if nkt == 1 else DC
            AT, BT = 1 + kturns, 1 + nkt
            a_full, a_taken = sem(nm + "_a_full"), sem(nm + "_a_taken")
            b_full, b_taken = sem(nm + "_b_full"), sem(nm + "_b_taken")
            o_taken = sem(nm + "_o_taken")
            y_full, y_taken = sem(nm + "_y_full"), x_updated
            kbd_ready = [sem(f"{nm}_kbd_ready{e}") for e in range(DC)]
            qbd_ready = sem(nm + "_qbd_ready")
            mask_ready = sem(nm + "_mask_ready")

            def sync(sp):
                with sp.Fori(1, PAIRS) as i:
                    for u in range(2):
                        sp.wait_ge(b_full, (i - 1) * (2 * BT) + (u + 1) * BT)
                        sp.dma_start(CT[u][:, :, :], a["ctxT"][:, :, bass.ds((2 * i + u) * TC, TC)])\
                          .then_inc(ctx_in[u], 16)

            def spread_keys(eng, u, e):
                k = KT0[u][:, e, 0:KT].unsqueeze(1).to_broadcast([128, 8, KT])
                m = const("headmask").unsqueeze(2).to_broadcast([128, 8, KT])
                eng.tensor_tensor(KBD[u][:, e * 8 * KT:(e + 1) * 8 * KT].rearrange("p (h k) -> p h k", h=8), k, m,
                                  ALU.mult).then_inc(kbd_ready[e], 1)

            def tensor(pe):
                def turn_xn(i, u):
                    pe.wait_ge(a_taken, i * (2 * AT) + u * AT)
                    transpose_xn(pe, None, 2 * i + u, u, ps[0], a_full)

                def make_q(i, u):
                    pe.wait_ge(a_taken, i * (2 * AT) + u * AT + 1)
                    pe.wait_ge(b_taken, i * (2 * BT) + u * BT)
                    for e in range(DC):
                        for c in range(DC):
                            last = pe.matmul(ps[1][:, e * T:(e + 1) * T], wq0[:, c, e * 128:(e + 1) * 128],
                                             XT[u][:, c, :], start=(c == 0), stop=(c == DC - 1))
                    last.then_inc(b_full, 1)

                def make_k(i, u):
                    pe.wait_ge(ctx_in[u], 16 * (i + 1))
                    for k in range(kturns):
                        pe.wait_ge(a_taken, i * (2 * AT) + u * AT + 1 + k)
                        es = range(DC) if nkt == 1 else [k]
                        for j, e in enumerate(es):
                            for c in range(DC):
                                last = pe.matmul(ps[0][:, j * keys:(j + 1) * keys],
                                                 wk0[:, c, e * 128:(e + 1) * 128], CT[u][:, c, 0:keys],
                                                 start=(c == 0), stop=(c == DC - 1))
                        last.then_inc(a_full, 1)

                def make_v(i, u):
                    for k in range(nkt):
                        pe.wait_ge(b_taken, i * (2 * BT) + u * BT + 1 + k)
                        for c in range(DC):
                            last = pe.matmul(ps[1][0:KT, 0:D], CT[u][:, c, k * KT:(k + 1) * KT], wv0[:, c, :],
                                             start=(c == 0), stop=(c == DC - 1))
                        last.then_inc(b_full, 1)

                def first():
                    for u in range(2):
                        turn_xn(0, u)
                        make_q(0, u)
                        make_k(0, u)
                        if u == 0:
                            make_v(0, u)

                def body(i, last_pair):
                    def beside(g):
                        if g == 0:
                            make_v(i, 1)
                        if last_pair:
                            return
                        if g == tiles - 5:
                            turn_xn(i + 1, 0)
                        if g == tiles - 4:
                            make_q(i + 1, 0)
                        if g == tiles - 3:
                            make_k(i + 1, 0)
                        if g == tiles - 2:
                            make_v(i + 1, 0)
                            turn_xn(i + 1, 1)
                        if g == tiles - 1:
                            make_q(i + 1, 1)
                            make_k(i + 1, 1)

                    def scores(g, bank):
                        u, j = g // per, g % per
                        head = j * nh
                        e, k = head // 8, head % 8
                        if j == 0:
                            pe.wait_ge(b_taken, i * (2 * BT) + u * BT + 1)
                            if nkt == 1:
                                for half in range(DC):
                                    pe.wait_ge(kbd_ready[half], 2 * i + u + 1)
                            else:
                                pe.wait_ge(a_taken, i * (2 * AT) + (u + 1) * AT)
                        if nkt == 1:
                            return pe.matmul(bank[0:T, 0:nh * keys], QT0[u][:, e, :],
                                             KBD[u][:, head * KT:(head + nh) * KT], start=True, stop=True)
                        pe.wait_ge(qbd_ready, i * tiles + g + 1)
                        return pe.matmul(bank[0:T, 0:keys], QBD[g % 2][:, :], KT0[u][:, e, :],
                                         start=True, stop=True)

                    def values(g, probsT):
                        u, j = g // per, g % per
                        if j == 0:
                            pe.wait_ge(b_taken, i * (2 * BT) + (u + 1) * BT)
                            pe.wait_ge(o_taken, 2 * i + u)
                        for h in range(nh):
                            head = j * nh + h
                            r, q = PAD0 * (head % 4), head // 4
                            for k in range(nkt):
                                last = pe.matmul(ps[2][r:r + PAD0, q * T:(q + 1) * T], V0[u][0:KT, k, head, :],
                                                 probsT[0:KT, (h * nkt + k) * T:(h * nkt + k + 1) * T],
                                                 start=(k == 0), stop=(k == nkt - 1))
                        return last

                    def after(g):
                        u, j = g // per, g % per
                        if j == per - 1:
                            b = 2 * i + u
                            pe.wait_ge(o_taken, b + 1)
                            pe.wait_ge(y_taken, b)
                            for q in range(4):
                                pe.matmul(ps[3][0:T, 0:D], O0[:, q * T:(q + 1) * T], wo0[:, q, :],
                                          start=(q == 0), stop=False)
                            pe.matmul(ps[3][0:T, 0:D], const("ones")[0:1, 0:T], bo0[:, :], start=False, stop=True)\
                              .then_inc(y_full, 1)

                    att.tensor(pe, i, scores, values, after, beside)

                over_pairs(pe, first, body)

            def scalar(act):
                def take_xn(i, u):
                    act.wait_ge(a_full, i * (2 * AT) + u * AT + 1)
                    act.activation(XT[u][:, :, :].rearrange("p c t -> p (c t)"), ps[0][:, 0:DC * T], ACT.Copy)\
                       .then_inc(a_taken, 1)

                def take_k(i, u):
                    for k in range(kturns):
                        act.wait_ge(a_full, i * (2 * AT) + u * AT + 2 + k)
                        es = range(DC) if nkt == 1 else [k]
                        for j, e in enumerate(es):
                            last = act.activation(KT0[u][:, e, 0:keys], ps[0][:, j * keys:(j + 1) * keys],
                                                  ACT.Identity, bias=bqk0[:, 1, e:e + 1])
                        last.then_inc(a_taken, 1)

                def first():
                    for u in range(2):
                        take_xn(0, u)
                        take_k(0, u)

                def body(i, last_pair):
                    def beside(g):
                        if last_pair:
                            return
                        if g == tiles - 5:
                            take_xn(i + 1, 0)
                        if g == (tiles - 2 if kturns == 1 else tiles - 3):
                            take_k(i + 1, 0)
                        if g == tiles - 2:
                            take_xn(i + 1, 1)
                        if g == tiles - 1:
                            take_k(i + 1, 1)

                    def after(g):
                        if g % per == per - 1:
                            b = 2 * i + g // per
                            act.wait_ge(att.values_done[g % 2], i * (tiles // 2) + g // 2 + 1)
                            act.wait_ge(y_full, b)
                            act.activation(O0[:, :], ps[2][:, 0:4 * T], ACT.Copy).then_inc(o_taken, 1)

                    att.scalar(act, i, after, beside)

                over_pairs(act, first, body)

            def vector(dve):
                def take_q(i, u):
                    dve.tensor_scalar(MB[u][:, 0:keys], const("keyidx", T)[:, 0:keys],
                                      last_key[:, bass.ds(2 * i + u, 1)], LOWEST, ALU.is_gt, ALU.mult)\
                       .then_inc(mask_ready, 1)
                    dve.wait_ge(b_full, i * (2 * BT) + u * BT + 1)
                    for e in range(DC):
                        last = dve.tensor_scalar(QT0[u][:, e, :], ps[1][:, e * T:(e + 1) * T],
                                                 bqk0[:, 0, e:e + 1], DH0 ** -0.5, ALU.add, ALU.mult)
                    last.then_inc(b_taken, 1)

                def take_v(i, u):
                    for k in range(nkt):
                        dve.wait_ge(b_full, i * (2 * BT) + u * BT + 2 + k)
                        dve.tensor_tensor(V0[u][0:KT, k, :, 0:DH0],
                                          ps[1][0:KT, 0:D].rearrange("p (h d) -> p h d", h=H0),
                                          bv0[0:KT, :].rearrange("p (h d) -> p h d", h=H0), ALU.add)\
                           .then_inc(b_taken, 1)

                def spread(i, u):
                    if nkt == 1:
                        dve.wait_ge(a_taken, i * (2 * AT) + (u + 1) * AT)
                        spread_keys(dve, u, 0)

                def first():
                    take_q(0, 0)
                    take_v(0, 0)
                    spread(0, 0)
                    take_q(0, 1)
                    spread(0, 1)

                def body(i, last_pair):
                    def mask(g, h):
                        if h is None and g % per == 0:
                            dve.wait_ge(mask_ready, 2 * i + g // per + 1)
                        return MB[g // per][:, 0:keys]

                    def after(g):
                        if g % per == per - 1:
                            b = 2 * i + g // per
                            dve.wait_ge(y_full, b + 1)
                            xb = X[:, bass.ds(b, 1), :].rearrange("p o d -> p (o d)")
                            dve.scalar_tensor_tensor(xb, ps[3][0:T, 0:D], tanh_gates[:, 0:1], xb,
                                                     ALU.mult, ALU.add).then_inc(y_taken, 1)

                    def beside(g):
                        if g == 0:
                            take_v(i, 1)
                            layer_norm(dve, (i + 1) & (PAIRS - 1), i + 1,
                                       lambda: dve.wait_ge(a_full, i * (2 * AT) + AT + 1))
                        if last_pair:
                            return
                        if g == tiles - 3:
                            take_q(i + 1, 0)
                        if g == tiles - 1:
                            take_v(i + 1, 0)
                            spread(i + 1, 0)
                            take_q(i + 1, 1)
                            spread(i + 1, 1)

                    att.vector(dve, i, mask, after, beside)

                over_pairs(dve, first, body)

            def gpsimd(pool):
                def spread(i, u):
                    pool.wait_ge(a_taken, i * (2 * AT) + (u + 1) * AT)
                    if nkt == 1:
                        spread_keys(pool, u, 1)

                def first():
                    spread(0, 0)
                    spread(0, 1)

                def body(i, last_pair):
                    def before(g):
                        if nkt == 1:
                            return
                        u, head = g // per, g % per
                        if head == 0:
                            pool.wait_ge(b_taken, i * (2 * BT) + u * BT + 1)
                        pool.wait_ge(att.scores_taken[g % 2], i * (tiles // 2) + g // 2)
                        pool.tensor_tensor(QBD[g % 2][:, :], QT0[u][:, head // 8, :],
                                           const("headmask")[:, head % 8:head % 8 + 1].to_broadcast([128, T]), ALU.mult)\
                            .then_inc(qbd_ready, 1)

                    def beside(g):
                        if g == 0:
                            layer_norm_root(pool, i + 1)
                        if g == tiles - 1 and not last_pair:
                            spread(i + 1, 0)
                            spread(i + 1, 1)

                    att.gpsimd(pool, i, before, beside)

                over_pairs(pool, first, body)

            return sync, tensor, scalar, vector, gpsimd

        m_a_full, m_a_taken = sem("m_a_full"), sem("m_a_taken")
        m_logit_full, m_logit_taken = sem("m_logit_full"), sem("m_logit_taken")
        m_neg_max, m_exp = sem("m_neg_max"), sem("m_exp")
        m_gates = sem("m_gates")
        m_gt_full, m_gt_taken = sem("m_gt_full"), sem("m_gt_taken")
        m_bias_full = sem("m_bias_full")
        m_expert_full = sem("m_expert_full")
        m_expert_taken = [sem(f"m_expert_taken{q}") for q in range(4)]
        m_step = sem("m_step")

        def experts_tensor(pe):
            pe.wait_ge(weights_moe_in, 16 * 4)

            def make_logits(i, u):
                b = 2 * i + u
                pe.wait_ge(m_a_taken, b)
                transpose_xn(pe, b, 2 * PAIRS + b, u, ps[0], m_a_full)
                pe.wait_ge(m_a_taken, b + 1)
                pe.wait_ge(m_logit_taken, b)
                for c in range(DC):
                    pe.matmul(ps[1][0:T, 0:NE], XT[u][:, c, :], wg0[:, c, :], start=(c == 0), stop=False)
                pe.matmul(ps[1][0:T, 0:NE], const("ones")[0:1, 0:T], bg0[:, :], start=False, stop=True)\
                  .then_inc(m_logit_full, 1)

            def make_experts(i, u):
                b = 2 * i + u
                for q in range(4):
                    pe.wait_ge(m_expert_taken[q], b)
                    for c in range(DC):
                        last = pe.matmul(ps[2 + q][0:T, :], XT[u][:, c, :], we0[:, c, q * 512:(q + 1) * 512],
                                         start=(c == 0), stop=(c == DC - 1))
                    last.then_inc(m_expert_full, 1)
                    if q == 0:
                        pe.wait_ge(m_gates, b + 1)
                        pe.wait_ge(m_gt_taken, b)
                        pe.transpose(ps[6][0:NE, 0:T], G[u][:, :], ident[0:T, 0:T]).then_inc(m_gt_full, 1)
                pe.wait_ge(m_gt_taken, b + 1)
                pe.wait_ge(x_updated, B + b)
                pe.matmul(ps[7][0:T, 0:D], GT[u][:, :], be0[:, :], start=True, stop=True).then_inc(m_bias_full, 1)

            def body(i, last_pair):
                for u in range(2):
                    make_experts(i, u)
                    if not last_pair:
                        make_logits(i + 1, u)

            over_pairs(pe, lambda: (make_logits(0, 0), make_logits(0, 1)), body)

        def experts_scalar(act):
            def route(i, u):
                b = 2 * i + u
                act.wait_ge(m_a_full, b + 1)
                act.activation(XT[u][:, :, :].rearrange("p c t -> p (c t)"), ps[0][:, 0:DC * T], ACT.Copy)\
                   .then_inc(m_a_taken, 1)
                act.wait_ge(m_neg_max, b + 1)
                act.activation(router[:, 1, :], logit[:, :], ACT.Exp, bias=router[:, 0, 0:1],
                               accum_out=router[:, 0, 1:2]).then_inc(m_exp, 1)

            def body(i, last_pair):
                for u in range(2):
                    b = 2 * i + u
                    act.wait_ge(m_gt_full, b + 1)
                    act.activation(GT[u][:, :], ps[6][0:NE, 0:T], ACT.Copy).then_inc(m_gt_taken, 1)
                    if not last_pair:
                        route(i + 1, u)

            over_pairs(act, lambda: (route(0, 0), route(0, 1)), body)

        def experts_vector(dve):
            dve.wait_ge(consts_in, 16)

            def gate(i, u, chain):
                b = 2 * i + u
                dve.wait_ge(m_logit_full, b + 1)
                dve.tensor_copy(logit[:, :], ps[1][0:T, 0:NE]).then_inc(m_logit_taken, 1)
                dve.wait_ge(m_logit_taken, b + 1)
                dve.tensor_reduce(router[:, 0, 0:1], logit[:, :], AX_X, ALU.max, negate=True).then_inc(m_neg_max, 1)
                dve.wait_ge(m_exp, b + 1)
                chain(dve.reciprocal(router[:, 0, 2:3], router[:, 0, 1:2]))
                chain(dve.tensor_scalar(router[:, 2, :], router[:, 1, :], router[:, 0, 2:3], None, ALU.mult), carry=True)
                chain(dve.max(router[:, 3, :], router[:, 2, :]), carry=True)
                chain(dve.max_index(router_i[:, :], router[:, 3, :], router[:, 2, :]))
                chain(dve.tensor_copy(router[:, 4, :], router_i[:, :]))
                for j in range(2):
                    chain(dve.tensor_scalar(router[:, 5 + j, :], const("iota8", T), router[:, 4, j:j + 1],
                                            router[:, 3, j:j + 1], ALU.is_equal, ALU.mult))
                dve.tensor_tensor(G[u][:, :], router[:, 5, :], router[:, 6, :], ALU.add).then_inc(m_gates, 1)
                dve.wait_ge(m_gates, b + 1)

            def weigh(i, u, chain):
                b = 2 * i + u
                for e in range(NE):
                    p = ps[2 + e // 2][0:T, (e % 2) * D:(e % 2 + 1) * D]
                    if e % 2 == 0:
                        dve.wait_ge(m_expert_full, 4 * b + e // 2 + 1)
                    if e == 0:
                        ins = dve.tensor_scalar(Y[:, :], p, G[u][:, e:e + 1], None, ALU.mult)
                    else:
                        ins = dve.scalar_tensor_tensor(Y[:, :], p, G[u][:, e:e + 1], Y[:, :], ALU.mult, ALU.add)
                    if e % 2 == 1:
                        ins.then_inc(m_expert_taken[e // 2], 1)
                        dve.wait_ge(m_expert_taken[e // 2], b + 1)
                    else:
                        chain(ins)
                dve.wait_ge(m_bias_full, b + 1)
                chain(dve.tensor_tensor(Y[:, :], Y[:, :], ps[7][0:T, 0:D], ALU.add))
                xb = X[:, bass.ds(b, 1), :].rearrange("p o d -> p (o d)")
                dve.scalar_tensor_tensor(xb, Y[:, :], tanh_gates[:, 2:3], xb, ALU.mult, ALU.add)\
                   .then_inc(x_updated, 1)
                dve.wait_ge(x_updated, B + b + 1)

            gating, weighing = 7, 5

            def first():
                chain = Chain(dve, m_step, 0, 2 * gating, scratch[:, :])
                gate(0, 0, chain)
                gate(0, 1, chain)
                chain.end()

            def body(i, last_pair):
                chain = Chain(dve, m_step, i, 2 * (gating + weighing), scratch[:, :], before=2 * gating)
                layer_norm(dve, (i + 1) & (PAIRS - 1), PAIRS + i + 1, lambda: dve.wait_ge(m_a_full, 2 * i + 2))
                for u in range(2):
                    weigh(i, u, chain)
                    if not last_pair:
                        gate(i + 1, u, chain)
                if not last_pair:
                    chain.end()

            over_pairs(dve, first, body)

        def experts_gpsimd(pool):
            layer_norm_root(pool, PAIRS + 1)
            pool.wait_ge(x_updated, B)
            prepare_steps(pool)
            with pool.Fori(1, PAIRS) as i:
                layer_norm_root(pool, PAIRS + i + 1)

        c_ctx_used = sem("c_ctx_used")
        c_a_full, c_a_taken = sem("c_a_full"), sem("c_a_taken")
        c_f_full, c_f_taken = sem("c_f_full"), sem("c_f_taken")
        c_t_full = sem("c_t_full")
        c_t_taken = [sem(f"c_t_taken{e}") for e in range(DC)]
        c_kept = sem("c_kept")
        c_padded = sem("c_padded")
        c_penalty = sem("c_penalty")
        c_added_v, c_added_p = sem("c_added_v"), sem("c_added_p")
        c_tanh = sem("c_tanh")
        c_dotted = sem("c_dotted")
        c_r_taken = [sem(f"c_r_taken{v}") for v in range(2)]
        c_rT_full = sem("c_rT_full")
        c_rho = sem("c_rho")
        c_neg_max, c_exp, c_shares, c_ws = sem("c_neg_max"), sem("c_exp"), sem("c_shares"), sem("c_ws")
        c_wb_taken = [sem(f"c_wb_taken{u}") for u in range(2)]
        c_step = sem("c_step")
        c_y = sem("c_y")
        c_shared = sem("c_shared")
        reps_ready = sem("reps_ready")
        live_found = sem("live_found")
        spans_found = sem("spans_found")
        prepared = sem("prepared")
        steps_set = sem("steps_set")

        free = bufs["score_sb"][0:1, :, :].rearrange("p r k -> p (r k)")

        def find_live_pairs(dve):
            dve.wait_ge(qmask_row_in, 16)
            padded = free[:, 0:DC * TCP].rearrange("p (b k) -> p b k", b=DC)
            link(dve, dve.memset(padded, 0.0))
            for part in range(B // DC):
                link(dve, dve.tensor_copy(padded[:, :, FRONT:TCP], qmask_row[:, DC * part:DC * (part + 1), :]))
                link(dve, dve.tensor_reduce(live[:, 0, DC * part:DC * (part + 1), :],
                                            padded.rearrange("p b (c k) -> p b c k", k=2 * CH), AX_X, ALU.max,
                                            apply_absolute_value=True))
            dve.tensor_scalar(live[:, 1, :, :], live[:, 0, :, :], 0.0, None, ALU.is_gt).then_inc(live_found, 1)
            dve.wait_ge(live_found, 1)

        def find_spans(dve):
            key = const("keyidx", 1)[:, 0:NCH]
            row = lambda ap: ap.unsqueeze(1).to_broadcast([1, B, NCH])
            link(dve, dve.tensor_scalar(live[:, 2, 0, :], key, -1.0, float(NCH), ALU.mult, ALU.add))
            link(dve, dve.tensor_scalar(live[:, 2, 1, :], key, 1.0, None, ALU.add))
            for n in range(2):
                link(dve, dve.tensor_tensor(live[:, 3, :, :], live[:, 1, :, :], row(live[:, 2, n, :]), ALU.mult))
                ins = dve.tensor_reduce(span[:, n, :], live[:, 3, :, :], AX_X, ALU.max)
                if n == 0:
                    link(dve, ins)
            ins.then_inc(spans_found, 1)
            dve.wait_ge(spans_found, 1)

        def prepare_steps(pool):
            index = const("keyidx", 1)
            chain = Chain(pool, prepared, 0, 0)
            pool.wait_ge(spans_found, 1)
            chain(pool.tensor_scalar(span[:, 2, :], span[:, 0, :], -1.0, float(NCH), ALU.mult, ALU.add))
            chain(pool.tensor_tensor(span[:, 3, :], span[:, 1, :], span[:, 2, :], ALU.subtract))
            chain(pool.tensor_scalar(span[:, 3, :], span[:, 3, :], 0.0, None, ALU.max))
            chain(pool.tensor_copy(span[:, 5, 0:1], span[:, 3, 0:1]))
            for b in range(1, B):
                chain(pool.tensor_tensor(span[:, 5, b:b + 1], span[:, 5, b - 1:b], span[:, 3, b:b + 1], ALU.add))
            chain(pool.tensor_tensor(span[:, 4, :], span[:, 5, :], span[:, 3, :], ALU.subtract))
            chain(pool.tensor_tensor(span[:, 0, :], span[:, 2, :], span[:, 4, :], ALU.subtract))
            chain(pool.tensor_scalar(span[:, 0, :], span[:, 0, :], 2.0 * CH, None, ALU.mult))
            chain(pool.tensor_scalar(span[:, 1, :], index[:, 0:B], float(PACK), None, ALU.mult))
            chain(pool.tensor_tensor(span[:, 6, :], span[:, 0, :], span[:, 1, :], ALU.add))
            chain(pool.tensor_copy(span[:, 7, 0:1], span[:, 6, 0:1]))
            chain(pool.tensor_tensor(span[:, 7, 1:B], span[:, 6, 1:B], span[:, 6, 0:B - 1], ALU.subtract))
            started = free[:, 0:B * NPAIRS].rearrange("p (b s) -> p b s", b=B)
            chain(pool.tensor_tensor(started, index[:, 1:NPAIRS + 1].unsqueeze(1).to_broadcast([1, B, NPAIRS]),
                                     span[:, 4, :].unsqueeze(2).to_broadcast([1, B, NPAIRS]), ALU.subtract))
            chain(pool.tensor_scalar(started, started, 0.0, 1.0, ALU.max, ALU.min))
            chain(pool.tensor_tensor(started, started, span[:, 7, :].unsqueeze(2).to_broadcast([1, B, NPAIRS]),
                                     ALU.mult))
            n = B // 2
            while n > 0:
                chain(pool.tensor_tensor(started[:, 0:n, :], started[:, 0:n, :], started[:, n:2 * n, :], ALU.add))
                n //= 2
            total = free[:, B * NPAIRS:(B + 1) * NPAIRS]
            chain(pool.tensor_scalar(total, index[:, 0:NPAIRS], 2.0 * CH, None, ALU.mult))
            chain(pool.tensor_tensor(total, total, started[:, 0, :], ALU.add))
            chain(pool.tensor_copy(steps_of[:, :], total))
            chain(pool.tensor_copy(pairs_of[:, 0:1], span[:, 5, B - 1:B]))
            chain(pool.tensor_scalar(total[:, 0:1], span[:, 5, B - 1:B], -1.0, 0.0, ALU.add, ALU.max))
            pool.tensor_copy(pairs_of[:, 1:2], total[:, 0:1]).then_inc(steps_set, 1)
            pool.wait_ge(weights_c_in, 16 * 6)
            for e in range(DC):
                pool.tensor_copy(w1_rep[:, e, :], w1_col[:, e:e + 1].to_broadcast([128, 32])).then_inc(reps_ready, 1)
                for k in range(2):
                    pool.tensor_copy(wcwb_rep[:, k, e, :], wcwb_col[:, k, e:e + 1].to_broadcast([128, T]))\
                        .then_inc(reps_ready, 1)

        def steps_loop(eng, pair, last=None):
            pairs = eng.value_load(pairs_of[0:1, 0:1], min_val=0, max_val=NPAIRS)
            with eng.If(pairs > 0):
                pair(0, True)
            with eng.Fori(0, NPAIRS // (RUN * SEG)) as r:
                with eng.If(pairs > r * (RUN * SEG) + 1):
                    with eng.Fori(0, RUN) as g:
                        with eng.If(pairs > r * (RUN * SEG) + g * SEG + 1):
                            with eng.Fori(0, SEG) as k:
                                j = r * (RUN * SEG) + g * SEG + k + 1
                                with eng.If(pairs > j):
                                    pair(j.with_bounds(min_val=1, max_val=NPAIRS - 1), False)
            if last is not None:
                final = eng.value_load(pairs_of[0:1, 1:2], min_val=0, max_val=NPAIRS - 1)
                with eng.If(pairs > 0):
                    last(final + 1)

        def pair_at(eng, j):
            entry = eng.value_load(steps_of[0:1, bass.ds(j, 1)], min_val=0, max_val=B * PACK - 1)
            batch = entry >> PACK.bit_length() - 1
            row = entry & (PACK - 1)
            return ((row + batch * TCP).with_bounds(min_val=0, max_val=B * TCP - 2 * CH),
                    (batch * T).with_bounds(min_val=0, max_val=(B - 1) * T))

        def additive_sync(sp):
            sp.wait_ge(x_updated, B)
            for u in range(2):
                sp.dma_start(CT[u][:, :, :], a["ctxT"][:, :, u * TC:(u + 1) * TC]).then_inc(ctx_in[u], 16)
            with sp.Fori(1, PAIRS) as i:
                for u in range(2):
                    sp.wait_ge(c_t_full, 4 * (i - 1) + 2 * u + 2)
                    sp.dma_start(CT[u][:, :, :], a["ctxT"][:, :, bass.ds((2 * i + u) * TC, TC)]).then_inc(ctx_in[u], 16)
            for u in range(2):
                sp.wait_ge(c_t_full, 4 * (PAIRS - 1) + 2 * u + 2)
                sp.dma_start(CT[u][:, :, :], a["ctxT"][:, :, u * TC:(u + 1) * TC]).then_inc(ctx_in[u], 16)
            with sp.Fori(1, PAIRS) as i:
                for u in range(2):
                    sp.wait_ge(c_ctx_used, 2 * (i - 1) + u + 1)
                    sp.dma_start(CT[u][:, :, :], a["ctxT"][:, :, bass.ds((2 * i + u) * TC, TC)]).then_inc(ctx_in[u], 16)

        def additive_tensor(pe):
            pe.wait_ge(weights_c_in, 16 * 6)
            for q in range(4):
                pe.wait_ge(m_expert_taken[q], B)
            with pe.Fori(0, PAIRS) as i:
                for u in range(2):
                    b = 2 * i + u
                    pe.wait_ge(c_a_taken, b)
                    transpose_xn(pe, b, 4 * PAIRS + b, u, ps[0], c_a_full)
                for u in range(2):
                    b = 2 * i + u
                    pe.wait_ge(c_a_taken, b + 1)
                    pe.wait_ge(c_f_taken, b)
                    for e in range(DC):
                        for c in range(DC):
                            last = pe.matmul(ps[1][:, e * T:(e + 1) * T], wf1[:, c, e * 128:(e + 1) * 128],
                                             XT[u][:, c, :], start=(c == 0), stop=(c == DC - 1))
                    last.then_inc(c_f_full, 1)
                    pe.wait_ge(ctx_in[u], 16 * (PAIRS + i + 1))
                    for e in range(DC):
                        pe.wait_ge(c_t_taken[e], b)
                        for c in range(DC):
                            last = pe.matmul(ps[2 + e][:, 0:TC], ws1[:, c, e * 128:(e + 1) * 128], CT[u][:, c, :],
                                             start=(c == 0), stop=(c == DC - 1))
                        last.then_inc(c_t_full, 1)
            pe.wait_ge(reps_ready, 3 * DC)
            pe.wait_ge(steps_set, 1)

            def back(j, v):
                pe.wait_ge(c_r_taken[v], j)
                pe.wait_ge(c_rho, 2 * j + v - 1)
                for k in range(4):
                    last = pe.transpose(ps[6 + v][0:T, k * 128:(k + 1) * 128], R[v][:, k * T:(k + 1) * T], ident)
                last.then_inc(c_rT_full, 1)

            def pair(j, first):
                for v in range(2):
                    for e in range(DC):
                        if not first and v == 0:
                            back(j, e)
                        pe.wait_ge(c_tanh, 4 * j + 2 * v + e + 1)
                        for q in range(4):
                            last = pe.matmul(ps[4 + v][32 * q:32 * q + 32, 0:4 * T], w1_rep[:, e, :],
                                             H[v][:, e, 4 * q:4 * q + 4, :].rearrange("p k t -> p (k t)"),
                                             start=(e == 0), stop=(e == DC - 1))
                        last.then_inc(c_dotted, 1)

            steps_loop(pe, pair, lambda pairs: (back(pairs, 0), back(pairs, 1)))
            pe.wait_ge(c_f_taken, B)
            for e in range(DC):
                pe.wait_ge(c_t_taken[e], B)
            with pe.Fori(0, PAIRS) as i:
                for u in range(2):
                    pe.wait_ge(ctx_in[u], 16 * (2 * PAIRS + 1 + i))
                    pe.wait_ge(c_wb_taken[u], i)
                    for k in range(2):
                        for c in range(DC):
                            last = pe.matmul(ps[2 * u + k][0:T, 0:TC], wcwb_rep[:, k, c, :], CT[u][:, c, :],
                                             start=(c == 0), stop=(c == DC - 1))
                    last.then_inc(c_ctx_used, 1)

        def additive_scalar(act):
            act.wait_ge(c_padded, 3)
            act.wait_ge(steps_set, 1)
            with act.Fori(0, PAIRS) as i:
                for u in range(2):
                    b = 2 * i + u
                    act.wait_ge(c_a_full, b + 1)
                    act.activation(XT[u][:, :, :].rearrange("p c t -> p (c t)"), ps[0][:, 0:DC * T], ACT.Copy)\
                       .then_inc(c_a_taken, 1)
                for u in range(2):
                    b = 2 * i + u
                    for e in range(DC):
                        act.wait_ge(c_t_full, 2 * b + 1 + e)
                        act.activation(TT[:, e, bass.ds(b * TCP + FRONT, TC)], ps[2 + e][:, 0:TC], ACT.Copy)\
                           .then_inc(c_t_taken[e], 1)

            def take(j):
                act.wait_ge(c_dotted, 4 * j - 2)
                act.activation(R[0][:, :], ps[4][:, 0:4 * T], ACT.Copy).then_inc(c_r_taken[0], 1)

            def pair(j, first):
                if not first:
                    take(j)
                for v in range(2):
                    for e in range(DC):
                        act.wait_ge(c_added_v, 4 * j + 2 * v + e + 1)
                        act.wait_ge(c_added_p, 4 * j + 2 * v + e + 1)
                        h = H[v][:, e, :, :].rearrange("p k t -> p (k t)")
                        act.activation(h, h, ACT.Tanh).then_inc(c_tanh, 1)

            steps_loop(act, pair, take)
            act.wait_ge(c_neg_max, 1)
            with act.Fori(0, PAIRS) as i:
                for u in range(2):
                    b = 2 * i + u
                    act.wait_ge(c_wb_taken[u], i)
                    act.activation(E[u][:, :], RHO[:, bass.ds(b * TCP + FRONT, TC)], ACT.Exp, bias=soft[:, 0, bass.ds(b, 1)],
                                   accum_out=soft[:, 1, bass.ds(b, 1)]).then_inc(c_exp, 1)
            act.wait_ge(c_shares, 1)
            for k in range(2):
                act.activation(soft[:, 5 + k, :], soft[:, 3 + k, :], ACT.Tanh, bias=bcwb[:, k:k + 1]).then_inc(c_ws, 1)

        def add_halves(eng, j, first, lo, n, done, between=nothing):
            at, features = pair_at(eng, j)
            for v in range(2):
                if v == 1:
                    between()
                for e in range(DC):
                    if not first:
                        eng.wait_ge(c_dotted, 4 * j + 2 * v + e - 3)
                    t = TT[:, e, bass.ds(at + v * CH + lo, n)].unsqueeze(2).to_broadcast([128, n, T])
                    f = FT[:, e, bass.ds(features, T)].unsqueeze(1).to_broadcast([128, n, T])
                    eng.tensor_tensor(H[v][:, e, lo:lo + n, :], t, f, ALU.add).then_inc(done, 1)

        def additive_vector(dve):
            dve.wait_ge(c_padded, 3)
            dve.wait_ge(qmask_in, 16)

            def project(i, end):
                for u in range(2):
                    b = 2 * i + u
                    dve.tensor_scalar(RHO[:, bass.ds(b * TCP + FRONT, TC)],
                                      qmask_i[:, bass.ds(b, 1), :].rearrange("p o k -> p (o k)"),
                                      -MASKED, MASKED, ALU.mult, ALU.add).then_inc(c_penalty, 1)
                if not end:
                    layer_norm(dve, i + 1, 2 * PAIRS + i + 1,
                               lambda: (dve.wait_ge(c_a_full, 2 * i + 2), dve.wait_ge(c_kept, 2 * i + 2)))
                for u in range(2):
                    b = 2 * i + u
                    dve.wait_ge(c_f_full, b + 1)
                    for e in range(DC):
                        last = dve.tensor_scalar(FT[:, e, bass.ds(b * T, T)], ps[1][:, e * T:(e + 1) * T], bf1[:, e:e + 1],
                                                 None, ALU.add)
                    last.then_inc(c_f_taken, 1)

            with dve.Fori(0, PAIRS - 1) as i:
                project(i, False)
            project(PAIRS - 1, True)
            dve.wait_ge(c_f_taken, B)
            dve.wait_ge(c_penalty, B)
            for e in range(DC):
                dve.wait_ge(c_t_taken[e], B)

            dve.memset(scratch[:, :], 0.0).then_inc(c_rho, 2)

            def keep(j):
                at, _ = pair_at(dve, j - 1)
                for v in range(2):
                    r = RHO[:, bass.ds(at + v * CH, CH)].rearrange("p (q k) -> p k q", q=4)
                    dve.wait_ge(c_rT_full, 2 * j + v - 1)
                    dve.tensor_tensor(r, ps[6 + v][0:T, :].rearrange("p (k q r) -> p k q r", k=4, q=4)[:, :, :, 0],
                                      r, ALU.add).then_inc(c_rho, 1)

            def take(j):
                dve.wait_ge(c_dotted, 4 * j)
                dve.tensor_copy(R[1][:, :], ps[5][:, 0:4 * T]).then_inc(c_r_taken[1], 1)

            def pair(j, first):
                add_halves(dve, j, first, 0, CH - POOL_ROWS, c_added_v, nothing if first else (lambda: take(j)))
                if not first:
                    keep(j)

            steps_loop(dve, pair, lambda pairs: (take(pairs), keep(pairs)))
            pairs = dve.value_load(pairs_of[0:1, 0:1], min_val=0, max_val=NPAIRS)
            dve.wait_ge(c_rho, 2 * pairs + 2)
            rho = RHO[:, :].rearrange("p (b k) -> p b k", b=B)[:, :, FRONT:TCP]
            dve.tensor_reduce(soft[:, 0, :], rho, AX_X, ALU.max, negate=True).then_inc(c_neg_max, 1)
            with dve.Fori(0, PAIRS) as i:
                for u in range(2):
                    b = 2 * i + u
                    dve.wait_ge(c_exp, b + 1)
                    dve.wait_ge(c_ctx_used, b + 1)
                    for k in range(2):
                        last = dve.tensor_tensor_reduce(weighed[u][:, k, :], E[u][:, :], ps[2 * u + k][0:T, 0:TC],
                                                        1.0, 0.0, ALU.mult, ALU.add, share[:, u, k:k + 1])
                    last.then_inc(c_wb_taken[u], 1)
                for u in range(2):
                    dve.wait_ge(c_wb_taken[u], i + 1)
                dve.tensor_copy(soft[:, 3:5, bass.ds(2 * i, 2)].rearrange("p k u -> p u k"), share[:, :, :])                   .then_inc(c_shared, 1)
                dve.wait_ge(c_shared, i + 1)
            chain = Chain(dve, c_step, 0, 1)
            chain(dve.reciprocal(soft[:, 2, :], soft[:, 1, :]))
            dve.tensor_tensor(soft[:, 3:5, :], soft[:, 3:5, :], soft[:, 2:3, :].to_broadcast([T, 2, B]), ALU.mult)\
               .then_inc(c_shares, 1)
            dve.wait_ge(c_ws, 2)

            def update(i):
                for u in range(2):
                    b = 2 * i + u
                    dve.tensor_scalar(W[u][:, :], XNA[:, bass.ds(b, 1), :].rearrange("p o d -> p (o d)"),
                                      soft[:, 5, bass.ds(b, 1)], soft[:, 6, bass.ds(b, 1)], ALU.mult, ALU.add)\
                       .then_inc(c_y, 1)
                for u in range(2):
                    b = 2 * i + u
                    dve.wait_ge(c_y, b + 1)
                    xb = X[:, bass.ds(b, 1), :].rearrange("p o d -> p (o d)")
                    dve.scalar_tensor_tensor(xb, W[u][:, :], tanh_gates[:, 1:2], xb, ALU.mult, ALU.add)\
                       .then_inc(x_updated, 1)
                dve.wait_ge(x_updated, 2 * B + 2 * i + 2)

            dve.wait_ge(c_kept, B)
            update(0)
            layer_norm(dve, 0, 3 * PAIRS, lambda: dve.wait_ge(c_a_full, B))
            with dve.Fori(1, PAIRS) as i:
                update(i)

        def additive_gpsimd(pool):
            pool.wait_ge(x_updated, B)
            for tile, pieces in ((RHO, [RHO[:, :]]), (TT, [TT[:, e, :] for e in range(DC)])):
                for piece in pieces:
                    pool.memset(piece, 0.0).then_inc(c_padded, 1)

            def keep_xn(i):
                for u in range(2):
                    b = 2 * i + u
                    pool.wait_ge(xn_ready, 4 * PAIRS + b + 1)
                    pool.tensor_copy(XNA[:, bass.ds(b, 1), :].rearrange("p o d -> p (o d)"), XN[u][:, :]).then_inc(c_kept, 1)

            with pool.Fori(0, PAIRS - 1) as i:
                keep_xn(i)
                layer_norm_root(pool, 2 * PAIRS + i + 1)
            keep_xn(PAIRS - 1)
            pool.wait_ge(c_f_taken, B)
            for e in range(DC):
                pool.wait_ge(c_t_taken[e], B)
            steps_loop(pool, lambda j, first: add_halves(pool, j, first, CH - POOL_ROWS, POOL_ROWS, c_added_p))
            layer_norm_root(pool, 3 * PAIRS)

        d_v_full, d_v_taken = sem("d_v_full"), sem("d_v_taken")
        o_step = sem("o_step")
        o_picked = sem("o_picked")
        o_bd = sem("o_bd")

        def pick_tokens(dve):
            chain = Chain(dve, o_step, 0, 0, scratch[:, :])
            dve.wait_ge(d_v_taken, 2 * B)
            dve.memset(scratch[:, :], 0.0)
            def each(step):
                for b in range(B):
                    last = step(b)
                chain(last)
            each(lambda b: dve.max(top[:, b, 0:8], SC[:, b, :]))
            each(lambda b: dve.match_replace(rest[:, b, :], top[:, b, 0:8], SC[:, b, :], LOWEST))
            each(lambda b: dve.max(top[:, b, 8:16], rest[:, b, :]))
            each(lambda b: dve.max_index(top_i[:, b, 0:8], top[:, b, 0:8], SC[:, b, :]))
            each(lambda b: dve.max_index(top_i[:, b, 8:16], top[:, b, 8:16], rest[:, b, :]))
            dve.tensor_copy(IDX[:, :, :], top_i[:, :, 0:KSEL]).then_inc(o_picked, 1)
            dve.tensor_copy(VAL[:, :, :], top[:, :, 0:KSEL]).then_inc(o_picked, 1)
            dve.wait_ge(o_picked, 2)
            idx = IDX[:, :, :].rearrange("n b j -> n (b j)").unsqueeze(1).to_broadcast([NH, NH, T])
            diag = ident[0:NH, 0:NH].unsqueeze(2).to_broadcast([NH, NH, T])
            dve.tensor_tensor(BD[:, :, :], idx, diag, ALU.mult).then_inc(o_bd, 1)

        PER1 = 2
        dense = Attention(sem, "d", att_bufs, 2 * PER1, 4, T, T)
        d_a_full, d_a_taken = sem("d_a_full"), sem("d_a_taken")
        d_q_full, d_q_taken = sem("d_q_full"), sem("d_q_taken")
        d_o_taken = sem("d_o_taken")
        d_rope_step, d_roped = sem("d_rope_step"), sem("d_roped")
        d_kept = sem("d_kept")
        d_zeroed = sem("d_zeroed")
        d_y_full = sem("d_y_full")

        def rotate(eng, qk, cos, sin, step, base, done):
            h = ROT // 2
            ins = eng.tensor_tensor(RA[:, :, :, :], qk[:, :, :, 0:ROT], cos, ALU.mult)
            ins.then_inc(step, 1)
            for r in range(2):
                eng.tensor_tensor(RB[:, :, :, r * h:(r + 1) * h], qk[:, :, :, (1 - r) * h:(2 - r) * h],
                                  sin[:, :, :, r * h:(r + 1) * h], ALU.mult).then_inc(step, 1)
            eng.wait_ge(step, base + 3)
            eng.tensor_tensor(qk[:, :, :, 0:ROT], RA[:, :, :, :], RB[:, :, :, :], ALU.add).then_inc(done, 1)

        def transpose_qk(pe, qk, full, taken, at):
            for k in range(2):
                pe.wait_ge(taken, at + k)
                for q in range(4):
                    last = pe.transpose(ps[0][:, q * T:(q + 1) * T],
                                        qk[:, k, 2 * q:2 * q + 2, :].rearrange("p h d -> p (h d)"), ident[0:T, 0:T])
                last.then_inc(full, 1)

        def take_qk(act, qt, kbd, full, taken, at):
            act.wait_ge(full, at + 1)
            act.activation(qt[:, :, :].rearrange("p q t -> p (q t)"), ps[0][:, 0:4 * T], ACT.Copy, scale=HP ** -0.5)\
               .then_inc(taken, 1)
            act.wait_ge(full, at + 2)
            for k in range(2):
                last = act.activation(kbd[64 * k:64 * k + 64, :, k * T:(k + 1) * T],
                                      ps[0][64 * k:64 * k + 64, 0:4 * T].rearrange("p (q t) -> p q t", q=4), ACT.Copy)
            last.then_inc(taken, 1)

        def pair_scores(pe, bank, qt, kbd, first, n):
            for k in range(n):
                last = pe.matmul(bank[0:T, k * 2 * T:(k + 1) * 2 * T], qt[:, first + k, :], kbd[:, first + k, :],
                                 start=True, stop=True)
            return last

        def pair_values(pe, v, probsT, first, n):
            for k in range(n):
                head = first + k
                r = 64 * (head % 2)
                last = pe.matmul(ps[3][r:r + 64, (head // 2) * T:(head // 2 + 1) * T], v[:, head * HP:(head + 1) * HP],
                                 probsT[0:T, k * T:(k + 1) * T], start=True, stop=True)
            return last

        def dense_tensor(pe):
            pe.wait_ge(weights_d_in, 16 * 5)
            for u in range(2):
                pe.wait_ge(c_wb_taken[u], PAIRS)

            def turn_xn(i, u):
                pe.wait_ge(d_a_taken, 8 * i + u)
                transpose_xn(pe, None, 6 * PAIRS + 2 * i + u, u, ps[0], d_a_full)

            def make_qk(i, u):
                pe.wait_ge(d_a_taken, 8 * i + u + 1)
                pe.wait_ge(d_q_taken, 2 * i + u)
                for k in range(2):
                    if k == 1:
                        pe.wait_ge(d_a_taken, 8 * i + 2 + u)
                    for c in range(DC):
                        last = pe.matmul(ps[1 - k][0:T, :], XT[u][:, c, :], wqkv1[:, c, k * 512:(k + 1) * 512],
                                         start=(c == 0), stop=(c == DC - 1))
                    last.then_inc((d_q_full, d_a_full)[k], 1)

            def make_v(i, u):
                b = 2 * i + u
                pe.wait_ge(d_v_taken, 2 * b)
                for c in range(DC):
                    last = pe.matmul(ps[2][0:T, :], XT[u][:, c, :], wqkv1[:, c, 1024:1536],
                                     start=(c == 0), stop=(c == DC - 1))
                last.then_inc(d_v_full, 1)
                pe.wait_ge(d_v_taken, 2 * b + 1)
                for c in range(DC):
                    last = pe.matmul(ps[2][0:NH, 0:T], wr1[:, c, :], XT[u][:, c, :], start=(c == 0), stop=(c == DC - 1))
                last.then_inc(d_v_full, 1)

            def turn_qk(i, u):
                pe.wait_ge(d_roped, 2 * i + u + 1)
                transpose_qk(pe, QK1[u], d_a_full, d_a_taken, 8 * i + 4 + 2 * u)

            def first():
                for u in range(2):
                    turn_xn(0, u)
                for u in range(2):
                    make_qk(0, u)
                    make_v(0, u)
                for u in range(2):
                    turn_qk(0, u)

            def body(i, last_pair):
                def beside(g):
                    if last_pair:
                        return
                    if g == 1:
                        turn_xn(i + 1, 0)
                        turn_xn(i + 1, 1)
                    if g == 2:
                        make_qk(i + 1, 0)
                    if g == 3:
                        pe.wait_ge(x_updated, 3 * B + 2 * i + 1)
                        make_v(i + 1, 0)
                        make_qk(i + 1, 1)

                def scores(g, bank):
                    u, j = g // PER1, g % PER1
                    if j == 0:
                        pe.wait_ge(d_a_taken, 8 * i + 6 + 2 * u)
                    return pair_scores(pe, bank, QT1[u], KBD1[u], 2 * j, 2)

                def values(g, probsT):
                    u, j = g // PER1, g % PER1
                    if j == 0:
                        pe.wait_ge(d_o_taken, 2 * i + u)
                    return pair_values(pe, V1[u], probsT, 4 * j, 4)

                def after(g):
                    u, j = g // PER1, g % PER1
                    if j == PER1 - 1:
                        b = 2 * i + u
                        pe.wait_ge(d_o_taken, b + 1)
                        if last_pair and u == 1:
                            bank = ps[0]
                            pe.wait_ge(d_a_taken, 8 * PAIRS)
                        else:
                            bank = ps[2]
                            pe.wait_ge(x_updated, 3 * B + b)
                            pe.wait_ge(d_v_taken, 4 * i + 4 + (0 if last_pair else 2 * u))
                        for q in range(4):
                            last = pe.matmul(bank[0:T, 0:D], O1[:, q * T:(q + 1) * T], wo1[:, q, :],
                                             start=(q == 0), stop=(q == 3))
                        last.then_inc(d_y_full, 1)

                dense.tensor(pe, i, scores, values, after, beside)
                if not last_pair:
                    turn_qk(i + 1, 0)
                    pe.wait_ge(x_updated, 3 * B + 2 * i + 2)
                    make_v(i + 1, 1)
                    turn_qk(i + 1, 1)

            over_pairs(pe, first, body)

        def dense_scalar(act):
            act.wait_ge(d_zeroed, 2)

            def take_xn(i, u):
                act.wait_ge(d_a_full, 8 * i + u + 1)
                act.activation(XT[u][:, :, :].rearrange("p c t -> p (c t)"), ps[0][:, 0:DC * T], ACT.Copy)\
                   .then_inc(d_a_taken, 1)

            def take_rows(i, u):
                act.wait_ge(d_q_full, 2 * i + u + 1)
                act.activation(QK1[u][:, 0, :, :].rearrange("p h d -> p (h d)"), ps[1][0:T, :], ACT.Copy)\
                   .then_inc(d_q_taken, 1)
                act.wait_ge(d_a_full, 8 * i + 3 + u)
                act.activation(QK1[u][:, 1, :, :].rearrange("p h d -> p (h d)"), ps[0][0:T, :], ACT.Copy)\
                   .then_inc(d_a_taken, 1)

            def take_columns(i, u):
                take_qk(act, QT1[u], KBD1[u], d_a_full, d_a_taken, 8 * i + 4 + 2 * u)

            def first():
                for step in (take_xn, take_rows, take_columns):
                    for u in range(2):
                        step(0, u)

            def body(i, last_pair):
                def beside(g):
                    if last_pair:
                        return
                    if g == 1:
                        take_xn(i + 1, 0)
                        take_xn(i + 1, 1)
                    if g > 1:
                        take_rows(i + 1, g - 2)

                def after(g):
                    if g % PER1 == PER1 - 1:
                        b = 2 * i + g // PER1
                        act.wait_ge(dense.values_done[g % 2], i * PER1 + g // 2 + 1)
                        act.wait_ge(d_y_full, b)
                        act.activation(O1[:, :], ps[3][:, 0:4 * T], ACT.Copy).then_inc(d_o_taken, 1)

                dense.scalar(act, i, after, beside)
                if not last_pair:
                    take_columns(i + 1, 0)
                    take_columns(i + 1, 1)

            over_pairs(act, first, body)

        def dense_vector(dve):
            cos = const("cos", T).unsqueeze(1).unsqueeze(1).to_broadcast([T, 2, NH, ROT])
            sin = const("sin", T).unsqueeze(1).unsqueeze(1).to_broadcast([T, 2, NH, ROT])
            def take_v(i, u):
                b = 2 * i + u
                dve.wait_ge(d_v_full, 2 * b + 1)
                dve.tensor_copy(V1[u][:, :], ps[2][0:T, :]).then_inc(d_v_taken, 1)
                dve.wait_ge(d_v_full, 2 * b + 2)
                dve.tensor_copy(SC[:, bass.ds(b, 1), :].rearrange("p o t -> p (o t)"), ps[2][0:NH, 0:T])\
                   .then_inc(d_v_taken, 1)

            def rope(i, u, very_first=False):
                if not very_first:
                    dve.wait_ge(d_roped, 2 * i + u)
                dve.wait_ge(d_q_taken, 2 * i + u + 1)
                dve.wait_ge(d_a_taken, 8 * i + 3 + u)
                rotate(dve, QK1[u][:, :, :, :], cos, sin, d_rope_step, 3 * (2 * i + u), d_roped)

            def first():
                take_v(0, 0)
                rope(0, 0, very_first=True)
                take_v(0, 1)
                rope(0, 1)

            def body(i, last_pair):
                def mask(g, h):
                    return const("causal", T)

                def update(u):
                    b = 2 * i + u
                    dve.wait_ge(d_y_full, b + 1)
                    y = ps[0 if last_pair and u == 1 else 2][0:T, 0:D]
                    xb = X[:, bass.ds(b, 1), :].rearrange("p o d -> p (o d)")
                    dve.scalar_tensor_tensor(xb, y, tanh_gates[:, 3:4], xb, ALU.mult, ALU.add).then_inc(x_updated, 1)

                def after(g):
                    if g % PER1 == PER1 - 1 and not last_pair:
                        update(g // PER1)

                def beside(g):
                    if last_pair:
                        return
                    if g == 0:
                        layer_norm(dve, i + 1, 3 * PAIRS + i + 1,
                                   lambda: (dve.wait_ge(d_a_full, 8 * i + 2), dve.wait_ge(d_kept, 2 * i + 2)))
                    if g == 3:
                        take_v(i + 1, 0)
                        rope(i + 1, 0)
                        rope(i + 1, 1)

                dense.vector(dve, i, mask, after, beside)
                if last_pair:
                    pick_tokens(dve)
                    update(0)
                    update(1)
                else:
                    take_v(i + 1, 1)

            over_pairs(dve, first, body)

        def dense_gpsimd(pool):
            pool.wait_ge(c_neg_max, 1)
            for u in range(2):
                pool.memset(KBD1[u][:, :, :], 0.0).then_inc(d_zeroed, 1)

            def keep_xn(i):
                for u in range(2):
                    pool.wait_ge(xn_ready, 6 * PAIRS + 2 * i + u + 1)
                    pool.tensor_copy(XNA[:, bass.ds(2 * i + u, 1), :].rearrange("p o d -> p (o d)"), XN[u][:, :])\
                        .then_inc(d_kept, 1)

            def first():
                keep_xn(0)

            def body(i, last_pair):
                def beside(g):
                    if g == 0 and not last_pair:
                        layer_norm_root(pool, 3 * PAIRS + i + 1)

                dense.gpsimd(pool, i, beside=beside)
                if not last_pair:
                    keep_xn(i + 1)

            over_pairs(pool, first, body)

        mosa = Attention(sem, "d", att_bufs, dense.tiles, NH // RING, T, T)
        assert mosa.tiles == RING
        o_cols_full = sem("o_cols_full")
        o_pos_full, o_pos_taken = sem("o_pos_full"), sem("o_pos_taken")
        o_onehot = sem("o_onehot")
        o_g_full, o_g_taken = sem("o_g_full"), sem("o_g_taken")
        o_cs_full, o_cs_taken = sem("o_cs_full"), sem("o_cs_taken")
        o_pn_full, o_pn_taken = sem("o_pn_full"), sem("o_pn_taken")
        o_qkv_full, o_qkv_taken = sem("o_qkv_full"), sem("o_qkv_taken")
        o_rope_step, o_roped = sem("o_rope_step"), sem("o_roped")
        o_a_full, o_a_taken = sem("o_a_full"), sem("o_a_taken")
        o_mask, o_halved, o_gate = sem("o_mask"), sem("o_halved"), sem("o_gate")
        o_o_taken = sem("o_o_taken")
        o_z_full, o_z_taken = sem("o_z_full"), sem("o_z_taken")
        o_z_out, o_z_in = [sem(f"o_z_out{part}") for part in range(2)], sem("o_z_in")
        o_row = sem("o_row")
        o_y_full = sem("o_y_full")
        z_rows = nc.dram_tensor("z_rows", (T, NH, D), F32, kind="Internal").ap()

        def mosa_sync(sp):
            by_head = z_rows.rearrange("(b j) n d -> n j b d", b=B)
            half = NH // 2
            for part in range(2):
                sp.wait_ge(o_z_taken, (part + 1) * half)
                sp.dma_start(z_rows[:, part * half:(part + 1) * half, :], Z[:, part * half:(part + 1) * half, :])\
                  .then_inc(o_z_out[part], 16)
            for part in range(2):
                sp.wait_ge(o_z_out[part], 16)
                for n in range(part * half, (part + 1) * half):
                    sp.dma_start(Z2[n * KSEL:(n + 1) * KSEL, :, :], by_head[n]).then_inc(o_z_in, 16)
            with sp.Fori(0, B) as b:
                sp.wait_ge(x_updated, 4 * B + b + 1)
                sp.dma_start(out[bass.ds(b, 1), :, :].rearrange("o t d -> t (o d)"),
                             X[:, bass.ds(b, 1), :].rearrange("p o d -> p (o d)")).then_inc(stored, 16)
            sp.wait_ge(stored, 16 * B)

        def mosa_tensor(pe):
            pe.wait_ge(o_picked, 2)
            pe.transpose(ps[1][0:T, 0:NH], IDX[:, :, :].rearrange("n b j -> n (b j)"), ident[0:NH, 0:NH])
            pe.transpose(ps[1][0:T, NH:2 * NH], VAL[:, :, :].rearrange("n b j -> n (b j)"), ident[0:NH, 0:NH])\
              .then_inc(o_cols_full, 1)
            pe.wait_ge(o_bd, 1)
            for k in range(2):
                pe.matmul(ps[4 + k][0:T, 0:4 * T], const("ones", NH)[:, 0:T],
                          BD[:, 4 * k:4 * k + 4, :].rearrange("p n r -> p (n r)"), start=True, stop=True)\
                  .then_inc(o_pos_full, 1)
            pe.wait_ge(o_onehot, 1)
            for n in range(NH):
                last = pe.matmul(ps[6][0:T, n * 2 * ROT:(n + 1) * 2 * ROT], OH[:, n, :, :].rearrange("p b j -> p (b j)"),
                                 consts[0:T, CONST["cos"][0]:CONST["sin"][1]], start=True, stop=True)
            last.then_inc(o_cs_full, 1)
            for turn in range(4):
                c, half = turn // 2, turn % 2
                if turn >= 2:
                    pe.wait_ge(o_g_taken, turn - 1)
                for b in range(4):
                    last = pe.matmul(ps[2 * (turn % 2)][:, b * T:(b + 1) * T], XNA[:, 4 * half + b, c * 128:(c + 1) * 128],
                                     OH[:, :, 4 * half + b, :], start=True, stop=True)
                last.then_inc(o_g_full, 1)
            pe.wait_ge(o_onehot, 2)
            for b in range(B):
                last = pe.matmul(ps[7][0:T, b:b + 1], OHB[:, b, :, :].rearrange("p n j -> p (n j)"), const("tokcol", T),
                                 start=True, stop=True)
            last.then_inc(o_pn_full, 1)
            pe.wait_ge(o_g_taken, 4)
            pe.wait_ge(o_pos_taken, 2)
            for turn in range(4):
                if turn >= 2:
                    pe.wait_ge(o_qkv_taken, turn - 1)
                for k in range(2):
                    n = 2 * turn + k
                    for c in range(DC):
                        last = pe.matmul(ps[4 + turn % 2][0:T, k * 3 * HP:(k + 1) * 3 * HP],
                                         XG[:, c, n, :, :].rearrange("p b j -> p (b j)"), wqkvm[:, c, n, :],
                                         start=(c == 0), stop=(c == DC - 1))
                last.then_inc(o_qkv_full, 1)
            pe.wait_ge(o_roped, 1)
            transpose_qk(pe, QK1[0], o_a_full, o_a_taken, 0)
            pe.wait_ge(o_a_taken, 2)
            pe.wait_ge(o_qkv_taken, 4)
            pe.wait_ge(o_cs_taken, 1)
            pe.wait_ge(o_pn_taken, 1)

            mosa.tensor(pe, PAIRS, lambda g, bank: pair_scores(pe, bank, QT1[0], KBD1[0], g, 1),
                        lambda g, probsT: pair_values(pe, V1[0], probsT, 2 * g, 2), lambda g: None)
            pe.wait_ge(o_o_taken, 1)
            for turn in range(4):
                if turn >= 2:
                    pe.wait_ge(o_z_taken, 2 * (turn - 1))
                for k in range(2):
                    n = 4 * (turn // 2) + 2 * k + turn % 2
                    r = 64 * (n % 2)
                    last = pe.matmul(ps[1 + turn % 2][0:T, k * D:(k + 1) * D],
                                     O1[r:r + 64, (n // 2) * T:(n // 2 + 1) * T], wom[r:r + 64, n // 2, :],
                                     start=True, stop=True)
                last.then_inc(o_z_full, 1)
            pe.wait_ge(o_z_in, 16 * NH)
            with pe.Fori(0, PAIRS) as i:
                for u in range(2):
                    b = 2 * i + u
                    pe.wait_ge(o_row, b + 1)
                    pe.wait_ge(x_updated, 4 * B + 2 * i)
                    pe.matmul(ps[6 + u][0:T, 0:D], OHR[u][:, :], Z2[:, bass.ds(b, 1), :].rearrange("p o d -> p (o d)"),
                              start=True, stop=True).then_inc(o_y_full, 1)

        def mosa_scalar(act):
            act.wait_ge(o_halved, 1)
            act.activation(GATE[:, :], GATE[:, :], ACT.Tanh).then_inc(o_gate, 1)
            for k in range(2):
                act.wait_ge(o_pos_full, k + 1)
                act.activation(POSB[:, 4 * k:4 * k + 4, :].rearrange("p n r -> p (n r)"), ps[4 + k][0:T, 0:4 * T],
                               ACT.Copy).then_inc(o_pos_taken, 1)
            act.wait_ge(o_cs_full, 1)
            act.activation(CS[:, :, :].rearrange("p n r -> p (n r)"), ps[6][0:T, :], ACT.Copy).then_inc(o_cs_taken, 1)
            for turn in range(4):
                c, half = turn // 2, turn % 2
                act.wait_ge(o_g_full, turn + 1)
                act.activation(XG[:, c, :, 4 * half:4 * half + 4, :].rearrange("p n b j -> p b n j"),
                               ps[2 * (turn % 2)][:, 0:4 * T].rearrange("p (b n j) -> p b n j", b=4, n=NH), ACT.Copy)\
                   .then_inc(o_g_taken, 1)
            for turn in range(4):
                act.wait_ge(o_qkv_full, turn + 1)
                src = ps[4 + turn % 2][0:T, 0:6 * HP].rearrange("p (n k d) -> p n k d", n=2, k=3)
                for k in range(2):
                    act.activation(QK1[0][:, k, 2 * turn:2 * turn + 2, :], src[:, :, k, :], ACT.Copy)
                act.activation(V1[0][:, 2 * turn * HP:(2 * turn + 2) * HP].rearrange("p (n d) -> p n d", n=2),
                               src[:, :, 2, :], ACT.Copy).then_inc(o_qkv_taken, 1)
            take_qk(act, QT1[0], KBD1[0], o_a_full, o_a_taken, 0)
            mosa.scalar(act, PAIRS, lambda g: None)
            for s in range(2):
                act.wait_ge(mosa.values_done[s], (PAIRS + 1) * RING // 2)
            act.activation(O1[:, :], ps[3][:, 0:4 * T], ACT.Copy).then_inc(o_o_taken, 1)

        def mosa_vector(dve):
            chain = Chain(dve, o_step, 1, 5)
            dve.wait_ge(o_cols_full, 1)
            dve.tensor_copy(POSC[:, :], ps[1][0:T, 0:NH])
            dve.tensor_scalar(GATE[:, :], ps[1][0:T, NH:2 * NH], 0.5, None, ALU.mult).then_inc(o_halved, 1)
            dve.wait_ge(o_halved, 1)
            dve.wait_ge(o_pos_taken, 2)
            tok = const("tokcol", T)
            dve.tensor_scalar(OH[:, :, :, :].rearrange("p n b j -> p (n b j)"), POSB[:, :, :].rearrange("p n r -> p (n r)"),
                              tok, None, ALU.is_equal).then_inc(o_onehot, 1)
            dve.tensor_scalar(OHB[:, :, :, :].rearrange("p b n j -> p n b j"),
                              POSB[:, :, :].rearrange("p n (b j) -> p n b j", b=B),
                              tok, None, ALU.is_equal).then_inc(o_onehot, 1)
            for n in range(NH):
                last = dve.tensor_scalar(MM[:, n, :], POSB[:, n, :], POSC[:, n:n + 1], MASKED, ALU.is_gt, ALU.mult)
            chain(last)
            dve.tensor_tensor(MM[:, :, :], MM[:, :, :], const("batchmask", T).unsqueeze(1).to_broadcast([T, NH, T]), ALU.min)\
               .then_inc(o_mask, 1)
            dve.wait_ge(o_pn_full, 1)
            dve.tensor_copy(POSN[:, :], ps[7][0:T, 0:B]).then_inc(o_pn_taken, 1)
            dve.wait_ge(o_cs_taken, 1)
            dve.wait_ge(o_qkv_taken, 4)
            cos = CS[:, :, 0:ROT].unsqueeze(1).to_broadcast([T, 2, NH, ROT])
            sin = CS[:, :, ROT:2 * ROT].unsqueeze(1).to_broadcast([T, 2, NH, ROT])
            rotate(dve, QK1[0][:, :, :, :], cos, sin, o_rope_step, 0, o_roped)
            dve.wait_ge(o_mask, 1)
            mosa.vector(dve, PAIRS, lambda g, h: None if h is None else MM[:, 2 * g + h, :], lambda g: None)
            dve.wait_ge(o_gate, 1)
            chain(dve.tensor_scalar(GATE[:, :], GATE[:, :], 0.5, 0.5, ALU.mult, ALU.add))
            for turn in range(4):
                dve.wait_ge(o_z_full, turn + 1)
                for k in range(2):
                    n = 4 * (turn // 2) + 2 * k + turn % 2
                    dve.tensor_scalar(Z[:, n, :], ps[1 + turn % 2][0:T, k * D:(k + 1) * D], GATE[:, n:n + 1], None, ALU.mult)\
                       .then_inc(o_z_taken, 1)
            dve.wait_ge(o_pn_taken, 1)
            with dve.Fori(0, PAIRS) as i:
                for u in range(2):
                    b = 2 * i + u
                    dve.wait_ge(o_y_full, 2 * i)
                    dve.tensor_scalar(OHR[u][:, :], const("tokrow", T), POSN[:, bass.ds(b, 1)], None, ALU.is_equal)\
                       .then_inc(o_row, 1)
                for u in range(2):
                    b = 2 * i + u
                    dve.wait_ge(o_y_full, b + 1)
                    xb = X[:, bass.ds(b, 1), :].rearrange("p o d -> p (o d)")
                    dve.scalar_tensor_tensor(xb, ps[6 + u][0:T, 0:D], tanh_gates[:, 3:4], xb, ALU.mult, ALU.add)\
                       .then_inc(x_updated, 1)

        def mosa_gpsimd(pool):
            mosa.gpsimd(pool, PAIRS)

        narrow, wide = cross0(1), cross0(NKT)
        SYNC, PE_, ACT_, DVE_, POOL_ = range(5)

        def cross0_on(eng, which):
            eng.wait_ge(wide_set, 1)
            flag = eng.value_load(wide_i[0:1, 0:1], min_val=0, max_val=2)
            with eng.If(flag == 0):
                narrow[which](eng)
            with eng.Else():
                wide[which](eng)

        block = ctx.enter_context(nc.Block())

        @block.sync
        def _(sp):
            sp.dma_start(qmask_row, a["qmask"].rearrange("b t -> (b t)").partition_broadcast(1)).then_inc(qmask_row_in, 16)
            sp.dma_start(consts[:, :], a["consts"]).then_inc(consts_in, 16)
            sp.dma_start(bnd_i[:, :], a["boundsT"]).then_inc(small_in, 16)
            sp.dma_start(gates[:, :], a["gates"].partition_broadcast(T)).then_inc(small_in, 16)
            sp.dma_start(X[:, :, :], a["x"].rearrange("b t d -> t b d")).then_inc(x_in, 16)
            sp.dma_start(wq0[:, :, :], a["wqT0"]).then_inc(weights0_in, 16)
            sp.dma_start(wk0[:, :, :], a["wkT0"]).then_inc(weights0_in, 16)
            for u in range(2):
                sp.dma_start(CT[u][:, :, :], a["ctxT"][:, :, u * TC:(u + 1) * TC]).then_inc(ctx_in[u], 16)
            sp.dma_start(wv0[:, :, :], a["wvT0"]).then_inc(weights0_in, 16)
            sp.dma_start(wo0[:, :, :], a["woT0"]).then_inc(weights0_in, 16)
            sp.dma_start(bqk0[:, :, :], a["bqk0"]).then_inc(weights0_in, 16)
            sp.dma_start(bv0[:, :], a["bv0"].partition_broadcast(128)).then_inc(weights0_in, 16)
            sp.dma_start(bo0[:, :], a["bo0"].partition_broadcast(1)).then_inc(weights0_in, 16)
            for w, name in ((wg0, "wgT0"), (we0, "weT0")):
                sp.dma_start(w[:, :, :], a[name]).then_inc(weights_moe_in, 16)
            sp.dma_start(bg0[:, :], a["bg0"].partition_broadcast(1)).then_inc(weights_moe_in, 16)
            sp.dma_start(be0[:, :], a["be0"]).then_inc(weights_moe_in, 16)
            sp.wait_ge(live_found, 1)
            sp.dma_start(qmask_i[:, :, :], a["qmask"].rearrange("b t -> (b t)").partition_broadcast(T)).then_inc(qmask_in, 16)
            for w, name in ((ws1, "ws1"), (wf1, "wf1")):
                sp.dma_start(w[:, :, :], a[name]).then_inc(weights_c_in, 16)
            sp.dma_start(w1_col[:, :], a["w1_col"]).then_inc(weights_c_in, 16)
            sp.dma_start(wcwb_col[:, :, :], a["wcwb_col"]).then_inc(weights_c_in, 16)
            sp.dma_start(bf1[:, :], a["bf1"]).then_inc(weights_c_in, 16)
            sp.dma_start(bcwb[:, :], a["bcwb"].partition_broadcast(T)).then_inc(weights_c_in, 16)
            for w, name in ((wqkv1, "wqkv1"), (wo1, "wo1"), (wr1, "wr1"), (wom, "wom")):
                sp.dma_start(w[:, :, :], a[name]).then_inc(weights_d_in, 16)
            sp.dma_start(wqkvm[:, :, :, :].rearrange("p c h d -> p c (h d)"), a["wqkvm"]).then_inc(weights_d_in, 16)
            cross0_on(sp, SYNC)
            additive_sync(sp)
            mosa_sync(sp)

        @block.tensor
        def _(pe):
            pe.wait_ge(consts_in, 16)
            pe.wait_ge(bnd_ready, 1)
            pe.matmul(ps[3][0:T, 0:B], const("tri", T), bnd_f[:, :], start=True, stop=True).then_inc(last_key_full, 1)
            pe.wait_ge(wide_ready, 1)
            pe.transpose(ps[3][0:1, 0:T], wide_col[:, :], ident[0:T, 0:T]).then_inc(wide_full, 1)
            pe.wait_ge(weights0_in, 16 * 7)
            pe.wait_ge(zeroed, 1)
            cross0_on(pe, PE_)
            experts_tensor(pe)
            additive_tensor(pe)
            dense_tensor(pe)
            mosa_tensor(pe)

        @block.scalar
        def _(act):
            act.wait_ge(small_in, 32)
            act.activation(tanh_gates[:, :], gates[:, :], ACT.Tanh).then_inc(tanh_ready, 1)
            act.wait_ge(weights0_in, 16 * 7)
            cross0_on(act, ACT_)
            experts_scalar(act)
            additive_scalar(act)
            dense_scalar(act)
            mosa_scalar(act)

        @block.vector
        def _(dve):
            find_live_pairs(dve)
            dve.wait_ge(small_in, 32)
            dve.tensor_copy(bnd_f[:, :], bnd_i[:, :]).then_inc(bnd_ready, 1)
            link(dve, dve.memset(var_eps[:, 1, :], -0.5))
            dve.wait_ge(last_key_full, 1)
            link(dve, dve.tensor_copy(last_key[:, :], ps[3][0:T, 0:B]))
            link(dve, dve.tensor_scalar(beyond[:, 0, :], last_key[:, :], KT - 1.0, None, ALU.is_gt))
            link(dve, dve.tensor_scalar(beyond[:, 1, :], last_key[:, :], 0.0, None, ALU.is_lt))
            link(dve, dve.tensor_tensor(beyond[:, 2, :], beyond[:, 0, :], beyond[:, 1, :], ALU.add))
            dve.tensor_reduce(wide_col[:, :], beyond[:, 2, :], AX_X, ALU.max).then_inc(wide_ready, 1)
            dve.wait_ge(wide_full, 1)
            dve.tensor_reduce(wide_i[:, :], ps[3][0:1, 0:T], AX_X, ALU.max).then_inc(wide_set, 1)
            dve.wait_ge(x_in, 16)
            layer_norm(dve, 0, 0, lambda: None)
            find_spans(dve)
            dve.wait_ge(weights0_in, 16 * 7)
            dve.wait_ge(tanh_ready, 1)
            dve.wait_ge(zeroed, 1)
            cross0_on(dve, DVE_)
            experts_vector(dve)
            additive_vector(dve)
            dense_vector(dve)
            mosa_vector(dve)

        @block.gpsimd
        def _(pool):
            pool.memset(zeros[:, :], 0.0)
            for u in range(2):
                last = pool.memset(V0[u][:, :, :, :], 0.0)
            last.then_inc(zeroed, 1)
            layer_norm_root(pool, 0)
            pool.wait_ge(consts_in, 16)
            cross0_on(pool, POOL_)
            experts_gpsimd(pool)
            additive_gpsimd(pool)
            dense_gpsimd(pool)
            mosa_gpsimd(pool)


def layout(i):
    import numpy as np
    n = {k: np.asarray(v) for k, v in i.items()}

    def rows(w):
        return np.ascontiguousarray(w.reshape(w.shape[0] // 128, 128, -1).transpose(1, 0, 2))

    a = {"x": np.ascontiguousarray(n["x"])}
    a["ctxT"] = rows(n["ctx_1024"].transpose(2, 0, 1).reshape(D, B * TC))
    a["boundsT"] = np.ascontiguousarray(n["mask_BxS_ik0"].T)
    a["wqT0"] = rows(n["L0_xattn_wq"].T)
    a["wkT0"] = rows(n["L0_xattn_wk"].T)
    a["wvT0"] = rows(n["L0_xattn_wv"].T)
    wo = np.zeros((128, 4, D), n["L0_xattn_wo"].dtype)
    for q in range(4):
        for h in range(4):
            head = 4 * q + h
            wo[PAD0 * h:PAD0 * h + DH0, q] = n["L0_xattn_wo"].T[head * DH0:(head + 1) * DH0]
    a["woT0"] = wo
    a["bqk0"] = np.ascontiguousarray(np.stack([n["L0_xattn_bq"], n["L0_xattn_bk"]]).reshape(2, DC, 128).transpose(2, 0, 1))
    a["bv0"] = n["L0_xattn_bv"]
    a["bo0"] = n["L0_xattn_bo"]
    a["wgT0"] = rows(n["L0_ffn_Wg"].T)
    a["bg0"] = n["L0_ffn_bg"]
    a["weT0"] = rows(n["L0_ffn_W"].transpose(2, 0, 1).reshape(D, NE * D))
    a["be0"] = n["L0_ffn_b"]
    a["qmask"] = np.ascontiguousarray(n["mask_BxS2_ik0"])
    a["ws1"] = rows(n["L1_xattn_Ws"])
    a["wf1"] = rows(n["L1_xattn_W"])
    a["w1_col"] = np.ascontiguousarray(n["L1_xattn_w"].reshape(DC, 128).T)
    a["wcwb_col"] = np.ascontiguousarray(
        np.concatenate([n["L1_xattn_Wcw"], n["L1_xattn_Wcb"]]).reshape(2, DC, 128).transpose(2, 0, 1))
    a["bf1"] = np.ascontiguousarray(n["L1_xattn_b"].reshape(DC, 128).T)
    a["bcwb"] = np.concatenate([n["L1_xattn_bcw"], n["L1_xattn_bcb"]])
    a["wqkv1"] = rows(n["L1_ffn_dense_wqkv"].reshape(D, NH, 3, HP).transpose(0, 2, 1, 3).reshape(D, 3 * NH * HP))
    a["wo1"] = rows(n["L1_ffn_dense_wo"])
    a["wr1"] = rows(n["L1_ffn_mosa_router_w"])
    a["wqkvm"] = rows(n["L1_ffn_mosa_wqkv"].reshape(D, NH * 3 * HP))
    a["wom"] = rows(n["L1_ffn_mosa_wo"])
    a["gates"] = np.concatenate([n["g_xattn"], n["g_ffn"]])
    a["consts"] = shape_constants(np)
    return a


def shape_constants(np):
    c = np.zeros((128, NCONST), np.float32)

    def put(name, v):
        lo, hi = CONST[name]
        c[:v.shape[0], lo:hi] = v

    put("ident", np.eye(128))
    t = np.arange(T)
    put("tri", (t[:, None] <= t[None, :]) * 1.0)
    put("headmask", (np.arange(128)[:, None] // DH0 == np.arange(8)[None, :]) * 1.0)
    put("keyidx", np.broadcast_to(np.arange(TC), (128, TC)))
    put("causal", (t[None, :] > t[:, None]) * MASKED)
    k = T // B
    put("batchmask", (t[None, :] // k != t[:, None] // k) * MASKED)
    put("tokcol", t[:, None])
    put("tokrow", np.broadcast_to(t, (128, T)))
    half = ROT // 2
    inv = np.float32(10000.0) ** (-np.arange(half, dtype=np.float32) / half)
    ang = t[:, None].astype(np.float32) * inv
    put("cos", np.concatenate([np.cos(ang), np.cos(ang)], 1))
    put("sin", np.concatenate([-np.sin(ang), np.sin(ang)], 1))
    put("iota8", np.broadcast_to(np.arange(NE), (128, NE)))
    put("ones", np.ones((128, 128)))
    return c


def kernel(**inputs):
    import numpy as np
    import concourse.bacc as bacc
    from concourse.bass_utils import run_bass_kernel_spmd

    nc = bacc.Bacc("TRN2", target_bir_lowering=False, num_devices=1)
    arrays, args = {}, {}
    for name, v in layout(inputs).items():
        v = np.ascontiguousarray(v)
        arrays["in_" + name] = v
        args[name] = nc.dram_tensor("in_" + name, v.shape, mybir.dt.from_np(v.dtype), kind="ExternalInput").ap()
    out = nc.dram_tensor("out", (B, T, D), F32, kind="ExternalOutput").ap()
    flamingo_kernel(nc, args, out)
    r = run_bass_kernel_spmd(nc, [arrays], core_ids=[0])
    return r.results[0]["out"]
```
